# Optimizing a Trainium2 kernel written in Bass

```python
import numpy as np
import jax
import jax.numpy as jnp

def _softmax(x, axis=-1):
    return jax.nn.softmax(x, axis=axis)

def _gelu(x):
    return jax.nn.gelu(x, approximate=True)

def _silu(x):
    return jax.nn.silu(x)

def _sigmoid(x):
    return jax.nn.sigmoid(x)

def _layernorm(x, axis=-1, eps=1e-05):
    m = jnp.mean(x, axis=axis, keepdims=True)
    v = jnp.var(x, axis=axis, keepdims=True)
    return (x - m) / jnp.sqrt(v + eps)

def _scatter_add(tgt, idx, src, axis=0):
    return tgt.at[idx].add(src)

def _segment_sum(src, seg, n):
    return jax.ops.segment_sum(src, seg, n)
kernel_name = 'mk_cond_seq_d4_seqx_r4_be7c60'

def setup_inputs(seed: int=0):
    np.random.seed(seed)
    _w = jnp.asarray

    def _rec_inputs():
        import jax
        import jax.numpy as jnp
        _rk = jax.random.key(seed)
        x = 1.648e-05 + 1 * jax.random.normal(jax.random.fold_in(_rk, 1), (16, 256, 256), jnp.float32)
        _lenS = 256 - jax.random.randint(jax.random.fold_in(_rk, 7), (16,), 0, max(1, 256 // 4) + 1, jnp.int32)
        _lenS2 = 256 - jax.random.randint(jax.random.fold_in(_rk, 8), (16,), 0, max(1, 256 // 4) + 1, jnp.int32)
        cond_1024 = 0.00191187 + 0.999416 * jax.random.normal(jax.random.fold_in(_rk, 11), (16, 256), jnp.float32)
        _validS = jnp.arange(256)[None, :] < _lenS[:, None]
        _validS2 = jnp.arange(256)[None, :] < _lenS2[:, None]
        _causal = jnp.tril(jnp.ones((256, 256), dtype=bool))
        mask_BxSxSx11_ik0 = jnp.where(jnp.ones((16, 256, 256, 11), dtype=bool), 0, 1).astype(jnp.int32)
        mask_BxS_bf0 = jnp.logical_not(jnp.ones((16, 256), dtype=bool))
        return (x, cond_1024, mask_BxSxSx11_ik0, mask_BxS_bf0)
    x, cond_1024, mask_BxSxSx11_ik0, mask_BxS_bf0 = _rec_inputs()

    def _L0_cond_setup():
        import jax, jax.numpy as jnp
        import numpy as np
        NONGT = 20
        H = 16
        NEG = -9000000000000000.0

        def _gat_attention(self_feat, cond_adj, label_bias, Wq, bq, Wk, bk, Wout, bout):
            B, N, F = self_feat.shape
            ng = min(NONGT, N)
            dh = F // H
            kv = self_feat[:, :ng]
            qh = (self_feat @ Wq.T + bq).reshape(B, N, H, dh)
            kh = (kv @ Wk.T + bk).reshape(B, ng, H, dh)
            aff = jnp.einsum('bnhd,bmhd->bnhm', qh, kh) * (1.0 / np.sqrt(dh))
            mask = cond_adj[:, :, None, :] > 0
            aff = jnp.where(mask, aff, NEG) + label_bias[:, :, None, :]
            w = jax.nn.softmax(aff, axis=-1)
            out_t = jnp.einsum('bnhm,bmf->bnhf', w, kv)
            out = jnp.einsum('bnhf,hgf->bnhg', out_t, Wout) + bout.reshape(H, F // H)
            return out.reshape(B, N, F)

        def _forward(v, q, adj, W_self, b_self, w_bias, b_bias, Wq, bq, Wk, bk, Wout, bout):
            adj_f = adj.astype(jnp.float32)
            exp_v = v
            row_zero = exp_v.sum(-1) == 0
            q_exp = jnp.where(row_zero[..., None], 0.0, q[:, None, :])
            vcq = jnp.concatenate([exp_v, q_exp], axis=-1)
            self_feat = vcq @ W_self.T + b_self
            output = self_feat
            for d in range(2):
                A = adj_f if d == 0 else jnp.swapaxes(adj_f, 1, 2)
                A = A[:, :, :NONGT, :]
                cond = A.sum(-1)
                vb = A @ w_bias + b_bias
                output = output + _gat_attention(self_feat, cond, vb, Wq[d], bq[d], Wk[d], bk[d], Wout[d], bout[d])
            rel = jax.nn.relu(output)
            return exp_v + rel
        key = jax.random.key(seed)
        ks = jax.random.split(key, 8)
        B, N, L, F, Q = (64, 36, 11, 256, 256)
        IN = F + Q
        s = 0.02
        return {'v': jax.random.normal(ks[0], (B, N, F), jnp.float32), 'q': jax.random.normal(ks[1], (B, Q), jnp.float32), 'adj': jax.random.randint(ks[2], (B, N, N, L), 0, 2, jnp.int32), 'W_self': jax.random.normal(ks[3], (F, IN), jnp.float32) * s, 'b_self': jnp.zeros((F,), jnp.float32), 'w_bias': jax.random.normal(ks[4], (L,), jnp.float32) * s, 'b_bias': jnp.zeros((), jnp.float32), 'Wq': jax.random.normal(ks[5], (2, F, F), jnp.float32) * s, 'bq': jnp.zeros((2, F), jnp.float32), 'Wk': jax.random.normal(ks[6], (2, F, F), jnp.float32) * s, 'bk': jnp.zeros((2, F), jnp.float32), 'Wout': jax.random.normal(ks[7], (2, H, F // H, F), jnp.float32) * s, 'bout': jnp.zeros((2, F), jnp.float32)}
    _L0_cond_all = _L0_cond_setup()
    _L0_cond_in = {k: v for k, v in _L0_cond_all.items() if k in ('W_self', 'b_self', 'w_bias', 'b_bias', 'Wq', 'bq', 'Wk', 'bk', 'Wout', 'bout')}
    del _L0_cond_all

    def _L1_cond_setup():
        import jax, jax.numpy as jnp
        import numpy as np
        B, N, D, H = (4, 256, 256, 16)
        DFF = 4 * D
        GATE_SCALE = 0.1
        LN_EPS = 1e-05

        def _layernorm(v, g, b):
            mu = jnp.mean(v, axis=-1, keepdims=True)
            var = jnp.mean(jnp.square(v - mu), axis=-1, keepdims=True)
            return (v - mu) * jax.lax.rsqrt(var + LN_EPS) * g + b

        def _attention(y, qkv_w, qkv_b, proj_w, proj_b):
            Bq, Nq, C = y.shape
            dh = C // H
            qkv = (y @ qkv_w + qkv_b).reshape(Bq, Nq, 3, H, dh)
            q, k, v = jnp.moveaxis(qkv, 2, 0)
            scale = dh ** (-0.5)
            attn = jnp.einsum('bqhd,bkhd->bhqk', q, k) * scale
            attn = jax.nn.softmax(attn, axis=-1)
            out = jnp.einsum('bhqk,bkhd->bqhd', attn, v).reshape(Bq, Nq, C)
            return out @ proj_w + proj_b
        key = jax.random.key(seed)
        ks = jax.random.split(key, 32)
        s = 0.02

        def w(k, shape):
            return jax.random.normal(k, shape, dtype=jnp.float32) * s
        inp = {'x': jax.random.normal(ks[0], (B, N, D), dtype=jnp.float32), 'cond': jax.random.normal(ks[1], (B, D), dtype=jnp.float32), 'g1_w': w(ks[2], (D, D)), 'g1_b': w(ks[3], (D,)), 'b1_w': w(ks[4], (D, D)), 'b1_b': w(ks[5], (D,)), 'a1_w': w(ks[6], (D, D)), 'a1_b': w(ks[7], (D,)), 'g2_w': w(ks[8], (D, D)), 'g2_b': w(ks[9], (D,)), 'b2_w': w(ks[10], (D, D)), 'b2_b': w(ks[11], (D,)), 'a2_w': w(ks[12], (D, D)), 'a2_b': w(ks[13], (D,)), 'ln1_g': jnp.ones((D,), jnp.float32), 'ln1_b': jnp.zeros((D,), jnp.float32), 'ln2_g': jnp.ones((D,), jnp.float32), 'ln2_b': jnp.zeros((D,), jnp.float32), 'qkv_w': w(ks[14], (D, 3 * D)), 'qkv_b': w(ks[15], (3 * D,)), 'proj_w': w(ks[16], (D, D)), 'proj_b': w(ks[17], (D,)), 'fc1_w': w(ks[18], (D, DFF)), 'fc1_b': w(ks[19], (DFF,)), 'fc2_w': w(ks[20], (DFF, D)), 'fc2_b': w(ks[21], (D,))}
        return inp
    _L1_cond_all = _L1_cond_setup()
    _L1_cond_in = {k: v for k, v in _L1_cond_all.items() if k in ('g1_w', 'g1_b', 'b1_w', 'b1_b', 'a1_w', 'a1_b', 'g2_w', 'g2_b', 'b2_w', 'b2_b', 'a2_w', 'a2_b', 'ln1_g', 'ln1_b', 'ln2_g', 'ln2_b', 'qkv_w', 'qkv_b', 'proj_w', 'proj_b', 'fc1_w', 'fc1_b', 'fc2_w', 'fc2_b')}
    del _L1_cond_all

    def _L2_cond_setup():
        import jax, jax.numpy as jnp
        import numpy as np
        DIM = 256
        HEADS = 16
        HIDDEN = 1024
        EPS = 1e-05

        def _ln(h):
            mu = jnp.mean(h, axis=-1, keepdims=True)
            var = jnp.var(h, axis=-1, keepdims=True)
            return (h - mu) / jnp.sqrt(var + EPS)
        key = jax.random.key(seed)
        ks = jax.random.split(key, 11)
        B, N, D, H = (2, 512, DIM, HIDDEN)
        s = lambda fan: 1.0 / np.sqrt(fan)
        return {'x': jax.random.normal(ks[0], (B, N, D), jnp.float32), 'c': jax.random.normal(ks[1], (B, D), jnp.float32), 'w_qkv': jax.random.normal(ks[2], (D, 3 * D), jnp.float32) * s(D), 'w_proj': jax.random.normal(ks[3], (D, D), jnp.float32) * s(D), 'b_proj': jax.random.normal(ks[4], (D,), jnp.float32) * 0.01, 'w_fc1': jax.random.normal(ks[5], (D, H), jnp.float32) * s(D), 'b_fc1': jax.random.normal(ks[6], (H,), jnp.float32) * 0.01, 'w_fc2': jax.random.normal(ks[7], (H, D), jnp.float32) * s(H), 'b_fc2': jax.random.normal(ks[8], (D,), jnp.float32) * 0.01, 'w_ada': jax.random.normal(ks[9], (D, 6 * D), jnp.float32) * s(D), 'b_ada': jax.random.normal(ks[10], (6 * D,), jnp.float32) * 0.01}
    _L2_cond_all = _L2_cond_setup()
    _L2_cond_in = {k: v for k, v in _L2_cond_all.items() if k in ('w_qkv', 'w_proj', 'b_proj', 'w_fc1', 'b_fc1', 'w_fc2', 'b_fc2', 'w_ada', 'b_ada')}
    del _L2_cond_all

    def _L3_cond_setup():
        import math
        import jax, jax.numpy as jnp
        import numpy as np
        H = 256
        NH = 16
        HD = H // NH
        CD = 256
        MLP = 1024
        EPS = 1e-05

        def _layernorm(x):
            mu = jnp.mean(x, axis=-1, keepdims=True)
            var = jnp.var(x, axis=-1, keepdims=True)
            return (x - mu) * jax.lax.rsqrt(var + EPS)

        def _adaln(x, cond, W, b):
            ss = cond @ W.T + b
            scale, shift = jnp.split(ss, 2, axis=-1)
            return _layernorm(x) * (1.0 + scale[:, None, :]) + shift[:, None, :]
        key = jax.random.key(seed)
        ks = jax.random.split(key, 16)
        s = 0.02
        inp = {'x': jax.random.normal(ks[0], (2, 512, H), jnp.float32), 'cond': jax.random.normal(ks[1], (2, CD), jnp.float32), 'key_padding_mask': jnp.zeros((2, 512), dtype=bool), 'w_adaln1': jax.random.normal(ks[2], (2 * H, CD), jnp.float32) * s, 'b_adaln1': jnp.zeros((2 * H,), jnp.float32), 'w_adaln2': jax.random.normal(ks[3], (2 * H, CD), jnp.float32) * s, 'b_adaln2': jnp.zeros((2 * H,), jnp.float32), 'wq': jax.random.normal(ks[4], (H, H), jnp.float32) * s, 'bq': jnp.zeros((H,), jnp.float32), 'wk': jax.random.normal(ks[5], (H, H), jnp.float32) * s, 'bk': jnp.zeros((H,), jnp.float32), 'wv': jax.random.normal(ks[6], (H, H), jnp.float32) * s, 'bv': jnp.zeros((H,), jnp.float32), 'wo': jax.random.normal(ks[7], (H, H), jnp.float32) * s, 'bo': jnp.zeros((H,), jnp.float32), 'w1': jax.random.normal(ks[8], (MLP, H), jnp.float32) * s, 'b1': jnp.zeros((MLP,), jnp.float32), 'w2': jax.random.normal(ks[9], (H, MLP), jnp.float32) * s, 'b2': jnp.zeros((H,), jnp.float32)}
        return inp
    _L3_cond_all = _L3_cond_setup()
    _L3_cond_in = {k: v for k, v in _L3_cond_all.items() if k in ('w_adaln1', 'b_adaln1', 'w_adaln2', 'b_adaln2', 'wq', 'bq', 'wk', 'bk', 'wv', 'bv', 'wo', 'bo', 'w1', 'b1', 'w2', 'b2')}
    del _L3_cond_all
    return {'x': x, 'cond_1024': cond_1024, 'mask_BxSxSx11_ik0': mask_BxSxSx11_ik0, 'mask_BxS_bf0': mask_BxS_bf0, 'L0_cond_W_self': _L0_cond_in['W_self'], 'L0_cond_b_self': _L0_cond_in['b_self'], 'L0_cond_w_bias': _L0_cond_in['w_bias'], 'L0_cond_b_bias': _L0_cond_in['b_bias'], 'L0_cond_Wq': _L0_cond_in['Wq'], 'L0_cond_bq': _L0_cond_in['bq'], 'L0_cond_Wk': _L0_cond_in['Wk'], 'L0_cond_bk': _L0_cond_in['bk'], 'L0_cond_Wout': _L0_cond_in['Wout'], 'L0_cond_bout': _L0_cond_in['bout'], 'L1_cond_g1_w': _L1_cond_in['g1_w'], 'L1_cond_g1_b': _L1_cond_in['g1_b'], 'L1_cond_b1_w': _L1_cond_in['b1_w'], 'L1_cond_b1_b': _L1_cond_in['b1_b'], 'L1_cond_a1_w': _L1_cond_in['a1_w'], 'L1_cond_a1_b': _L1_cond_in['a1_b'], 'L1_cond_g2_w': _L1_cond_in['g2_w'], 'L1_cond_g2_b': _L1_cond_in['g2_b'], 'L1_cond_b2_w': _L1_cond_in['b2_w'], 'L1_cond_b2_b': _L1_cond_in['b2_b'], 'L1_cond_a2_w': _L1_cond_in['a2_w'], 'L1_cond_a2_b': _L1_cond_in['a2_b'], 'L1_cond_ln1_g': _L1_cond_in['ln1_g'], 'L1_cond_ln1_b': _L1_cond_in['ln1_b'], 'L1_cond_ln2_g': _L1_cond_in['ln2_g'], 'L1_cond_ln2_b': _L1_cond_in['ln2_b'], 'L1_cond_qkv_w': _L1_cond_in['qkv_w'], 'L1_cond_qkv_b': _L1_cond_in['qkv_b'], 'L1_cond_proj_w': _L1_cond_in['proj_w'], 'L1_cond_proj_b': _L1_cond_in['proj_b'], 'L1_cond_fc1_w': _L1_cond_in['fc1_w'], 'L1_cond_fc1_b': _L1_cond_in['fc1_b'], 'L1_cond_fc2_w': _L1_cond_in['fc2_w'], 'L1_cond_fc2_b': _L1_cond_in['fc2_b'], 'L2_cond_w_qkv': _L2_cond_in['w_qkv'], 'L2_cond_w_proj': _L2_cond_in['w_proj'], 'L2_cond_b_proj': _L2_cond_in['b_proj'], 'L2_cond_w_fc1': _L2_cond_in['w_fc1'], 'L2_cond_b_fc1': _L2_cond_in['b_fc1'], 'L2_cond_w_fc2': _L2_cond_in['w_fc2'], 'L2_cond_b_fc2': _L2_cond_in['b_fc2'], 'L2_cond_w_ada': _L2_cond_in['w_ada'], 'L2_cond_b_ada': _L2_cond_in['b_ada'], 'L3_cond_w_adaln1': _L3_cond_in['w_adaln1'], 'L3_cond_b_adaln1': _L3_cond_in['b_adaln1'], 'L3_cond_w_adaln2': _L3_cond_in['w_adaln2'], 'L3_cond_b_adaln2': _L3_cond_in['b_adaln2'], 'L3_cond_wq': _L3_cond_in['wq'], 'L3_cond_bq': _L3_cond_in['bq'], 'L3_cond_wk': _L3_cond_in['wk'], 'L3_cond_bk': _L3_cond_in['bk'], 'L3_cond_wv': _L3_cond_in['wv'], 'L3_cond_bv': _L3_cond_in['bv'], 'L3_cond_wo': _L3_cond_in['wo'], 'L3_cond_bo': _L3_cond_in['bo'], 'L3_cond_w1': _L3_cond_in['w1'], 'L3_cond_b1': _L3_cond_in['b1'], 'L3_cond_w2': _L3_cond_in['w2'], 'L3_cond_b2': _L3_cond_in['b2']}

def reference(x, cond_1024, mask_BxSxSx11_ik0, mask_BxS_bf0, L0_cond_W_self, L0_cond_b_self, L0_cond_w_bias, L0_cond_b_bias, L0_cond_Wq, L0_cond_bq, L0_cond_Wk, L0_cond_bk, L0_cond_Wout, L0_cond_bout, L1_cond_g1_w, L1_cond_g1_b, L1_cond_b1_w, L1_cond_b1_b, L1_cond_a1_w, L1_cond_a1_b, L1_cond_g2_w, L1_cond_g2_b, L1_cond_b2_w, L1_cond_b2_b, L1_cond_a2_w, L1_cond_a2_b, L1_cond_ln1_g, L1_cond_ln1_b, L1_cond_ln2_g, L1_cond_ln2_b, L1_cond_qkv_w, L1_cond_qkv_b, L1_cond_proj_w, L1_cond_proj_b, L1_cond_fc1_w, L1_cond_fc1_b, L1_cond_fc2_w, L1_cond_fc2_b, L2_cond_w_qkv, L2_cond_w_proj, L2_cond_b_proj, L2_cond_w_fc1, L2_cond_b_fc1, L2_cond_w_fc2, L2_cond_b_fc2, L2_cond_w_ada, L2_cond_b_ada, L3_cond_w_adaln1, L3_cond_b_adaln1, L3_cond_w_adaln2, L3_cond_b_adaln2, L3_cond_wq, L3_cond_bq, L3_cond_wk, L3_cond_bk, L3_cond_wv, L3_cond_bv, L3_cond_wo, L3_cond_bo, L3_cond_w1, L3_cond_b1, L3_cond_w2, L3_cond_b2):
    import jax
    import jax.numpy as jnp

    def _L0_cond_ref(v, q, adj, W_self, b_self, w_bias, b_bias, Wq, bq, Wk, bk, Wout, bout):
        import jax, jax.numpy as jnp
        import numpy as np
        NONGT = 20
        H = 16
        NEG = -9000000000000000.0

        def _gat_attention(self_feat, cond_adj, label_bias, Wq, bq, Wk, bk, Wout, bout):
            B, N, F = self_feat.shape
            ng = min(NONGT, N)
            dh = F // H
            kv = self_feat[:, :ng]
            qh = (self_feat @ Wq.T + bq).reshape(B, N, H, dh)
            kh = (kv @ Wk.T + bk).reshape(B, ng, H, dh)
            aff = jnp.einsum('bnhd,bmhd->bnhm', qh, kh) * (1.0 / np.sqrt(dh))
            mask = cond_adj[:, :, None, :] > 0
            aff = jnp.where(mask, aff, NEG) + label_bias[:, :, None, :]
            w = jax.nn.softmax(aff, axis=-1)
            out_t = jnp.einsum('bnhm,bmf->bnhf', w, kv)
            out = jnp.einsum('bnhf,hgf->bnhg', out_t, Wout) + bout.reshape(H, F // H)
            return out.reshape(B, N, F)

        def _forward(v, q, adj, W_self, b_self, w_bias, b_bias, Wq, bq, Wk, bk, Wout, bout):
            adj_f = adj.astype(jnp.float32)
            exp_v = v
            row_zero = exp_v.sum(-1) == 0
            q_exp = jnp.where(row_zero[..., None], 0.0, q[:, None, :])
            vcq = jnp.concatenate([exp_v, q_exp], axis=-1)
            self_feat = vcq @ W_self.T + b_self
            output = self_feat
            for d in range(2):
                A = adj_f if d == 0 else jnp.swapaxes(adj_f, 1, 2)
                A = A[:, :, :NONGT, :]
                cond = A.sum(-1)
                vb = A @ w_bias + b_bias
                output = output + _gat_attention(self_feat, cond, vb, Wq[d], bq[d], Wk[d], bk[d], Wout[d], bout[d])
            rel = jax.nn.relu(output)
            return exp_v + rel
        return _forward(v, q, adj, W_self, b_self, w_bias, b_bias, Wq, bq, Wk, bk, Wout, bout)

    def _L1_cond_ref(x, cond, g1_w, g1_b, b1_w, b1_b, a1_w, a1_b, g2_w, g2_b, b2_w, b2_b, a2_w, a2_b, ln1_g, ln1_b, ln2_g, ln2_b, qkv_w, qkv_b, proj_w, proj_b, fc1_w, fc1_b, fc2_w, fc2_b):
        import jax, jax.numpy as jnp
        import numpy as np
        B, N, D, H = (4, 256, 256, 16)
        DFF = 4 * D
        GATE_SCALE = 0.1
        LN_EPS = 1e-05

        def _layernorm(v, g, b):
            mu = jnp.mean(v, axis=-1, keepdims=True)
            var = jnp.mean(jnp.square(v - mu), axis=-1, keepdims=True)
            return (v - mu) * jax.lax.rsqrt(var + LN_EPS) * g + b

        def _attention(y, qkv_w, qkv_b, proj_w, proj_b):
            Bq, Nq, C = y.shape
            dh = C // H
            qkv = (y @ qkv_w + qkv_b).reshape(Bq, Nq, 3, H, dh)
            q, k, v = jnp.moveaxis(qkv, 2, 0)
            scale = dh ** (-0.5)
            attn = jnp.einsum('bqhd,bkhd->bhqk', q, k) * scale
            attn = jax.nn.softmax(attn, axis=-1)
            out = jnp.einsum('bhqk,bkhd->bqhd', attn, v).reshape(Bq, Nq, C)
            return out @ proj_w + proj_b
        gamma1 = cond @ g1_w + g1_b
        beta1 = cond @ b1_w + b1_b
        alpha1 = jnp.tanh(cond @ a1_w + a1_b) * GATE_SCALE
        gamma2 = cond @ g2_w + g2_b
        beta2 = cond @ b2_w + b2_b
        alpha2 = jnp.tanh(cond @ a2_w + a2_b) * GATE_SCALE
        y = _layernorm(x, ln1_g, ln1_b)
        y = y * (1.0 + gamma1[:, None, :]) + beta1[:, None, :]
        y = _attention(y, qkv_w, qkv_b, proj_w, proj_b)
        x = x + y * alpha1[:, None, :]
        z = _layernorm(x, ln2_g, ln2_b)
        z = z * (1.0 + gamma2[:, None, :]) + beta2[:, None, :]
        z = jax.nn.gelu(z @ fc1_w + fc1_b, approximate=False) @ fc2_w + fc2_b
        x = x + z * alpha2[:, None, :]
        return x

    def _L2_cond_ref(x, c, w_qkv, w_proj, b_proj, w_fc1, b_fc1, w_fc2, b_fc2, w_ada, b_ada):
        import jax, jax.numpy as jnp
        import numpy as np
        DIM = 256
        HEADS = 16
        HIDDEN = 1024
        EPS = 1e-05

        def _ln(h):
            mu = jnp.mean(h, axis=-1, keepdims=True)
            var = jnp.var(h, axis=-1, keepdims=True)
            return (h - mu) / jnp.sqrt(var + EPS)
        B, N, D = x.shape
        hd = D // HEADS
        scale = hd ** (-0.5)
        mod = jax.nn.silu(c) @ w_ada + b_ada
        shift_msa, scale_msa, gate_msa, shift_mlp, scale_mlp, gate_mlp = jnp.split(mod, 6, axis=1)
        h = _ln(x) * (1.0 + scale_msa[:, None, :]) + shift_msa[:, None, :]
        qkv = (h @ w_qkv).reshape(B, N, 3, HEADS, hd)
        q = qkv[:, :, 0].transpose(0, 2, 1, 3)
        k = qkv[:, :, 1].transpose(0, 2, 1, 3)
        v = qkv[:, :, 2].transpose(0, 2, 1, 3)
        attn = jax.nn.softmax(jnp.einsum('bhqd,bhkd->bhqk', q, k) * scale, axis=-1)
        o = jnp.einsum('bhqk,bhkd->bhqd', attn, v).transpose(0, 2, 1, 3).reshape(B, N, D)
        o = o @ w_proj + b_proj
        x = x + gate_msa[:, None, :] * o
        h2 = _ln(x) * (1.0 + scale_mlp[:, None, :]) + shift_mlp[:, None, :]
        m = jax.nn.gelu(h2 @ w_fc1 + b_fc1, approximate=False) @ w_fc2 + b_fc2
        return x + gate_mlp[:, None, :] * m

    def _L3_cond_ref(x, cond, key_padding_mask, w_adaln1, b_adaln1, w_adaln2, b_adaln2, wq, bq, wk, bk, wv, bv, wo, bo, w1, b1, w2, b2):
        import math
        import jax, jax.numpy as jnp
        import numpy as np
        H = 256
        NH = 16
        HD = H // NH
        CD = 256
        MLP = 1024
        EPS = 1e-05

        def _layernorm(x):
            mu = jnp.mean(x, axis=-1, keepdims=True)
            var = jnp.var(x, axis=-1, keepdims=True)
            return (x - mu) * jax.lax.rsqrt(var + EPS)

        def _adaln(x, cond, W, b):
            ss = cond @ W.T + b
            scale, shift = jnp.split(ss, 2, axis=-1)
            return _layernorm(x) * (1.0 + scale[:, None, :]) + shift[:, None, :]
        B, L, D = x.shape
        normed = _adaln(x, cond, w_adaln1, b_adaln1)
        q = (normed @ wq.T + bq).reshape(B, L, NH, HD)
        k = (normed @ wk.T + bk).reshape(B, L, NH, HD)
        v = (normed @ wv.T + bv).reshape(B, L, NH, HD)
        scale = math.sqrt(HD)
        scores = jnp.einsum('blhd,bmhd->bhlm', q, k) / scale
        scores = jnp.where(key_padding_mask[:, None, None, :], -jnp.inf, scores)
        attn = jax.nn.softmax(scores, axis=-1)
        attn_out = jnp.einsum('bhlm,bmhd->blhd', attn, v).reshape(B, L, D)
        x = x + attn_out @ wo.T + bo
        normed = _adaln(x, cond, w_adaln2, b_adaln2)
        h = jax.nn.gelu(normed @ w1.T + b1, approximate=False)
        x = x + h @ w2.T + b2
        return x
    x = _L0_cond_ref(x, cond_1024, mask_BxSxSx11_ik0, L0_cond_W_self, L0_cond_b_self, L0_cond_w_bias, L0_cond_b_bias, L0_cond_Wq, L0_cond_bq, L0_cond_Wk, L0_cond_bk, L0_cond_Wout, L0_cond_bout)
    x = _L1_cond_ref(x, cond_1024, L1_cond_g1_w, L1_cond_g1_b, L1_cond_b1_w, L1_cond_b1_b, L1_cond_a1_w, L1_cond_a1_b, L1_cond_g2_w, L1_cond_g2_b, L1_cond_b2_w, L1_cond_b2_b, L1_cond_a2_w, L1_cond_a2_b, L1_cond_ln1_g, L1_cond_ln1_b, L1_cond_ln2_g, L1_cond_ln2_b, L1_cond_qkv_w, L1_cond_qkv_b, L1_cond_proj_w, L1_cond_proj_b, L1_cond_fc1_w, L1_cond_fc1_b, L1_cond_fc2_w, L1_cond_fc2_b)
    x = _L2_cond_ref(x, cond_1024, L2_cond_w_qkv, L2_cond_w_proj, L2_cond_b_proj, L2_cond_w_fc1, L2_cond_b_fc1, L2_cond_w_fc2, L2_cond_b_fc2, L2_cond_w_ada, L2_cond_b_ada)
    x = _L3_cond_ref(x, cond_1024, mask_BxS_bf0, L3_cond_w_adaln1, L3_cond_b_adaln1, L3_cond_w_adaln2, L3_cond_b_adaln2, L3_cond_wq, L3_cond_bq, L3_cond_wk, L3_cond_bk, L3_cond_wv, L3_cond_bv, L3_cond_wo, L3_cond_bo, L3_cond_w1, L3_cond_b1, L3_cond_w2, L3_cond_b2)
    return x

_drawn_inputs = setup_inputs


def setup_inputs(seed=0):
    import zlib

    import numpy as np

    out = dict(_drawn_inputs(seed))
    spreads = {'L0_cond_b_self': (0.0, 0.1),
     'L0_cond_bq': (0.0, 0.1),
     'L0_cond_bk': (0.0, 0.1),
     'L0_cond_bout': (0.0, 0.1),
     'L1_cond_ln1_g': (1.0, 0.6),
     'L1_cond_ln1_b': (0.0, 0.8),
     'L1_cond_ln2_g': (1.0, 0.6),
     'L1_cond_ln2_b': (0.0, 0.8),
     'L3_cond_b_adaln1': (0.0, 2.0),
     'L3_cond_b_adaln2': (0.0, 2.0),
     'L3_cond_bq': (0.0, 2.0),
     'L3_cond_bk': (0.0, 2.0),
     'L3_cond_bv': (0.0, 1.234),
     'L3_cond_bo': (0.0, 0.382),
     'L3_cond_b1': (0.0, 1.122),
     'L3_cond_b2': (0.0, 0.374)}
    factors = {'L1_cond_g1_w': 8.0,
     'L1_cond_g1_b': 8.0,
     'L1_cond_b1_w': 8.0,
     'L1_cond_b1_b': 8.0,
     'L1_cond_a1_w': 8.0,
     'L1_cond_a1_b': 8.0,
     'L1_cond_g2_w': 8.0,
     'L1_cond_g2_b': 8.0,
     'L1_cond_b2_w': 8.0,
     'L1_cond_b2_b': 8.0,
     'L1_cond_a2_w': 8.0,
     'L1_cond_a2_b': 8.0,
     'L1_cond_qkv_w': 8.0,
     'L1_cond_qkv_b': 8.0,
     'L1_cond_proj_w': 8.0,
     'L1_cond_proj_b': 64.0,
     'L1_cond_fc1_w': 8.0,
     'L1_cond_fc1_b': 45.568,
     'L1_cond_fc2_w': 8.0,
     'L1_cond_fc2_b': 64.0,
     'L2_cond_b_proj': 48.93,
     'L2_cond_b_fc1': 64.0,
     'L2_cond_b_fc2': 48.732,
     'L2_cond_b_ada': 16.313,
     'L3_cond_wq': 35.26,
     'L3_cond_wk': 34.906,
     'L3_cond_w_adaln1': 4.645,
     'L3_cond_w_adaln2': 5.283}
    for name, (base, spread) in spreads.items():
        noise = np.random.default_rng([zlib.crc32(name.encode()), seed]).standard_normal(out[name].shape)
        drawn = base * np.exp(spread * noise) if base else spread * noise
        out[name] = jnp.asarray(drawn.astype(out[name].dtype))
    for name, factor in factors.items():
        out[name] = (out[name] * factor).astype(out[name].dtype)
    return out
```

```python
from contextlib import ExitStack

import numpy as np
import concourse.bass as bass
from concourse import mybir

F32 = mybir.dt.float32
F32R = mybir.dt.float32r
BF16 = mybir.dt.bfloat16
I32 = mybir.dt.int32
ALU = mybir.AluOpType
ACT = mybir.ActivationFunctionType
AX_X = mybir.AxisListType.X

P = 128
B, N, D = 16, 256, 256
C = D // P
H, DH = 16, 16
HC = P // DH
PAIRS = B // 2
T = 2 * N
TILES = T // P
BT = N // P
LAYERS = 3
DFF = 1024
J = DFF // P
NK, L = 20, 11
NEG = -9000000000000000.0
EPS = 1e-5
QSCALE = DH ** -0.5
PARTS = 3
Q_PART = (0, 0, 1, 1, 0, 2)
K_PART = (0, 1, 0, 1, 2, 0)
KR = 16 * len(Q_PART)
KA = KR + 1
KM = KA + PARTS
BIG = 1e30
GH = 4
G = H // GH
RING = 8
GR = GH * NK
UNITS = 2 * H
W_CHUNK = 256


class Banks:

    def __init__(self, order, before):
        self.where, self.uses = {}, {}
        for name, bank in order:
            k = self.uses.get(bank, 0)
            self.where[name] = (bank, k)
            self.uses[bank] = k + 1
        self.before = before

    def use(self, name, step):
        bank, k = self.where[name]
        return bank, step * self.uses[bank] + self.before.get(bank, 0) + k

    def after(self, steps):
        banks = set(self.uses) | set(self.before)
        return {b: self.before.get(b, 0) + steps * self.uses.get(b, 0) for b in banks}


class Chain:

    def __init__(self, eng, sem, step, per_step, at=0):
        self.eng, self.sem, self.base, self.per_step, self.k = eng, sem, step * per_step, per_step, at

    def link(self, ins):
        self.k += 1
        assert self.k <= self.per_step
        ins.then_inc(self.sem, 1)
        self.eng.wait_ge(self.sem, self.base + self.k)


def mm3(pe, out, a_hi, a_lo, b_hi, b_lo, first, last):
    pe.matmul(out, a_hi, b_hi, start=first, stop=False)
    pe.matmul(out, a_hi, b_lo, start=False, stop=False)
    return pe.matmul(out, a_lo, b_hi, start=False, stop=last)


def settle(eng, passed, n):
    if not isinstance(n, int):
        eng.sem_inc(passed)


def graph_layer(nc, ins, xres, mod_p0, mod_p3, ident, identb, scr_mask):
    with ExitStack() as ctx:
        def sb(name, shape, dt=F32):
            return ctx.enter_context(nc.sbuf_tensor("g_" + name, shape, dt))

        def sem(name):
            return ctx.enter_context(nc.semaphore("g_" + name))

        bank = [ctx.enter_context(nc.psum_tensor(f"g_bank{i}", [P, 512], F32)) for i in range(8)]

        NW = 7
        NU = TILES * 2
        w_hi = sb("w_hi", [P, NW, C, D], F32R)
        w_lo = sb("w_lo", [P, NW, C, D], F32R)
        w_raw = sb("w_raw", [P, 2, C, D])
        wq_self = sb("wq_self", [P, C, D])
        ada_w = sb("ada_w", [P, C, 6 * D])
        cond = sb("cond", [P, C, B])
        cond_silu = sb("cond_silu", [P, C, B])
        ada_b = sb("ada_b", [P, LAYERS, 6, C])
        ln_gb = sb("ln_gb", [P, 4, C])
        out_b = sb("out_b", [P, LAYERS, 2, C])
        modv = sb("modv", [P, 6, C, B])
        mask = sb("mask", [LAYERS * B, N], mybir.dt.uint8)
        mask_rows = sb("mask_rows", [LAYERS * B, N], BF16)
        modt = sb("modt", [P, C, B])
        gbias = sb("gbias", [P, 7, C])
        bout = sb("bout", [P, C])
        lab = sb("lab", [P, L + 1])
        sel8 = sb("sel8", [P, HC])
        sel80 = sb("sel80", [GR, GH])
        qw = sb("qw", [P, C, PAIRS, 2])
        adj = sb("adj", [P, TILES * 2 * NK, L], I32)
        prod = sb("prod", [P, TILES * 2 * NK, L])
        vb = sb("vb", [P, TILES * 2 * NK])
        keep = sb("keep", [P, TILES * 2, NK])
        shift = sb("shift", [P, TILES * 2, NK])
        neg = sb("neg", [P, TILES * 2 * NK])
        x_tok = sb("x_tok", [P, TILES, D])
        rsum = sb("rsum", [P, TILES])
        nz = sb("nz", [P, TILES], BF16)
        nzb = sb("nzb", [P, T])
        feat = sb("feat", [P, C, T])
        f_hi = sb("f_hi", [P, C, T], F32R)
        f_lo = sb("f_lo", [P, C, T], F32R)
        st = sb("st", [P, C, T])
        s_hi = sb("s_hi", [P, C, T], F32R)
        s_lo = sb("s_lo", [P, C, T], F32R)
        q_f = sb("q_f", [P, 2, T])
        q_hi = sb("q_hi", [P, 2 * C, T], F32R)
        q_lo = sb("q_lo", [P, 2 * C, T], F32R)
        k_f = sb("k_f", [P, 2 * C, 2, NK])
        kbd = sb("kbd", [P, 2, 2 * C, HC * NK])
        kbd_hi = sb("kbd_hi", [P, 2, 2 * C, HC * NK], F32R)
        kbd_lo = sb("kbd_lo", [P, 2, 2 * C, HC * NK], F32R)
        s_rep = sb("s_rep", [P, 2, C, 2, GR], F32R)
        vbd = sb("vbd", [GR, 2, 2, G, GH * DH])
        aff = sb("aff", [P, 2, H, NK])
        e = sb("e", [P, NU, H, NK])
        mx = sb("mx", [P, H])
        den = sb("den", [P, NU, H])
        wt = sb("wt", [GR, 2, G, T])

        raw_in = [sem(f"raw_in{i}") for i in range(2)]
        x_in = [sem(f"x_in{i}") for i in range(PAIRS)]
        consts, ada_in, adj_in = sem("consts"), sem("ada_in"), sem("adj_in")
        w_split, qw_ps, qw_done, mod_ps, mod_done = sem("w_split"), sem("qw_ps"), sem("qw_done"), sem("mod_ps"), sem("mod_done")
        mod_raw, mod_tanh, silu = sem("mod_raw"), sem("mod_tanh"), sem("silu")
        ready = sem("ready")
        mask_in, mask_done, mask_out = sem("mask_in"), sem("mask_done"), sem("mask_out")
        passed = sem("passed")
        adj_used, x_copied, nz_ready, xt_split, s_ready, s_split = (
            sem("adj_used"), sem("x_copied"), sem("nz_ready"), sem("xt_split"), sem("s_ready"), sem("s_split"))
        q_hi_done, q_lo_done, kbd_split, rep_ready = sem("q_hi_done"), sem("q_lo_done"), sem("kbd_split"), sem("rep_ready")
        shifted, exped, dens, weights, relu_out = (
            sem("shifted"), sem("exped"), sem("dens"), sem("weights"), sem("relu_out"))
        prep_chain, soft_chain, st_chain, set_chain = sem("prep_chain"), sem("soft_chain"), sem("st_chain"), sem("set_chain")

        order = ([("xt0", 0), ("xt1", 1), ("nz", 2), ("s0", 3), ("s1", 4), ("q0", 5), ("q1", 6), ("q2", 7), ("q3", 0)]
                 + [("k", 1), ("v0", 2), ("v1", 3)] + [(f"aff{u}", 4 + u % 4) for u in range(NU)]
                 + [(f"wt{i}", i % 2) for i in range(2 * G)] + [("out0", 2), ("out1", 3), ("back0", 6), ("back1", 7)])
        uses = Banks(order, {})
        full = [sem(f"full{i}") for i in range(8)]
        free = [sem(f"free{i}") for i in range(8)]

        def wait_full(eng, name, n):
            i, k = uses.use(name, n)
            eng.wait_ge(full[i], k + 1)
            return bank[i], free[i]

        def take(pe, name, n, first=False):
            i, k = uses.use(name, n)
            if not (first and uses.where[name][1] == 0):
                pe.wait_ge(free[i], k)
            return bank[i], full[i]

        def pair_loop(eng, step):
            step(0, True)
            with eng.Fori(1, PAIRS) as n:
                step(n, False)

        block = ctx.enter_context(nc.Block())

        @block.sync
        def _(sp):
            for dst, src in ((cond[:], "cond"), (wq_self[:], "wq_self"), (ident[:], "ident"), (gbias[:], "gbias"),
                             (lab[:], "lab"), (sel8[:], "sel8"), (sel80[:], "sel80"), (ada_b[:], "ada_b"),
                             (ln_gb[:], "ln_gb"), (out_b[:], "out_b")):
                sp.dma_start(dst, ins[src]).then_inc(consts, 16)
            sp.dma_start(xres[:, 0], ins["x"][0]).then_inc(x_in[0], 16)
            sp.dma_start(adj[:], ins["adj"][0]).then_inc(adj_in, 16)
            for i in range(NW):
                if i >= 2:
                    sp.wait_ge(w_split, 2 * (i - 1))
                sp.dma_start(w_raw[:, i % 2], ins["gw"][i]).then_inc(raw_in[i % 2], 16)
            sp.dma_start(mask[(LAYERS - 1) * B:], ins["mask"]).then_inc(mask_in, 16)
            sp.wait_ge(mask_done, 2)
            sp.dma_start(scr_mask, mask_rows[:]).then_inc(mask_out, 16)
            for i in range(1, PAIRS):
                sp.dma_start(xres[:, i], ins["x"][i]).then_inc(x_in[i], 16)
            for layer in range(LAYERS):
                if layer:
                    sp.wait_ge(mod_ps, layer)
                w = (6 if layer < 2 else 4) * D
                sp.dma_start(ada_w[:, :, 0:w], ins[f"ada{layer}"]).then_inc(ada_in, 16)
            with sp.Fori(1, PAIRS) as n:
                sp.wait_ge(adj_used, 2 * n)
                sp.dma_start(adj[:], ins["adj"][n]).then_inc(adj_in, 16)
            sp.wait_ge(mask_out, 16)

        @block.tensor
        def _(pe):
            pe.wait_ge(consts, 160)
            for oc in range(C):
                for c in range(C):
                    mm = pe.matmul(bank[3][:, oc * B:(oc + 1) * B], wq_self[:, c, oc * P:(oc + 1) * P], cond[:, c, :],
                                   start=(c == 0), stop=(c == C - 1))
            mm.then_inc(qw_ps, 1)
            pe.wait_ge(silu, 1)
            for layer in range(LAYERS):
                pe.wait_ge(ada_in, 16 * (layer + 1))
                rhs = cond_silu if layer == 1 else cond
                for v in range(6 if layer < 2 else 4):
                    for oc in range(C):
                        at, o = (v * C + oc) * B, slice(v * D + oc * P, v * D + (oc + 1) * P)
                        for c in range(C):
                            mm = pe.matmul(bank[layer][:, at:at + B], ada_w[:, c, o], rhs[:, c, :],
                                           start=(c == 0), stop=(c == C - 1))
                mm.then_inc(mod_ps, 1)
            pe.wait_ge(qw_done, 1)
            pe.wait_ge(mod_raw, LAYERS)
            pe.wait_ge(ready, 3)
            pe.wait_ge(w_split, 2 * NW)

            def linear(out, w, oc, hi, lo):
                o = slice(oc * P, (oc + 1) * P)
                for c in range(C):
                    mm = mm3(pe, out[:], w_hi[:, w, c, o], w_lo[:, w, c, o], hi[:, c], lo[:, c], c == 0, c == C - 1)
                return mm

            def step(n, first):
                pe.wait_ge(x_copied, n + 1)
                for c in range(C):
                    out, done = take(pe, f"xt{c}", n, first)
                    for i in range(TILES):
                        mm = pe.transpose(out[:, i * P:(i + 1) * P], x_tok[:, i, c * P:(c + 1) * P], ident[:])
                    mm.then_inc(done, 1)
                pe.wait_ge(nz_ready, n + 1)
                out, done = take(pe, "nz", n, first)
                for i in range(TILES):
                    mm = pe.matmul(out[:, i * P:(i + 1) * P], nz[:, i:i + 1].to_broadcast([P, P]), identb[:],
                                   start=True, stop=True)
                mm.then_inc(done, 1)
                pe.wait_ge(xt_split, 2 * C * (n + 1))
                for oc in range(C):
                    out, done = take(pe, f"s{oc}", n, first)
                    linear(out, 0, oc, f_hi, f_lo).then_inc(done, 1)
                pe.wait_ge(s_split, 2 * C * (n + 1))
                for i in range(2 * C):
                    out, done = take(pe, f"q{i}", n, first)
                    linear(out, 1 + i // C, i % C, s_hi, s_lo).then_inc(done, 1)
                out, done = take(pe, "k", n, first)
                for i in range(2 * C):
                    o, w = slice((i % C) * P, (i % C + 1) * P), 3 + i // C
                    for c in range(C):
                        hi = s_hi[:, c, :].rearrange("p (b t) -> p b t", b=2)[:, :, 0:NK]
                        lo = s_lo[:, c, :].rearrange("p (b t) -> p b t", b=2)[:, :, 0:NK]
                        mm = mm3(pe, out[:, i * 2 * NK:(i + 1) * 2 * NK], w_hi[:, w, c, o], w_lo[:, w, c, o], hi, lo,
                                 c == 0, c == C - 1)
                mm.then_inc(done, 1)
                pe.wait_ge(rep_ready, 2 * (n + 1))
                for d in range(2):
                    out, done = take(pe, f"v{d}", n, first)
                    for b in range(2):
                        for g in range(G):
                            at, o = (b * G + g) * GH * DH, slice(g * GH * DH, (g + 1) * GH * DH)
                            for c in range(C):
                                mm = mm3(pe, out[0:GR, at:at + GH * DH], s_rep[:, 0, c, b], s_rep[:, 1, c, b],
                                         w_hi[:, 5 + d, c, o], w_lo[:, 5 + d, c, o], c == 0, c == C - 1)
                    mm.then_inc(done, 1)
                pe.wait_ge(kbd_split, 2 * (n + 1))
                pe.wait_ge(q_lo_done, 2 * C * (n + 1))
                for u in range(NU):
                    i, d = u // 2, u % 2
                    out, done = take(pe, f"aff{u}", n, first)
                    for c in range(C):
                        t, at = slice(i * P, (i + 1) * P), c * HC * NK
                        mm = mm3(pe, out[:, at:at + HC * NK], q_hi[:, d * C + c, t], q_lo[:, d * C + c, t],
                                 kbd_hi[:, i // BT, d * C + c], kbd_lo[:, i // BT, d * C + c], True, True)
                    mm.then_inc(done, 1)
                pe.wait_ge(weights, NU * (n + 1))
                for d in range(2):
                    for g in range(G):
                        out, done = take(pe, f"wt{d * G + g}", n, first)
                        for i in range(TILES):
                            src = e[:, i * 2 + d, g * GH:(g + 1) * GH].rearrange("p h m -> p (h m)")
                            mm = pe.transpose(out[0:GR, i * P:(i + 1) * P], src, ident[:])
                        mm.then_inc(done, 1)
                for i in (0, 1):
                    pe.wait_ge(free[i], uses.use(f"wt{2 * G - 2 + i}", n)[1] + 1)
                for c in range(C):
                    out, done = take(pe, f"out{c}", n, first)
                    for b in range(2):
                        for d in range(2):
                            for gg in range(2):
                                g = 2 * c + gg
                                mm = pe.matmul(out[64 * gg:64 * gg + GH * DH, b * N:(b + 1) * N], vbd[:, d, b, g],
                                               wt[:, d, g, b * N:(b + 1) * N], start=(d == 0), stop=(d == 1))
                    mm.then_inc(done, 1)
                pe.wait_ge(relu_out, C * (n + 1))
                for i in range(2):
                    out, done = take(pe, f"back{i}", n, first)
                    for tt in range(2):
                        for c in range(C):
                            t = slice((2 * i + tt) * P, (2 * i + tt + 1) * P)
                            mm = pe.transpose(out[:, tt * D + c * P:tt * D + (c + 1) * P], feat[:, c, t], ident[:])
                    mm.then_inc(done, 1)

            pair_loop(pe, step)

        @block.vector
        def _(dve):
            v = nc.vector
            link = Chain(dve, set_chain, 0, 100).link
            v.memset(vbd[:], 0.0).then_inc(ready, 1)
            dve.wait_ge(consts, 160)
            v.tensor_copy(identb[:], ident[:]).then_inc(ready, 1)
            v.tensor_tensor(bout[:], gbias[:, 5], gbias[:, 6], ALU.add).then_inc(ready, 1)
            dve.wait_ge(qw_ps, 1)
            v.tensor_copy(qw[:].rearrange("p c n b -> p (c n b)"), bank[3][:, 0:C * B]).then_inc(qw_done, 1)
            for i in range(NW):
                dve.wait_ge(raw_in[i % 2], 16 * (i // 2 + 1))
                v.tensor_copy(w_hi[:, i], w_raw[:, i % 2]).then_inc(w_split, 1)
                dve.wait_ge(w_split, 2 * i + 1)
                v.tensor_tensor(w_lo[:, i], w_raw[:, i % 2], w_hi[:, i].bitcast(F32), ALU.subtract).then_inc(w_split, 1)
            v.memset(mask_rows[:], 0.0).then_inc(mask_done, 1)
            dve.wait_ge(mask_in, 16)
            dve.wait_ge(mask_done, 1)
            v.tensor_scalar(mask_rows[(LAYERS - 1) * B:], mask[(LAYERS - 1) * B:], -BIG, BIG, ALU.mult,
                            ALU.mult).then_inc(mask_done, 1)
            for layer in range(LAYERS):
                nv = 6 if layer < 2 else 4
                order_v = (0, 1, 2, 3, 4, 5) if layer < 2 else (0, 1, 3, 4)
                dve.wait_ge(mod_ps, layer + 1)
                if layer:
                    dve.wait_ge(mod_done, layer)
                for k, vec in enumerate(order_v):
                    ins_ = v.tensor_tensor(modv[:, vec], bank[layer][:, k * C * B:(k + 1) * C * B].rearrange(
                        "p (c b) -> p c b", c=C), ada_b[:, layer, vec].unsqueeze(2).to_broadcast([P, C, B]), ALU.add)
                ins_.then_inc(mod_raw, 1)
                dve.wait_ge(mod_raw, layer + 1)
                if layer == 0:
                    dve.wait_ge(mod_tanh, 2)
                    link(v.tensor_scalar(modv[:, 2], modv[:, 2], 0.1, None, ALU.mult))
                    link(v.tensor_scalar(modv[:, 5], modv[:, 5], 0.1, None, ALU.mult))
                if layer == 2:
                    link(v.memset(modv[:, 2], 1.0))
                    link(v.memset(modv[:, 5], 1.0))
                def vector_of(mod, k):
                    return mod[:, layer * PAIRS:(layer + 1) * PAIRS, :, :, k].rearrange("p n b c -> p c (n b)")

                for ln in range(2):
                    a_out, b_out = (vector_of(mod_p3, 2 + k) if ln else vector_of(mod_p0, k) for k in range(2))
                    gate, gb = vector_of(mod_p3, 4 * ln), vector_of(mod_p3, 4 * ln + 1)
                    shift_v, scale_v, gate_v = modv[:, 3 * ln], modv[:, 3 * ln + 1], modv[:, 3 * ln + 2]
                    if layer == 0:
                        g_ = ln_gb[:, 2 * ln].unsqueeze(2).to_broadcast([P, C, B])
                        b_ = ln_gb[:, 2 * ln + 1].unsqueeze(2).to_broadcast([P, C, B])
                        link(v.tensor_scalar(scale_v, scale_v, 1.0, None, ALU.add))
                        link(v.tensor_tensor(a_out, scale_v, g_, ALU.mult))
                        link(v.tensor_tensor(modt[:], scale_v, b_, ALU.mult))
                        link(v.tensor_tensor(b_out, modt[:], shift_v, ALU.add))
                    else:
                        link(v.tensor_scalar(a_out, scale_v, 1.0, None, ALU.add))
                        link(v.tensor_copy(b_out, shift_v))
                    link(v.tensor_copy(gate, gate_v))
                    ob = out_b[:, layer, ln].unsqueeze(2).to_broadcast([P, C, B])
                    last = v.tensor_tensor(gb, gate_v, ob, ALU.mult)
                    link(last) if ln == 0 else last.then_inc(mod_done, 1)
            dve.wait_ge(mod_done, LAYERS)

            def step(n, first):
                prep = Chain(dve, prep_chain, n, 5).link
                dve.wait_ge(adj_in, 16 * (n + 1))
                prep(v.tensor_reduce(vb[:], adj[:], AX_X, ALU.add))
                v.tensor_scalar(keep[:].rearrange("p u m -> p (u m)"), vb[:], 0.0, None, ALU.is_gt).then_inc(adj_used, 1)
                prep(v.tensor_tensor(prod[:], adj[:], lab[:, 0:L].unsqueeze(1).to_broadcast([P, TILES * 2 * NK, L]), ALU.mult))
                prep(v.tensor_reduce(vb[:], prod[:], AX_X, ALU.add))
                dve.wait_ge(adj_used, 2 * n + 1)
                prep(v.tensor_scalar(neg[:], keep[:].rearrange("p u m -> p (u m)"), -NEG, NEG, ALU.mult, ALU.add))
                v.scalar_tensor_tensor(shift[:].rearrange("p u m -> p (u m)"), vb[:], lab[:, L:L + 1], neg[:],
                                       ALU.add, ALU.add).then_inc(adj_used, 1)
                dve.wait_ge(x_copied, n + 1)
                prep(v.tensor_reduce(rsum[:], x_tok[:], AX_X, ALU.add))
                v.tensor_scalar(nz[:], rsum[:], 0.0, None, ALU.not_equal).then_inc(nz_ready, 1)
                src, done = wait_full(dve, "nz", n)
                v.tensor_copy(nzb[:], src[:]).then_inc(done, 1)
                dve.wait_ge(done, uses.use("nz", n)[1] + 1)
                for oc in range(C):
                    src, done = wait_full(dve, f"s{oc}", n)
                    for b in range(2):
                        t = slice(b * N, (b + 1) * N)
                        last = v.scalar_tensor_tensor(st[:, oc, t], nzb[:, t], qw[:, oc, n, b:b + 1], src[:, t],
                                                      ALU.mult, ALU.add)
                    last.then_inc(done, 1)
                for i in range(2 * C):
                    src, done = wait_full(dve, f"q{i}", n)
                    if i >= 2 or not first:
                        dve.wait_ge(q_lo_done, 2 * C * n + i - 1)
                    v.tensor_scalar(q_f[:, i % 2], src[:], gbias[:, 1 + i // C, i % C:i % C + 1], QSCALE,
                                    ALU.add, ALU.mult).then_inc(done, 1)
                    dve.wait_ge(done, uses.use(f"q{i}", n)[1] + 1)
                    v.tensor_copy(q_hi[:, i], q_f[:, i % 2]).then_inc(q_hi_done, 1)
                kc = Chain(dve, st_chain, n, 1).link
                src, done = wait_full(dve, "k", n)
                last = v.tensor_tensor(k_f[:].rearrange("p i b m -> p i (b m)"),
                                       src[:, 0:2 * C * 2 * NK].rearrange("p (i m) -> p i m", i=2 * C),
                                       gbias[:, 3:5].rearrange("p d c -> p (d c)").unsqueeze(2).to_broadcast(
                                           [P, 2 * C, 2 * NK]), ALU.add)
                last.then_inc(done, 1)
                dve.wait_ge(done, uses.use("k", n)[1] + 1)
                for b in range(2):
                    for i in range(2 * C):
                        last = v.tensor_tensor(kbd[:, b, i].rearrange("p (h m) -> p h m", h=HC),
                                               k_f[:, i, b].unsqueeze(1).to_broadcast([P, HC, NK]),
                                               sel8[:].unsqueeze(2).to_broadcast([P, HC, NK]), ALU.mult)
                kc(last)
                v.tensor_copy(kbd_hi[:], kbd[:]).then_inc(kbd_split, 1)
                dve.wait_ge(kbd_split, 2 * n + 1)
                v.tensor_tensor(kbd_lo[:], kbd[:], kbd_hi[:].bitcast(F32), ALU.subtract).then_inc(kbd_split, 1)
                for d in range(2):
                    src, done = wait_full(dve, f"v{d}", n)
                    last = v.tensor_tensor(vbd[:, d].rearrange("p b g (h r) -> p (b g) h r", h=GH),
                                           src[0:GR].rearrange("p (q h r) -> p q h r", h=GH, r=DH),
                                           sel80[:].unsqueeze(1).unsqueeze(3).to_broadcast([GR, 2 * G, GH, DH]), ALU.mult)
                    last.then_inc(done, 1)
                soft = Chain(dve, soft_chain, n, 3 * NU).link
                def tail(u):
                    dve.wait_ge(exped, NU * n + u + 1)
                    soft(v.tensor_reduce(den[:, u], e[:, u], AX_X, ALU.add))
                    v.reciprocal(den[:, u], den[:, u]).then_inc(dens, 1)

                for u in range(NU):
                    src, done = wait_full(dve, f"aff{u}", n)
                    if u >= 2:
                        dve.wait_ge(exped, NU * n + u - 1)
                    elif not first:
                        dve.wait_ge(exped, NU * n)
                    a = aff[:, u % 2]
                    v.tensor_tensor(a, src[:, 0:H * NK].rearrange("p (h m) -> p h m", h=H),
                                    keep[:, u].unsqueeze(1).to_broadcast([P, H, NK]), ALU.mult).then_inc(done, 1)
                    dve.wait_ge(done, uses.use(f"aff{u}", n)[1] + 1)
                    soft(v.tensor_tensor(a, a, shift[:, u].unsqueeze(1).to_broadcast([P, H, NK]), ALU.add))
                    soft(v.tensor_reduce(mx[:], a, AX_X, ALU.max))
                    v.tensor_tensor(a, a, mx[:].unsqueeze(2).to_broadcast([P, H, NK]), ALU.subtract).then_inc(shifted, 1)
                    if u >= 1:
                        tail(u - 1)
                tail(NU - 1)
                for c in range(C):
                    src, done = wait_full(dve, f"out{c}", n)
                    v.tensor_tensor(feat[:, c], src[:], st[:, c], ALU.add).then_inc(done, 1)
                for i in range(2):
                    src, done = wait_full(dve, f"back{i}", n)
                    xs = xres[:, n, 2 * i:2 * i + 2, :]
                    v.tensor_tensor(xs, src[:].rearrange("p (t f) -> p t f", t=2), xs, ALU.add).then_inc(done, 1)

            pair_loop(dve, step)

        @block.scalar
        def _(act):
            a = nc.scalar
            act.wait_ge(consts, 160)
            a.activation(cond_silu[:], cond[:], ACT.Silu).then_inc(silu, 1)
            act.wait_ge(mod_raw, 1)
            a.activation(modv[:, 2], modv[:, 2], ACT.Tanh).then_inc(mod_tanh, 1)
            a.activation(modv[:, 5], modv[:, 5], ACT.Tanh).then_inc(mod_tanh, 1)

            def step(n, first):
                if first:
                    act.wait_ge(x_in[0], 16)
                else:
                    for i in (0, 1):
                        act.wait_ge(full[i], uses.use(f"xt{i}", n - 1)[1] + 1)
                    act.wait_ge(nz_ready, n)
                a.copy(x_tok[:], xres[:, n]).then_inc(x_copied, 1)
                for c in range(C):
                    src, done = wait_full(act, f"xt{c}", n)
                    if c == 0 and not first:
                        for i in (6, 7):
                            act.wait_ge(full[i], uses.use(f"back{i - 6}", n - 1)[1] + 1)
                    a.copy(feat[:, c], src[:]).then_inc(done, 1)
                for oc in range(C):
                    act.wait_ge(free[3 + oc], uses.use(f"s{oc}", n)[1] + 1)
                    a.activation(st[:, oc], st[:, oc], ACT.Identity, bias=gbias[:, 0, oc:oc + 1]).then_inc(s_ready, 1)
                for u in range(NU):
                    act.wait_ge(shifted, NU * n + u + 1)
                    a.activation(e[:, u], aff[:, u % 2], ACT.Exp).then_inc(exped, 1)
                for i in range(2 * G):
                    src, done = wait_full(act, f"wt{i}", n)
                    a.copy(wt[:, i // G, i % G], src[0:GR]).then_inc(done, 1)
                for c in range(C):
                    act.wait_ge(free[2 + c], uses.use(f"out{c}", n)[1] + 1)
                    a.activation(feat[:, c], feat[:, c], ACT.Relu, bias=bout[:, c:c + 1]).then_inc(relu_out, 1)

            act.wait_ge(ready, 3)
            step(0, True)
            for i in range(1, PAIRS):
                act.wait_ge(x_in[i], 16)
            with act.Fori(1, PAIRS) as n:
                step(n, False)

        @block.gpsimd
        def _(pool):
            g = nc.gpsimd

            def split(hi, lo, src, sem_, base):
                settle(pool, passed, base)
                g.tensor_scalar(hi, src, 1.0, None, ALU.mult).then_inc(sem_, 1)
                pool.wait_ge(sem_, base + 1)
                g.tensor_tensor(lo, src, hi.bitcast(F32), ALU.subtract).then_inc(sem_, 1)

            def step(n, first):
                for c in range(C):
                    pool.wait_ge(free[c], uses.use(f"xt{c}", n)[1] + 1)
                    if c == 0 and not first:
                        pool.wait_ge(full[4], uses.use("s1", n - 1)[1] + 1)
                    split(f_hi[:, c], f_lo[:, c], feat[:, c], xt_split, 2 * C * n + 2 * c)
                if not first:
                    pool.wait_ge(full[1], uses.use("k", n - 1)[1] + 1)
                for c in range(C):
                    pool.wait_ge(s_ready, C * n + c + 1)
                    split(s_hi[:, c], s_lo[:, c], st[:, c], s_split, 2 * C * n + 2 * c)
                if not first:
                    pool.wait_ge(full[3], uses.use("v1", n - 1)[1] + 1)
                for k, part in enumerate((s_hi, s_lo)):
                    pool.wait_ge(s_split, 2 * C * (n + 1))
                    settle(pool, passed, n)
                    for c in range(C):
                        for b in range(2):
                            last = g.tensor_copy(s_rep[:, k, c, b].rearrange("p (h m) -> p h m", h=GH),
                                                 part[:, c, b * N:b * N + NK].unsqueeze(1).to_broadcast([P, GH, NK]))
                    last.then_inc(rep_ready, 1)
                for i in range(2 * C):
                    pool.wait_ge(q_hi_done, 2 * C * n + i + 1)
                    g.tensor_tensor(q_lo[:, i], q_f[:, i % 2], q_hi[:, i].bitcast(F32), ALU.subtract).then_inc(q_lo_done, 1)
                for u in range(NU):
                    pool.wait_ge(dens, NU * n + u + 1)
                    g.tensor_tensor(e[:, u], e[:, u], den[:, u].unsqueeze(2).to_broadcast([P, H, NK]),
                                    ALU.mult).then_inc(weights, 1)

            pair_loop(pool, step)



P3A = [("otm0", 0), ("otm1", 1), ("otm2", 2), ("otm3", 0), ("ofm0", 1), ("ofm1", 2)]
P0E = [("ln1_0", 0), ("ln1_1", 1)]
P3B = [("proj0", 2), ("proj1", 0)]
P0Q0 = [("qk0", 1)]
P3C = [("xa0", 2), ("xa1", 0)]
P0Q1 = [("qk1", 1), ("qk2", 2), ("qk3", 0)]
P3D = [("ln2_0", 1), ("ln2_1", 2)] + [(f"fc1_{j}", 2) for j in range(2)] + [("fc2_0", 0), ("fc2_1", 1)] \
    + [(f"fc1_{j}", 2) for j in range(2, J)] + [("xb0", 2), ("xb1", 0)]
PV = [("v0", 1), ("v1", 2)]
PRELUDE = P0E + P0Q0 + P0Q1 + PV
FIRST = PRELUDE
MIDDLE = P3A + P0E + P3B + P0Q0 + P3C + P0Q1 + P3D + PV
BACK = P3A + P3B + P3C + P3D


def transformer_layers(nc, ins, xres, mod_p0, mod_p3, ident, identb, out_dram, scr_qk, scr_max, scr_mask):
    STEPS = LAYERS * PAIRS
    with ExitStack() as ctx:
        def sb(name, shape, dt=F32):
            return ctx.enter_context(nc.sbuf_tensor("t_" + name, shape, dt))

        def sem(name):
            return ctx.enter_context(nc.semaphore("t_" + name))

        def ps(name):
            return ctx.enter_context(nc.psum_tensor("t_" + name, [P, 512], F32))

        lin = [ps(f"lin{i}") for i in range(3)]
        mxb = [ps(f"mxb{i}") for i in range(2)]
        scb = [ps(f"scb{i}") for i in range(2)]
        avb = ps("avb")

        w0_hi = sb("w0_hi", [P, C, 3 * D], F32R)
        w0_lo = sb("w0_lo", [P, C, 3 * D], F32R)
        wp_hi = sb("wp_hi", [P, C, D], F32R)
        wp_lo = sb("wp_lo", [P, C, D], F32R)
        w1_hi = sb("w1_hi", [P, C, DFF], F32R)
        w1_lo = sb("w1_lo", [P, C, DFF], F32R)
        w2_hi = sb("w2_hi", [P, J, D], F32R)
        w2_lo = sb("w2_lo", [P, J, D], F32R)
        raw = sb("raw", [P, 2, W_CHUNK])
        bias0 = sb("bias0", [P, 2 * C])
        bias3 = sb("bias3", [P, C + J])
        m0 = sb("m0", [P, 2, C, 2])
        m3 = sb("m3", [P, 2, C, 6])
        stats = sb("stats", [P, 2, TILES, 6])
        mv = sb("mv", [P, 2, TILES, 2])
        var = sb("var", [P, 2, TILES])
        rstd = sb("rstd", [P, 2, TILES])
        mhalf = sb("mhalf", [P, TILES])
        xh0 = sb("xh0", [P, TILES, D])
        xh3 = sb("xh3", [P, TILES, D])
        h0 = sb("h0", [P, C, T])
        h0_hi = sb("h0_hi", [P, C, T], F32R)
        h0_lo = sb("h0_lo", [P, C, T], F32R)
        h3 = sb("h3", [P, C, T])
        h3_hi = sb("h3_hi", [P, C, T], F32R)
        h3_lo = sb("h3_lo", [P, C, T], F32R)
        qf = sb("qf", [P, T])
        qr = sb("qr", [P, 2, T])
        parts = sb("parts", [P, 2, PARTS, T], BF16)
        qp = [sb(f"qp{b}", [KM, H, N], BF16) for b in range(2)]
        kp = [sb(f"kp{b}", [KM, H, N], BF16) for b in range(2)]
        vaug = sb("vaug", [P, TILES, H, 2 * DH])
        mx = sb("mx", [P, BT, H])
        mr = sb("mr", [P, BT, H])
        mm_parts = sb("mm_parts", [P, BT, PARTS, H], BF16)
        mt = sb("mt", [PARTS * H, N], BF16)
        prob = sb("prob", [P, RING, BT * N])
        oe = sb("oe", [P, 2, G, N])
        rden = sb("rden", [P, TILES, H])
        gl = sb("gl", [P, 2, T])
        g_hi = sb("g_hi", [P, 2, T], F32R)
        g_lo = sb("g_lo", [P, 2, T], F32R)

        full = [sem(f"lin_full{i}") for i in range(3)]
        free = [sem(f"lin_free{i}") for i in range(3)]
        mx_full, mx_free, sc_full, exped, av_full, av_free = (
            sem("mx_full"), sem("mx_free"), sem("sc_full"), sem("exped"), sem("av_full"), sem("av_free"))
        raw_in = [sem(f"raw_in{i}") for i in range(2)]
        w_split, bias0_in, bias3_in, ready = sem("w_split"), sem("bias0_in"), sem("bias3_in"), sem("ready")
        m0_ready, m3_ready = sem("m0_ready"), sem("m3_ready")
        st0, st3, rstd0, rstd3, xh0_ready, xh3_ready = (
            sem("st0"), sem("st3"), sem("rstd0"), sem("rstd3"), sem("xh0_ready"), sem("xh3_ready"))
        h0_split, o_split, h3_split, gelu_split = sem("h0_split"), sem("o_split"), sem("h3_split"), sem("gelu_split")
        qk_chain, part3, scr_in = sem("qk_chain"), sem("part3"), [sem("scr_in0"), sem("scr_in1")]
        pack_in = [sem("pack_in0"), sem("pack_in1")]
        max_chain, mt_scr, mrow_in = sem("max_chain"), sem("mt_scr"), [sem("mrow_in0"), sem("mrow_in1")]
        rden_chain, fc2_read = sem("rden_chain"), sem("fc2_read")
        outs, half_ready = sem("outs"), sem("half_ready")
        passed = sem("passed")

        nothing = {i: 0 for i in range(3)}
        prelude = Banks(PRELUDE, nothing)
        first_ = Banks(FIRST, prelude.after(1))
        middle_ = Banks(MIDDLE, first_.after(1))
        last_ = Banks(P3A + P3B + P3C + P3D, middle_.after(STEPS - 2))
        tail_ = Banks(BACK, last_.after(1))

        class Kind:

            def __init__(self, banks, at):
                self.banks, self.at = banks, at

            def full(self, eng, name):
                i, k = self.banks.use(name, self.at)
                eng.wait_ge(full[i], k + 1)
                return lin[i], free[i]

            def read(self, eng, name):
                i, k = self.banks.use(name, self.at)
                eng.wait_ge(free[i], k + 1)

            def take(self, pe, name):
                i, k = self.banks.use(name, self.at)
                if not isinstance(k, int) or k > 0:
                    pe.wait_ge(free[i], k)
                return lin[i], full[i]

        PACKS = len(Q_PART) + len(K_PART) + 1
        PRE = Kind(prelude, 0)
        FST = Kind(first_, 0)
        LST = Kind(last_, 0)
        TAIL = Kind(tail_, 0)

        W0_CHUNKS = C * 3 * D // W_CHUNK
        W3_CHUNKS = (C * D + C * DFF + J * D) // W_CHUNK

        def schedule(eng, prelude_, body, back, switch0, switch3):
            switch0(0)
            prelude_()
            switch3(0)
            body(0, FST, 1, None)
            with eng.Fori(0, PAIRS - 2) as i:
                body(i + 1, Kind(middle_, i), i + 2, i)
            with eng.Fori(1, LAYERS) as l:
                switch0(l)
                with eng.Fori(0, 2) as i:
                    t = l * PAIRS + i - 1
                    body(t, Kind(middle_, t - 1), i, i + PAIRS - 2)
                switch3(l)
                with eng.Fori(0, PAIRS - 2) as i:
                    t = l * PAIRS + i + 1
                    body(t, Kind(middle_, t - 1), i + 2, i)
            body(STEPS - 1, LST, None, PAIRS - 2)
            back(STEPS - 1, TAIL, PAIRS - 1)

        block = ctx.enter_context(nc.Block())

        @block.tensor
        def _(pe):
            def mmx(out, w_hi, w_lo, oc, hi, lo):
                o = slice(oc * P, (oc + 1) * P)
                for c in range(C):
                    mm = mm3(pe, out, w_hi[:, c, o], w_lo[:, c, o], hi[:, c], lo[:, c], c == 0, c == C - 1)
                return mm

            def to_features(kind, name, src, c):
                out, done = kind.take(pe, name)
                for i in range(TILES):
                    mm = pe.transpose(out[:, i * P:(i + 1) * P], src[:, i, c * P:(c + 1) * P], ident[:])
                mm.then_inc(done, 1)

            def to_tokens(kind, name, i):
                out, done = kind.take(pe, name)
                for tt in range(2):
                    for c in range(C):
                        t = slice((2 * i + tt) * P, (2 * i + tt + 1) * P)
                        mm = pe.transpose(out[:, tt * D + c * P:tt * D + (c + 1) * P], h3[:, c, t], ident[:])
                mm.then_inc(done, 1)

            def ln1(kind, n):
                pe.wait_ge(xh0_ready, TILES * (n + 1))
                for c in range(C):
                    to_features(kind, f"ln1_{c}", xh0, c)

            def qk(kind, n, i):
                pe.wait_ge(h0_split, 2 * C * (n + 1))
                out, done = kind.take(pe, f"qk{i}")
                mmx(out[:], w0_hi, w0_lo, i, h0_hi, h0_lo).then_inc(done, 1)

            def values(kind, n, b):
                pe.wait_ge(h0_split, 2 * C * (n + 1))
                out, done = kind.take(pe, f"v{b}")
                for i in range(BT):
                    t = slice(b * N + i * P, b * N + (i + 1) * P)
                    for c in range(C):
                        mm = mm3(pe, out[:, i * D:(i + 1) * D], h0_hi[:, c, t], h0_lo[:, c, t],
                                 w0_hi[:, c, 2 * D:], w0_lo[:, c, 2 * D:], c == 0, c == C - 1)
                mm.then_inc(done, 1)

            def max_scores(t, first, b, h):
                u = h if b == 0 else H + h + (h >= 4)
                if h == 0:
                    pe.wait_ge(pack_in[b], 16 * PACKS * (t + 1))
                if u >= 2 or not first:
                    pe.wait_ge(mx_free, (UNITS + 2) * t + u - 1)
                for i in range(BT):
                    mm = pe.matmul(mxb[u % 2][:, i * N:(i + 1) * N], qp[b][0:KA, h, i * P:(i + 1) * P], kp[b][0:KA, h, :],
                                   start=True, stop=True)
                mm.then_inc(mx_full, 1)

            def max_rows(t, b):
                u = 20 if b == 0 else UNITS + 1
                pe.wait_ge(max_chain, 8 * t + 4 * b + 4)
                pe.wait_ge(mx_free, (UNITS + 2) * t + u - 1)
                settle(pe, passed, t)
                out = mxb[u % 2][0:PARTS * H, 0:N // 2].bitcast(BF16)
                for i in range(BT):
                    mm = pe.transpose(out[:, i * P:(i + 1) * P], mm_parts[:, i].rearrange("p k h -> p (k h)"), identb[:])
                mm.then_inc(mx_full, 1)

            def exp_scores(t, first, b, h):
                u = b * H + h
                if h == 0:
                    pe.wait_ge(mrow_in[b], 16 * (t + 1))
                if u >= 2 or not first:
                    pe.wait_ge(exped, UNITS * t + u - 1)
                for i in range(BT):
                    mm = pe.matmul(scb[u % 2][:, i * N:(i + 1) * N], kp[b][:, h, i * P:(i + 1) * P], qp[b][:, h, :],
                                   start=True, stop=True)
                mm.then_inc(sc_full, 1)

            def attend(t, first, gg):
                b, g = gg // G, gg % G
                pe.wait_ge(exped, UNITS * t + GH * (gg + 1))
                if gg or not first:
                    pe.wait_ge(av_free, 2 * G * t + gg)
                for i in range(BT):
                    for hh in range(GH):
                        mm = pe.matmul(avb[32 * hh:32 * hh + 32, 0:N], vaug[:, b * BT + i, g * GH + hh, :],
                                       prob[:, (gg * GH + hh) % RING, i * N:(i + 1) * N], start=(i == 0), stop=(i == BT - 1),
                                       skip_group_check=True)
                mm.then_inc(av_full, 1)

            def o_tokens(kind, n, i):
                pe.wait_ge(av_free, 2 * G * n + G * (i // BT + 1))
                out, done = kind.take(pe, f"otm{i}")
                for g in range(G):
                    mm = pe.transpose(out[:, g * P:(g + 1) * P], oe[:, i // BT, g, (i % BT) * P:(i % BT + 1) * P], ident[:])
                mm.then_inc(done, 1)

            def o_features(kind, n, b):
                for i in range(BT):
                    kind.read(pe, f"otm{b * BT + i}")
                out, done = kind.take(pe, f"ofm{b}")
                for c in range(C):
                    for i in range(BT):
                        mm = pe.transpose(out[:, c * N + i * P:c * N + (i + 1) * P], xh3[:, b * BT + i, c * P:(c + 1) * P],
                                          ident[:])
                mm.then_inc(done, 1)

            def project(kind, n, oc):
                pe.wait_ge(o_split, 2 * C * (n + 1))
                out, done = kind.take(pe, f"proj{oc}")
                mmx(out[:], wp_hi, wp_lo, oc, h3_hi, h3_lo).then_inc(done, 1)

            def x_mid_back(kind, n, i):
                for oc in range(C):
                    kind.read(pe, f"proj{oc}")
                to_tokens(kind, f"xa{i}", i)

            def ln2(kind, n):
                pe.wait_ge(xh3_ready, TILES * (n + 1))
                for c in range(C):
                    to_features(kind, f"ln2_{c}", xh3, c)

            def fc1(kind, n, j):
                pe.wait_ge(h3_split, 2 * C * (n + 1))
                out, done = kind.take(pe, f"fc1_{j}")
                mmx(out[:], w1_hi, w1_lo, j, h3_hi, h3_lo).then_inc(done, 1)

            def fc2(kind, n, j):
                pe.wait_ge(gelu_split, 2 * J * n + 2 * (j + 1))
                for oc in range(C):
                    i, k = kind.banks.use(f"fc2_{oc}", kind.at)
                    if j == 0:
                        kind.take(pe, f"fc2_{oc}")
                    o = slice(oc * P, (oc + 1) * P)
                    mm = mm3(pe, lin[i][:], w2_hi[:, j, o], w2_lo[:, j, o], g_hi[:, j % 2], g_lo[:, j % 2], j == 0, j == J - 1)
                    if j == J - 1:
                        mm.then_inc(full[i], 1)
                if j < J - 1:
                    mm.then_inc(fc2_read, 1)

            def x_out_back(kind, n, i):
                for oc in range(C):
                    kind.read(pe, f"fc2_{oc}")
                to_tokens(kind, f"xb{i}", i)

            def switch0(l):
                pe.wait_ge(w_split, 2 * ((W0_CHUNKS + W3_CHUNKS) * l + W0_CHUNKS))
                settle(pe, passed, l)

            def switch3(l):
                pe.wait_ge(w_split, 2 * (W0_CHUNKS + W3_CHUNKS) * (l + 1))
                settle(pe, passed, l)

            def prelude_():
                pe.wait_ge(ready, 5)
                ln1(PRE, 0)
                for i in range(2 * C):
                    qk(PRE, 0, i)
                for b in range(2):
                    values(PRE, 0, b)

            def mlp(kind, n, extra):
                fc1(kind, n, 0)
                for j in range(J):
                    if j + 1 < J:
                        fc1(kind, n, j + 1)
                    extra(j)
                    fc2(kind, n, j)
                for i in range(2):
                    x_out_back(kind, n, i)

            def attention(kind, t, first, p0):
                for u in range(UNITS):
                    if u < 4:
                        max_scores(t, first, 1, 12 + u)
                    if u == 6:
                        max_rows(t, 1)
                    exp_scores(t, first, u // H, u % H)
                    if u % GH == 1 and u > GH:
                        attend(t, first, u // GH - 1)
                    if u == 20 and p0:
                        values(kind, t + 1, 0)
                attend(t, first, 2 * G - 1)
                if p0:
                    values(kind, t + 1, 1)

            def body(t, kind, x0, x3):
                first = x3 is None
                maxes = iter([(0, h) for h in range(H)] + [(1, h) for h in range(12)])

                def some(k):
                    for _ in range(k):
                        max_scores(t, first, *next(maxes))

                if not first:
                    for i in range(TILES):
                        o_tokens(kind, t - 1, i)
                    for b in range(2):
                        o_features(kind, t - 1, b)
                if x0 is not None:
                    ln1(kind, t + 1)
                if not first:
                    for oc in range(C):
                        project(kind, t - 1, oc)
                if x0 is not None:
                    qk(kind, t + 1, 0)
                if not first:
                    for i in range(2):
                        x_mid_back(kind, t - 1, i)
                for i in range(1, 2 * C):
                    if x0 is not None:
                        qk(kind, t + 1, i)
                    some(2)
                if not first:
                    ln2(kind, t - 1)
                some(10)
                if not first:
                    def extra(j):
                        if j < 4:
                            some(1)
                        if j == 4:
                            max_rows(t, 0)
                        if j >= 4:
                            some(2)
                    mlp(kind, t - 1, extra)
                else:
                    some(4)
                    max_rows(t, 0)
                    some(8)
                attention(kind, t, first, x0 is not None)

            def back(t, kind, x3):
                for i in range(TILES):
                    o_tokens(kind, t, i)
                for b in range(2):
                    o_features(kind, t, b)
                for oc in range(C):
                    project(kind, t, oc)
                for i in range(2):
                    x_mid_back(kind, t, i)
                ln2(kind, t)
                mlp(kind, t, lambda j: None)

            schedule(pe, prelude_, body, back, switch0, switch3)

        @block.vector
        def _(dve):
            v = nc.vector

            def layer_norm(x, k, n, st, rstd_ready, xh, ready_):
                for i in range(TILES):
                    v.bn_stats(stats[:, k, i], x[:, i]).then_inc(st, 1)
                for i in range(TILES):
                    if i == 0:
                        dve.wait_ge(st, (2 * TILES + 1) * n + TILES)
                        settle(dve, passed, n)
                    v.bn_aggr(mv[:, k, i], stats[:, k, i]).then_inc(st, 1)
                dve.wait_ge(st, (2 * TILES + 1) * n + 2 * TILES)
                v.tensor_scalar(var[:, k], mv[:, k, :, 1], EPS, None, ALU.add).then_inc(st, 1)
                dve.wait_ge(rstd_ready, n + 1)
                for i in range(TILES):
                    v.tensor_scalar(xh[:, i], x[:, i], mv[:, k, i, 0:1], rstd[:, k, i:i + 1],
                                    ALU.subtract, ALU.mult).then_inc(ready_, 1)

            def front_norm(n, x0):
                v.tensor_copy(m0[:], mod_p0[:, n]).then_inc(m0_ready, 1)
                layer_norm(xres[:, x0], 0, n, st0, rstd0, xh0, xh0_ready)

            def qk(kind, n, i):
                src, done = kind.full(dve, f"qk{i}")
                link = Chain(dve, qk_chain, n, 3 * 2 * C, 3 * i).link
                if not isinstance(n, int) or n > 0 or i >= 2:
                    dve.wait_ge(scr_in[i % 2], 16 * (2 * n + i // 2))
                    dve.wait_ge(part3, 2 * C * n + i - 1)
                p = parts[:, i % 2]
                last = v.tensor_scalar(qf[:], src[:], bias0[:, i:i + 1], QSCALE if i < C else 1.0, ALU.add, ALU.mult)
                last.then_inc(done, 1)
                kind.read(dve, f"qk{i}")
                link(v.tensor_copy(p[:, 0], qf[:]))
                link(v.tensor_tensor(qr[:, i % 2], qf[:], p[:, 0], ALU.subtract))
                v.tensor_copy(p[:, 1], qr[:, i % 2]).then_inc(qk_chain, 1)

            def values(kind, n, b):
                src, done = kind.full(dve, f"v{b}")
                if not isinstance(n, int) or n > 0:
                    dve.wait_ge(av_full, 2 * G * n - (0 if b else G))
                v.tensor_copy(vaug[:, b * BT:(b + 1) * BT, :, 0:DH],
                              src[:].rearrange("p (i h d) -> p i h d", i=BT, h=H)).then_inc(done, 1)
                kind.read(dve, f"v{b}")

            def row_max(t, b, h):
                u = h if b == 0 else H + h + (h >= 4)
                dve.wait_ge(mx_full, (UNITS + 2) * t + u + 1)
                v.tensor_reduce(mx[:, :, h], mxb[u % 2][:].rearrange("p (i k) -> p i k", i=BT), AX_X,
                                ALU.max).then_inc(mx_free, 1)

            def max_parts(t, b):
                dve.wait_ge(mx_free, (UNITS + 2) * t + (H if b == 0 else UNITS + 1))
                link = Chain(dve, max_chain, t, 8, 4 * b).link
                link(v.tensor_scalar(mm_parts[:, :, 0], mx[:], -1.0, None, ALU.mult))
                link(v.scalar_tensor_tensor(mr[:], mx[:], -1.0, mm_parts[:, :, 0], ALU.mult, ALU.subtract))
                link(v.tensor_copy(mm_parts[:, :, 1], mr[:]))
                v.tensor_tensor(mm_parts[:, :, 2], mr[:], mm_parts[:, :, 1], ALU.subtract).then_inc(max_chain, 1)

            def max_rows(t, b, first):
                u = 20 if b == 0 else UNITS + 1
                dve.wait_ge(mx_full, (UNITS + 2) * t + u + 1)
                if b or not first:
                    dve.wait_ge(mt_scr, 16 * (2 * t + b))
                v.tensor_copy(mt[:], mxb[u % 2][0:PARTS * H, 0:N // 2].bitcast(BF16)).then_inc(mx_free, 1)

            def o_norm(kind, n, i):
                src, done = kind.full(dve, f"otm{i}")
                o = src[:].rearrange("p (h r) -> p h r", h=H)
                v.reciprocal(rden[:, i], o[:, :, DH]).then_inc(rden_chain, 1)
                dve.wait_ge(rden_chain, TILES * n + i + 1)
                v.tensor_tensor(xh3[:, i].rearrange("p (h d) -> p h d", h=H), o[:, :, 0:DH],
                                rden[:, i].unsqueeze(2).to_broadcast([P, H, DH]), ALU.mult).then_inc(done, 1)

            def add_x(kind, name, x3, i):
                src, done = kind.full(dve, name)
                xs = xres[:, x3, 2 * i:2 * i + 2, :]
                v.tensor_tensor(xs, src[:].rearrange("p (t f) -> p t f", t=2), xs, ALU.add).then_inc(done, 1)
                kind.read(dve, name)

            def mid_norm(kind, n, x3):
                for c in range(C):
                    kind.full(dve, f"ofm{c}")
                settle(dve, passed, n)
                layer_norm(xres[:, x3], 1, n, st3, rstd3, xh3, xh3_ready)

            def load_m3(n):
                v.tensor_copy(m3[:], mod_p3[:, n]).then_inc(m3_ready, 1)

            def split_weights(base, l, chunks, parity):
                for k, (hi, lo) in enumerate(chunks):
                    at = base + (W0_CHUNKS + W3_CHUNKS) * l + k
                    r = (parity + k) % 2
                    dve.wait_ge(raw_in[r], 16 * (((W0_CHUNKS + W3_CHUNKS) // 2) * l + (base + k) // 2 + 1))
                    v.tensor_copy(hi, raw[:, r]).then_inc(w_split, 1)
                    dve.wait_ge(w_split, 2 * at + 1)
                    v.tensor_tensor(lo, raw[:, r], hi.bitcast(F32), ALU.subtract).then_inc(w_split, 1)

            def pieces(hi, lo):
                h, o = (x[:].rearrange("p a b -> p (a b)") for x in (hi, lo))
                return [(h[:, k:k + W_CHUNK], o[:, k:k + W_CHUNK]) for k in range(0, h.shape[1], W_CHUNK)]

            def switch0(l):
                dve.wait_ge(bias0_in, 16 * (l + 1))
                split_weights(0, l, pieces(w0_hi, w0_lo), 0)

            def switch3(l):
                split_weights(W0_CHUNKS, l, pieces(wp_hi, wp_lo) + pieces(w1_hi, w1_lo) + pieces(w2_hi, w2_lo), W0_CHUNKS)

            def prelude_():
                v.memset(vaug[:, :, :, DH:], 1.0).then_inc(ready, 1)
                for b in range(2):
                    v.memset(kp[b][KR:KM], 1.0).then_inc(ready, 1)
                    v.memset(qp[b][KR:KA], 1.0).then_inc(ready, 1)
                front_norm(0, 0)
                for i in range(2 * C):
                    qk(PRE, 0, i)
                for b in range(2):
                    values(PRE, 0, b)

            def attention(kind, t, first, p0):
                for u in range(4):
                    row_max(t, 1, 12 + u)
                max_parts(t, 1)
                max_rows(t, 1, first)
                if p0:
                    for b in range(2):
                        values(kind, t + 1, b)

            def body(t, kind, x0, x3):
                first = x3 is None
                maxes = iter([(0, h) for h in range(H)] + [(1, h) for h in range(12)])

                def some(k):
                    for _ in range(k):
                        row_max(t, *next(maxes))

                if not first:
                    load_m3(t - 1)
                    for i in range(TILES):
                        o_norm(kind, t - 1, i)
                if x0 is not None:
                    front_norm(t + 1, x0)
                    qk(kind, t + 1, 0)
                if not first:
                    for i in range(2):
                        add_x(kind, f"xa{i}", x3, i)
                    mid_norm(kind, t - 1, x3)
                for i in range(1, 2 * C):
                    if x0 is not None:
                        qk(kind, t + 1, i)
                    some(2)
                some(10)
                max_parts(t, 0)
                some(4)
                max_rows(t, 0, first)
                some(8)
                if not first:
                    for i in range(2):
                        add_x(kind, f"xb{i}", x3, i)
                attention(kind, t, first, x0 is not None)

            def back(t, kind, x3):
                load_m3(t)
                for i in range(TILES):
                    o_norm(kind, t, i)
                for i in range(2):
                    add_x(kind, f"xa{i}", x3, i)
                mid_norm(kind, t, x3)
                for i in range(2):
                    add_x(kind, f"xb{i}", x3, i)

            schedule(dve, prelude_, body, back, switch0, switch3)

        @block.scalar
        def _(act):
            a = nc.scalar

            def modulate(kind, names, dst, m, scale, shift_):
                for c, name in enumerate(names):
                    src, done = kind.full(act, name)
                    for b in range(2):
                        t = slice(b * N, (b + 1) * N)
                        last = a.activation(dst[:, c, t], src[:, t], ACT.Identity, bias=m[:, b, c, shift_:shift_ + 1],
                                            scale=m[:, b, c, scale:scale + 1])
                    last.then_inc(done, 1)

            def ln1(kind, n):
                act.wait_ge(m0_ready, n + 1)
                if not isinstance(n, int) or n > 0:
                    act.wait_ge(h0_split, 2 * C * n)
                modulate(kind, ("ln1_0", "ln1_1"), h0, m0, 0, 1)

            def o_out(kind, n, b):
                src, done = kind.full(act, f"ofm{b}")
                for c in range(C):
                    last = a.activation(h3[:, c, b * N:(b + 1) * N], src[:, c * N:(c + 1) * N], ACT.Identity,
                                        bias=bias3[:, c:c + 1])
                last.then_inc(done, 1)

            def project(kind, n):
                act.wait_ge(m3_ready, n + 1)
                act.wait_ge(o_split, 2 * C * (n + 1))
                modulate(kind, ("proj0", "proj1"), h3, m3, 0, 1)

            def ln2(kind, n):
                for i in range(2):
                    kind.full(act, f"xa{i}")
                modulate(kind, ("ln2_0", "ln2_1"), h3, m3, 2, 3)

            def gelus(kind, n):
                for j in range(J):
                    src, done = kind.full(act, f"fc1_{j}")
                    if j >= 2:
                        act.wait_ge(gelu_split, 2 * J * n + 2 * (j - 1))
                    a.activation(gl[:, j % 2], src[:], ACT.Gelu, bias=bias3[:, C + j:C + j + 1]).then_inc(done, 1)
                act.wait_ge(h3_split, 2 * C * (n + 1))
                modulate(kind, ("fc2_0", "fc2_1"), h3, m3, 4, 5)

            def attention(t, first):
                for u in range(UNITS):
                    act.wait_ge(sc_full, UNITS * t + u + 1)
                    gg = u // GH
                    if gg >= 2 or not first:
                        act.wait_ge(av_full, 2 * G * t + gg - 1)
                    a.activation(prob[:, u % RING], scb[u % 2][:], ACT.Exp).then_inc(exped, 1)
                    if u % GH == 3 and u > GH:
                        o_copy(t, gg - 1)
                o_copy(t, 2 * G - 1)

            def o_copy(t, gg):
                act.wait_ge(av_full, 2 * G * t + gg + 1)
                a.copy(oe[:, gg // G, gg % G], avb[:, 0:N]).then_inc(av_free, 1)

            def switch0(l):
                pass

            def switch3(l):
                act.wait_ge(bias3_in, 16 * (l + 1))

            def prelude_():
                ln1(PRE, 0)

            def body(t, kind, x0, x3):
                first = x3 is None
                if not first:
                    for b in range(2):
                        o_out(kind, t - 1, b)
                if x0 is not None:
                    ln1(kind, t + 1)
                if not first:
                    project(kind, t - 1)
                    ln2(kind, t - 1)
                    gelus(kind, t - 1)
                attention(t, first)

            def back(t, kind, x3):
                for b in range(2):
                    o_out(kind, t, b)
                project(kind, t)
                ln2(kind, t)
                gelus(kind, t)

            schedule(act, prelude_, body, back, switch0, switch3)

        @block.gpsimd
        def _(pool):
            g = nc.gpsimd

            def split(hi, lo, src, done, base):
                settle(pool, passed, base)
                g.tensor_scalar(hi, src, 1.0, None, ALU.mult).then_inc(done, 1)
                pool.wait_ge(done, base + 1)
                g.tensor_tensor(lo, src, hi.bitcast(F32), ALU.subtract).then_inc(done, 1)

            def power(k, n, st, ready_):
                pool.wait_ge(st, (2 * TILES + 1) * (n + 1))
                g.tensor_tensor(rstd[:, k], var[:, k], mhalf[:], ALU.pow).then_inc(ready_, 1)

            def front(kind, n, prev_v):
                for c in range(C):
                    kind.read(pool, f"ln1_{c}")
                    split(h0_hi[:, c], h0_lo[:, c], h0[:, c], h0_split, 2 * C * n + 2 * c)

            def third(kind, n, i):
                pool.wait_ge(qk_chain, 3 * 2 * C * n + 3 * (i + 1))
                g.tensor_tensor(parts[:, i % 2, 2], qr[:, i % 2], parts[:, i % 2, 1], ALU.subtract).then_inc(part3, 1)

            def back_o(kind, n):
                for b in range(2):
                    kind.read(pool, f"ofm{b}")
                for c in range(C):
                    split(h3_hi[:, c], h3_lo[:, c], h3[:, c], o_split, 2 * C * n + 2 * c)

            def back_ln2(kind, n):
                for c in range(C):
                    kind.read(pool, f"ln2_{c}")
                    split(h3_hi[:, c], h3_lo[:, c], h3[:, c], h3_split, 2 * C * n + 2 * c)

            def back_gelu(kind, n):
                for j in range(J):
                    kind.read(pool, f"fc1_{j}")
                    if j >= 2:
                        pool.wait_ge(fc2_read, (J - 1) * n + j - 1)
                    split(g_hi[:, j % 2], g_lo[:, j % 2], gl[:, j % 2], gelu_split, 2 * J * n + 2 * j)

            def switch0(l):
                pass

            def switch3(l):
                pass

            def prelude_():
                g.memset(mhalf[:], -0.5).then_inc(half_ready, 1)
                pool.wait_ge(half_ready, 1)
                power(0, 0, st0, rstd0)
                front(PRE, 0, None)
                for i in range(2 * C):
                    third(PRE, 0, i)

            def body(t, kind, x0, x3):
                first = x3 is None
                if x0 is not None:
                    power(0, t + 1, st0, rstd0)
                if not first:
                    back_o(kind, t - 1)
                if x0 is not None:
                    front(kind, t + 1, None)
                    third(kind, t + 1, 0)
                if not first:
                    power(1, t - 1, st3, rstd3)
                if x0 is not None:
                    for i in range(1, 2 * C):
                        third(kind, t + 1, i)
                if not first:
                    back_ln2(kind, t - 1)
                    back_gelu(kind, t - 1)

            def back(t, kind, x3):
                back_o(kind, t)
                power(1, t, st3, rstd3)
                back_ln2(kind, t)
                back_gelu(kind, t)

            schedule(pool, prelude_, body, back, switch0, switch3)

        @block.sync
        def _(sp):
            CHUNKS = W0_CHUNKS + W3_CHUNKS

            def load_weights(l, chunks):
                for m in chunks:
                    if m >= 2 or not isinstance(l, int):
                        sp.wait_ge(w_split, 2 * (CHUNKS * l + m - 1))
                    sp.dma_start(raw[:, m % 2], ins["tw"][l, :, m]).then_inc(raw_in[m % 2], 16)

            def switch0(l):
                if not isinstance(l, int):
                    sp.wait_ge(part3, 2 * C * PAIRS * l)
                sp.dma_start(bias0[:], ins["tbias"][l, :, 0:2 * C]).then_inc(bias0_in, 16)
                load_weights(l, range(W0_CHUNKS))

            def switch3(l):
                if not isinstance(l, int):
                    sp.wait_ge(gelu_split, 2 * J * PAIRS * l)
                sp.dma_start(bias3[:], ins["tbias"][l, :, 2 * C:]).then_inc(bias3_in, 16)
                load_weights(l, range(W0_CHUNKS, CHUNKS))

            def scratch(n, first):
                for i in range(2 * C):
                    if i == 0 and not first:
                        for b in range(2):
                            sp.wait_ge(pack_in[b], 16 * PACKS * n)
                    sp.wait_ge(part3, 2 * C * n + i + 1)
                    sp.dma_start(scr_qk[i // C, :, (i % C) * P:(i % C + 1) * P, :].rearrange("k p t -> p k t"),
                                 parts[:, i % 2]).then_inc(scr_in[i % 2], 16)

            def pack(n, b, first):
                for r in range(2):
                    sp.wait_ge(scr_in[r], 16 * 2 * (n + 1))
                if not first:
                    sp.wait_ge(sc_full, UNITS * n - (0 if b else H))
                for side, dst, which in ((0, qp[b], Q_PART), (1, kp[b], K_PART)):
                    for j, part in enumerate(which):
                        src = scr_qk[side, part].rearrange("(h d) t -> d h t", d=DH)[:, :, b * N:(b + 1) * N]
                        sp.dma_start(dst[16 * j:16 * (j + 1)], src).then_inc(pack_in[b], 16)
                mask = scr_mask[2 * n + b].unsqueeze(0).unsqueeze(0).to_broadcast([1, H, N])
                sp.dma_start(kp[b][KR:KA], mask).then_inc(pack_in[b], 16)

            def max_rows(t, b):
                u = 20 if b == 0 else UNITS + 1
                sp.wait_ge(mx_free, (UNITS + 2) * t + u + 1)
                sp.dma_start(scr_max[b], mt[:]).then_inc(mt_scr, 16)
                sp.wait_ge(mt_scr, 16 * (2 * t + b + 1))
                sp.dma_start(qp[b][KA:KM], scr_max[b].rearrange("(k h) t -> k h t", k=PARTS)).then_inc(mrow_in[b], 16)

            def prelude_():
                sp.wait_ge(ready, 5)
                scratch(0, True)
                for b in range(2):
                    pack(0, b, True)

            def body(t, kind, x0, x3):
                if x0 is not None:
                    scratch(t + 1, False)
                for b in range(2):
                    max_rows(t, b)
                if x0 is not None:
                    for b in range(2):
                        pack(t + 1, b, False)

            def store(kind, pair):
                for i in range(2):
                    kind.read(sp, f"xb{i}")
                sp.dma_start(out_dram[pair], xres[:, pair]).then_inc(outs, 16)

            def body_or_last(t, kind, x0, x3):
                if x0 is None:
                    for pair in range(PAIRS - 2):
                        store(Kind(middle_, STEPS - 3), pair)
                body(t, kind, x0, x3)

            def back(t, kind, x3):
                store(LST, PAIRS - 2)
                store(kind, PAIRS - 1)
                sp.wait_ge(outs, 16 * PAIRS)

            schedule(sp, prelude_, body_or_last, back, switch0, switch3)


def build(nc, ins, out_dram):
    with ExitStack() as ctx:
        def sb(name, shape, dt=F32):
            return ctx.enter_context(nc.sbuf_tensor(name, shape, dt))

        xres = sb("xres", [P, PAIRS, TILES, D])
        mod_p0 = sb("mod_p0", [P, LAYERS * PAIRS, 2, C, 2])
        mod_p3 = sb("mod_p3", [P, LAYERS * PAIRS, 2, C, 6])
        ident = sb("ident", [P, P])
        identb = sb("identb", [P, P], BF16)
        scr_qk = nc.dram_tensor("scr_qk", (2, PARTS, D, T), BF16, kind="Internal").ap()
        scr_max = nc.dram_tensor("scr_max", (2, PARTS * H, N), BF16, kind="Internal").ap()
        scr_mask = nc.dram_tensor("scr_mask", (LAYERS * B, N), BF16, kind="Internal").ap()
        graph_layer(nc, ins, xres, mod_p0, mod_p3, ident, identb, scr_mask)
        transformer_layers(nc, ins, xres, mod_p0, mod_p3, ident, identb, out_dram, scr_qk, scr_max, scr_mask)


def kernel(**a):
    import concourse.bacc as bacc
    from concourse.bass_utils import run_bass_kernel_spmd

    def arr(name):
        return np.asarray(a[name])

    def rows(w):
        return np.asarray(w).reshape(-1, P, w.shape[-1]).transpose(1, 0, 2)

    def cols(v, k=C):
        return np.asarray(v).reshape(k, P).T

    f32 = np.float32
    x = arr("x").reshape(PAIRS, TILES, P, D).transpose(0, 2, 1, 3)
    mask = arr("mask_BxSxSx11_ik0")
    adj = np.stack([mask[:, :, :NK, :], mask[:, :NK, :, :].transpose(0, 2, 1, 3)], axis=2)
    adj = adj.reshape(PAIRS, TILES, P, 2 * NK, L).transpose(0, 2, 1, 3, 4).reshape(PAIRS, P, TILES * 2 * NK, L)
    w_self = arr("L0_cond_W_self")
    wq, wk, wout = arr("L0_cond_Wq"), arr("L0_cond_Wk"), arr("L0_cond_Wout").reshape(2, D, D)
    gw = np.stack([rows(w.T) for w in (w_self[:, :D], wq[0], wq[1], wk[0], wk[1], wout[0], wout[1])])
    bq, bk, bo = arr("L0_cond_bq"), arr("L0_cond_bk"), arr("L0_cond_bout")
    gbias = np.stack([cols(v) for v in (arr("L0_cond_b_self"), bq[0], bq[1], bk[0], bk[1], bo[0], bo[1])], axis=1)
    lab = np.broadcast_to(np.concatenate([arr("L0_cond_w_bias"), arr("L0_cond_b_bias").reshape(1)]), (P, L + 1))

    def m1(k):
        return arr(f"L1_cond_{k}")

    def m2(k):
        return arr(f"L2_cond_{k}")

    def m3(k):
        return arr(f"L3_cond_{k}")

    vec1 = ("b1", "g1", "a1", "b2", "g2", "a2")
    ada = [rows(np.concatenate([m1(v + "_w") for v in vec1], axis=1)), rows(m2("w_ada"))]
    w31, w32 = m3("w_adaln1"), m3("w_adaln2")
    ada.append(rows(np.concatenate([w31[D:], w31[:D], w32[D:], w32[:D]], axis=0).T))
    b31, b32 = m3("b_adaln1"), m3("b_adaln2")
    zero = np.zeros(D, f32)
    ada_b = np.stack([np.stack([cols(m1(v + "_b")) for v in vec1], axis=1),
                      np.stack([cols(v) for v in m2("b_ada").reshape(6, D)], axis=1),
                      np.stack([cols(v) for v in (b31[D:], b31[:D], zero, b32[D:], b32[:D], zero)], axis=1)], axis=1)
    ln_gb = np.stack([cols(m1(v)) for v in ("ln1_g", "ln1_b", "ln2_g", "ln2_b")], axis=1)
    out_b = np.stack([np.stack([cols(p), cols(f)], axis=1) for p, f in (
        (m1("proj_b"), m1("fc2_b")), (m2("b_proj"), m2("b_fc2")), (m3("bo"), m3("b2")))], axis=1)

    blocks = [(m1("qkv_w"), m1("proj_w"), m1("fc1_w"), m1("fc2_w")), (m2("w_qkv"), m2("w_proj"), m2("w_fc1"), m2("w_fc2")),
              (np.concatenate([m3("wq").T, m3("wk").T, m3("wv").T], axis=1), m3("wo").T, m3("w1").T, m3("w2").T)]
    tw = np.stack([np.concatenate([rows(w).reshape(P, -1) for w in ws], axis=1).reshape(P, -1, W_CHUNK) for ws in blocks])
    qkv_b = [m1("qkv_b"), np.zeros(3 * D, f32), np.concatenate([m3("bq"), m3("bk"), m3("bv")])]
    fc1_b = [m1("fc1_b"), m2("b_fc1"), m3("b1")]
    tbias = np.stack([np.concatenate([cols(b, 3 * C), cols(f, J)], axis=1) for b, f in zip(qkv_b, fc1_b)])

    sel8 = np.kron(np.eye(HC, dtype=f32), np.ones((DH, 1), f32))
    sel80 = np.kron(np.eye(GH, dtype=f32), np.ones((NK, 1), f32))
    inputs = {"x": x, "mask": arr("mask_BxS_bf0"), "adj": adj, "cond": cols_of(arr("cond_1024")), "wq_self": rows(w_self[:, D:].T), "gw": gw, "gbias": gbias,
              "lab": lab, "sel8": sel8, "sel80": sel80, "ident": np.eye(P, dtype=f32), "ada0": ada[0], "ada1": ada[1],
              "ada2": ada[2], "ada_b": ada_b, "ln_gb": ln_gb, "out_b": out_b, "tw": tw, "tbias": tbias}
    inputs = {k: np.ascontiguousarray(v) for k, v in inputs.items()}

    nc = bacc.Bacc("TRN2", target_bir_lowering=False, num_devices=1)
    ins = {k: nc.dram_tensor(f"in_{k}", v.shape, mybir.dt.from_np(v.dtype), kind="ExternalInput").ap()
           for k, v in inputs.items()}
    out = nc.dram_tensor("out_x", (PAIRS, P, TILES, D), F32, kind="ExternalOutput").ap()
    build(nc, ins, out)
    r = run_bass_kernel_spmd(nc, [{f"in_{k}": v for k, v in inputs.items()}], core_ids=[0])
    y = r.results[0]["out_x"]
    return y.transpose(0, 2, 1, 3).reshape(B, N, D)


def cols_of(cond):
    return cond.T.reshape(C, P, B).transpose(1, 0, 2)
```

```python
from contextlib import ExitStack

import numpy as np
import concourse.bass as bass
from concourse import mybir

F32 = mybir.dt.float32
F32R = mybir.dt.float32r
BF16 = mybir.dt.bfloat16
I32 = mybir.dt.int32
ALU = mybir.AluOpType
ACT = mybir.ActivationFunctionType
AX_X = mybir.AxisListType.X

P = 128
B, N, D = 16, 256, 256
C = D // P
H, DH = 16, 16
HC = P // DH
PAIRS = B // 2
T = 2 * N
TILES = T // P
BT = N // P
LAYERS = 3
DFF = 1024
J = DFF // P
NK, L = 20, 11
NEG = -9000000000000000.0
EPS = 1e-5
QSCALE = DH ** -0.5
PARTS = 3
Q_PART = (0, 0, 1, 1, 0, 2)
K_PART = (0, 1, 0, 1, 2, 0)
KR = 16 * len(Q_PART)
KA = KR + 1
KM = KA + PARTS
BIG = 1e30
GH = 4
G = H // GH
RING = 8
GR = GH * NK
SC = 4
UNITS = 2 * H
W_CHUNK = 512


class Banks:

    def __init__(self, order, before):
        self.where, self.uses = {}, {}
        for name, bank in order:
            k = self.uses.get(bank, 0)
            self.where[name] = (bank, k)
            self.uses[bank] = k + 1
        self.before = before

    def use(self, name, step):
        bank, k = self.where[name]
        return bank, step * self.uses[bank] + self.before.get(bank, 0) + k

    def after(self, steps):
        banks = set(self.uses) | set(self.before)
        return {b: self.before.get(b, 0) + steps * self.uses.get(b, 0) for b in banks}


class Chain:

    def __init__(self, eng, sem, step, per_step, at=0):
        self.eng, self.sem, self.base, self.per_step, self.k = eng, sem, step * per_step, per_step, at

    def link(self, ins):
        self.k += 1
        assert self.k <= self.per_step
        ins.then_inc(self.sem, 1)
        self.eng.wait_ge(self.sem, self.base + self.k)


def mm3(pe, out, a_hi, a_lo, b_hi, b_lo, first, last):
    pe.matmul(out, a_hi, b_hi, start=first, stop=False)
    pe.matmul(out, a_hi, b_lo, start=False, stop=False)
    return pe.matmul(out, a_lo, b_hi, start=False, stop=last)


def settle(eng, passed, n):
    if not isinstance(n, int):
        eng.sem_inc(passed)


def graph_layer(nc, ins, xres, mod_p0, mod_p3, ident, identb, scr_mask):
    with ExitStack() as ctx:
        def sb(name, shape, dt=F32):
            return ctx.enter_context(nc.sbuf_tensor("g_" + name, shape, dt))

        def sem(name):
            return ctx.enter_context(nc.semaphore("g_" + name))

        bank = [ctx.enter_context(nc.psum_tensor(f"g_bank{i}", [P, 512], F32)) for i in range(8)]

        NW = 7
        NU = TILES * 2
        w_hi = sb("w_hi", [P, NW, C, D], F32R)
        w_lo = sb("w_lo", [P, NW, C, D], F32R)
        w_raw = sb("w_raw", [P, 2, C, D])
        wq_self = sb("wq_self", [P, C, D])
        ada_w = sb("ada_w", [P, C, 6 * D])
        cond = sb("cond", [P, C, B])
        cond_silu = sb("cond_silu", [P, C, B])
        ada_b = sb("ada_b", [P, LAYERS, 6, C])
        ln_gb = sb("ln_gb", [P, 4, C])
        out_b = sb("out_b", [P, LAYERS, 2, C])
        modv = sb("modv", [P, 6, C, B])
        mask = sb("mask", [LAYERS * B, N], mybir.dt.uint8)
        mask_rows = sb("mask_rows", [LAYERS * B, N], BF16)
        modt = sb("modt", [P, C, B])
        gbias = sb("gbias", [P, 7, C])
        bout = sb("bout", [P, C])
        lab = sb("lab", [P, L + 1])
        sel8 = sb("sel8", [P, HC])
        sel80 = sb("sel80", [GR, GH])
        qw = sb("qw", [P, C, PAIRS, 2])
        adj = sb("adj", [P, TILES * 2 * NK, L], I32)
        prod = sb("prod", [P, TILES * 2 * NK, L])
        vb = sb("vb", [P, TILES * 2 * NK])
        keep = sb("keep", [P, TILES * 2, NK])
        shift = sb("shift", [P, TILES * 2, NK])
        neg = sb("neg", [P, TILES * 2 * NK])
        x_tok = sb("x_tok", [P, TILES, D])
        rsum = sb("rsum", [P, TILES])
        nz = sb("nz", [P, TILES], BF16)
        nzb = sb("nzb", [P, T])
        feat = sb("feat", [P, C, T])
        f_hi = sb("f_hi", [P, C, T], F32R)
        f_lo = sb("f_lo", [P, C, T], F32R)
        st = sb("st", [P, C, T])
        s_hi = sb("s_hi", [P, C, T], F32R)
        s_lo = sb("s_lo", [P, C, T], F32R)
        q_f = sb("q_f", [P, 2, T])
        q_hi = sb("q_hi", [P, 2 * C, T], F32R)
        q_lo = sb("q_lo", [P, 2 * C, T], F32R)
        k_f = sb("k_f", [P, 2 * C, 2, NK])
        kbd = sb("kbd", [P, 2, 2 * C, HC * NK])
        kbd_hi = sb("kbd_hi", [P, 2, 2 * C, HC * NK], F32R)
        kbd_lo = sb("kbd_lo", [P, 2, 2 * C, HC * NK], F32R)
        s_rep = sb("s_rep", [P, 2, C, 2, GR], F32R)
        vbd = sb("vbd", [GR, 2, 2, G, GH * DH])
        aff = sb("aff", [P, 2, H, NK])
        e = sb("e", [P, NU, H, NK])
        mx = sb("mx", [P, H])
        den = sb("den", [P, NU, H])
        wt = sb("wt", [GR, 2, G, T])

        raw_in = [sem(f"raw_in{i}") for i in range(2)]
        x_in = [sem(f"x_in{i}") for i in range(PAIRS)]
        consts, ada_in, adj_in = sem("consts"), sem("ada_in"), sem("adj_in")
        w_split, qw_ps, qw_done, mod_ps, mod_done = sem("w_split"), sem("qw_ps"), sem("qw_done"), sem("mod_ps"), sem("mod_done")
        mod_raw, mod_tanh, silu = sem("mod_raw"), sem("mod_tanh"), sem("silu")
        ready = sem("ready")
        mask_in, mask_done, mask_out = sem("mask_in"), sem("mask_done"), sem("mask_out")
        passed = sem("passed")
        adj_used, x_copied, nz_ready, xt_split, s_ready, s_split = (
            sem("adj_used"), sem("x_copied"), sem("nz_ready"), sem("xt_split"), sem("s_ready"), sem("s_split"))
        q_hi_done, q_lo_done, kbd_split, rep_ready = sem("q_hi_done"), sem("q_lo_done"), sem("kbd_split"), sem("rep_ready")
        shifted, exped, dens, weights, relu_out = (
            sem("shifted"), sem("exped"), sem("dens"), sem("weights"), sem("relu_out"))
        prep_chain, soft_chain, st_chain, set_chain = sem("prep_chain"), sem("soft_chain"), sem("st_chain"), sem("set_chain")

        order = ([("xt0", 0), ("xt1", 1), ("nz", 2), ("s0", 3), ("s1", 4), ("q0", 5), ("q1", 6), ("q2", 7), ("q3", 0)]
                 + [("k", 1), ("v0", 2), ("v1", 3)] + [(f"aff{u}", 4 + u % 4) for u in range(NU)]
                 + [(f"wt{i}", i % 2) for i in range(2 * G)] + [("out0", 2), ("out1", 3), ("back0", 6), ("back1", 7)])
        uses = Banks(order, {})
        full = [sem(f"full{i}") for i in range(8)]
        free = [sem(f"free{i}") for i in range(8)]

        def wait_full(eng, name, n):
            i, k = uses.use(name, n)
            eng.wait_ge(full[i], k + 1)
            return bank[i], free[i]

        def take(pe, name, n, first=False):
            i, k = uses.use(name, n)
            if not (first and uses.where[name][1] == 0):
                pe.wait_ge(free[i], k)
            return bank[i], full[i]

        def pair_loop(eng, step):
            step(0, True)
            with eng.Fori(1, PAIRS) as n:
                step(n, False)

        block = ctx.enter_context(nc.Block())

        @block.sync
        def _(sp):
            for dst, src in ((cond[:], "cond"), (wq_self[:], "wq_self"), (ident[:], "ident"), (gbias[:], "gbias"),
                             (lab[:], "lab"), (sel8[:], "sel8"), (sel80[:], "sel80"), (ada_b[:], "ada_b"),
                             (ln_gb[:], "ln_gb"), (out_b[:], "out_b")):
                sp.dma_start(dst, ins[src]).then_inc(consts, 16)
            sp.dma_start(xres[:, 0], ins["x"][0]).then_inc(x_in[0], 16)
            sp.dma_start(adj[:], ins["adj"][0]).then_inc(adj_in, 16)
            for i in range(NW):
                if i >= 2:
                    sp.wait_ge(w_split, 2 * (i - 1))
                sp.dma_start(w_raw[:, i % 2], ins["gw"][i]).then_inc(raw_in[i % 2], 16)
            sp.dma_start(mask[(LAYERS - 1) * B:], ins["mask"]).then_inc(mask_in, 16)
            sp.wait_ge(mask_done, 2)
            sp.dma_start(scr_mask, mask_rows[:]).then_inc(mask_out, 16)
            for i in range(1, PAIRS):
                sp.dma_start(xres[:, i], ins["x"][i]).then_inc(x_in[i], 16)
            for layer in range(LAYERS):
                if layer:
                    sp.wait_ge(mod_ps, layer)
                w = (6 if layer < 2 else 4) * D
                sp.dma_start(ada_w[:, :, 0:w], ins[f"ada{layer}"]).then_inc(ada_in, 16)
            with sp.Fori(1, PAIRS) as n:
                sp.wait_ge(adj_used, 2 * n)
                sp.dma_start(adj[:], ins["adj"][n]).then_inc(adj_in, 16)
            sp.wait_ge(mask_out, 16)

        @block.tensor
        def _(pe):
            pe.wait_ge(consts, 160)
            for oc in range(C):
                for c in range(C):
                    mm = pe.matmul(bank[3][:, oc * B:(oc + 1) * B], wq_self[:, c, oc * P:(oc + 1) * P], cond[:, c, :],
                                   start=(c == 0), stop=(c == C - 1))
            mm.then_inc(qw_ps, 1)
            pe.wait_ge(silu, 1)
            for layer in range(LAYERS):
                pe.wait_ge(ada_in, 16 * (layer + 1))
                rhs = cond_silu if layer == 1 else cond
                for v in range(6 if layer < 2 else 4):
                    for oc in range(C):
                        at, o = (v * C + oc) * B, slice(v * D + oc * P, v * D + (oc + 1) * P)
                        for c in range(C):
                            mm = pe.matmul(bank[layer][:, at:at + B], ada_w[:, c, o], rhs[:, c, :],
                                           start=(c == 0), stop=(c == C - 1))
                mm.then_inc(mod_ps, 1)
            pe.wait_ge(qw_done, 1)
            pe.wait_ge(mod_raw, LAYERS)
            pe.wait_ge(ready, 3)
            pe.wait_ge(w_split, 2 * NW)

            def linear(out, w, oc, hi, lo):
                o = slice(oc * P, (oc + 1) * P)
                for c in range(C):
                    mm = mm3(pe, out[:], w_hi[:, w, c, o], w_lo[:, w, c, o], hi[:, c], lo[:, c], c == 0, c == C - 1)
                return mm

            def step(n, first):
                pe.wait_ge(x_copied, n + 1)
                for c in range(C):
                    out, done = take(pe, f"xt{c}", n, first)
                    for i in range(TILES):
                        mm = pe.transpose(out[:, i * P:(i + 1) * P], x_tok[:, i, c * P:(c + 1) * P], ident[:])
                    mm.then_inc(done, 1)
                pe.wait_ge(nz_ready, n + 1)
                out, done = take(pe, "nz", n, first)
                for i in range(TILES):
                    mm = pe.matmul(out[:, i * P:(i + 1) * P], nz[:, i:i + 1].to_broadcast([P, P]), identb[:],
                                   start=True, stop=True)
                mm.then_inc(done, 1)
                pe.wait_ge(xt_split, 2 * C * (n + 1))
                for oc in range(C):
                    out, done = take(pe, f"s{oc}", n, first)
                    linear(out, 0, oc, f_hi, f_lo).then_inc(done, 1)
                pe.wait_ge(s_split, 2 * C * (n + 1))
                for i in range(2 * C):
                    out, done = take(pe, f"q{i}", n, first)
                    linear(out, 1 + i // C, i % C, s_hi, s_lo).then_inc(done, 1)
                out, done = take(pe, "k", n, first)
                for i in range(2 * C):
                    o, w = slice((i % C) * P, (i % C + 1) * P), 3 + i // C
                    for c in range(C):
                        hi = s_hi[:, c, :].rearrange("p (b t) -> p b t", b=2)[:, :, 0:NK]
                        lo = s_lo[:, c, :].rearrange("p (b t) -> p b t", b=2)[:, :, 0:NK]
                        mm = mm3(pe, out[:, i * 2 * NK:(i + 1) * 2 * NK], w_hi[:, w, c, o], w_lo[:, w, c, o], hi, lo,
                                 c == 0, c == C - 1)
                mm.then_inc(done, 1)
                pe.wait_ge(rep_ready, 2 * (n + 1))
                for d in range(2):
                    out, done = take(pe, f"v{d}", n, first)
                    for b in range(2):
                        for g in range(G):
                            at, o = (b * G + g) * GH * DH, slice(g * GH * DH, (g + 1) * GH * DH)
                            for c in range(C):
                                mm = mm3(pe, out[0:GR, at:at + GH * DH], s_rep[:, 0, c, b], s_rep[:, 1, c, b],
                                         w_hi[:, 5 + d, c, o], w_lo[:, 5 + d, c, o], c == 0, c == C - 1)
                    mm.then_inc(done, 1)
                pe.wait_ge(kbd_split, 2 * (n + 1))
                pe.wait_ge(q_lo_done, 2 * C * (n + 1))
                for u in range(NU):
                    i, d = u // 2, u % 2
                    out, done = take(pe, f"aff{u}", n, first)
                    for c in range(C):
                        t, at = slice(i * P, (i + 1) * P), c * HC * NK
                        mm = mm3(pe, out[:, at:at + HC * NK], q_hi[:, d * C + c, t], q_lo[:, d * C + c, t],
                                 kbd_hi[:, i // BT, d * C + c], kbd_lo[:, i // BT, d * C + c], True, True)
                    mm.then_inc(done, 1)
                pe.wait_ge(weights, NU * (n + 1))
                for d in range(2):
                    for g in range(G):
                        out, done = take(pe, f"wt{d * G + g}", n, first)
                        for i in range(TILES):
                            src = e[:, i * 2 + d, g * GH:(g + 1) * GH].rearrange("p h m -> p (h m)")
                            mm = pe.transpose(out[0:GR, i * P:(i + 1) * P], src, ident[:])
                        mm.then_inc(done, 1)
                for i in (0, 1):
                    pe.wait_ge(free[i], uses.use(f"wt{2 * G - 2 + i}", n)[1] + 1)
                for c in range(C):
                    out, done = take(pe, f"out{c}", n, first)
                    for b in range(2):
                        for d in range(2):
                            for gg in range(2):
                                g = 2 * c + gg
                                mm = pe.matmul(out[64 * gg:64 * gg + GH * DH, b * N:(b + 1) * N], vbd[:, d, b, g],
                                               wt[:, d, g, b * N:(b + 1) * N], start=(d == 0), stop=(d == 1))
                    mm.then_inc(done, 1)
                pe.wait_ge(relu_out, C * (n + 1))
                for i in range(2):
                    out, done = take(pe, f"back{i}", n, first)
                    for tt in range(2):
                        for c in range(C):
                            t = slice((2 * i + tt) * P, (2 * i + tt + 1) * P)
                            mm = pe.transpose(out[:, tt * D + c * P:tt * D + (c + 1) * P], feat[:, c, t], ident[:])
                    mm.then_inc(done, 1)

            pair_loop(pe, step)

        @block.vector
        def _(dve):
            v = nc.vector
            link = Chain(dve, set_chain, 0, 100).link
            v.memset(vbd[:], 0.0).then_inc(ready, 1)
            dve.wait_ge(consts, 160)
            v.tensor_copy(identb[:], ident[:]).then_inc(ready, 1)
            v.tensor_tensor(bout[:], gbias[:, 5], gbias[:, 6], ALU.add).then_inc(ready, 1)
            dve.wait_ge(qw_ps, 1)
            v.tensor_copy(qw[:].rearrange("p c n b -> p (c n b)"), bank[3][:, 0:C * B]).then_inc(qw_done, 1)
            for i in range(NW):
                dve.wait_ge(raw_in[i % 2], 16 * (i // 2 + 1))
                v.tensor_copy(w_hi[:, i], w_raw[:, i % 2]).then_inc(w_split, 1)
                dve.wait_ge(w_split, 2 * i + 1)
                v.tensor_tensor(w_lo[:, i], w_raw[:, i % 2], w_hi[:, i].bitcast(F32), ALU.subtract).then_inc(w_split, 1)
            v.memset(mask_rows[:], 0.0).then_inc(mask_done, 1)
            dve.wait_ge(mask_in, 16)
            dve.wait_ge(mask_done, 1)
            v.tensor_scalar(mask_rows[(LAYERS - 1) * B:], mask[(LAYERS - 1) * B:], -BIG, BIG, ALU.mult,
                            ALU.mult).then_inc(mask_done, 1)
            for layer in range(LAYERS):
                nv = 6 if layer < 2 else 4
                order_v = (0, 1, 2, 3, 4, 5) if layer < 2 else (0, 1, 3, 4)
                dve.wait_ge(mod_ps, layer + 1)
                if layer:
                    dve.wait_ge(mod_done, layer)
                for k, vec in enumerate(order_v):
                    ins_ = v.tensor_tensor(modv[:, vec], bank[layer][:, k * C * B:(k + 1) * C * B].rearrange(
                        "p (c b) -> p c b", c=C), ada_b[:, layer, vec].unsqueeze(2).to_broadcast([P, C, B]), ALU.add)
                ins_.then_inc(mod_raw, 1)
                dve.wait_ge(mod_raw, layer + 1)
                if layer == 0:
                    dve.wait_ge(mod_tanh, 2)
                    link(v.tensor_scalar(modv[:, 2], modv[:, 2], 0.1, None, ALU.mult))
                    link(v.tensor_scalar(modv[:, 5], modv[:, 5], 0.1, None, ALU.mult))
                if layer == 2:
                    link(v.memset(modv[:, 2], 1.0))
                    link(v.memset(modv[:, 5], 1.0))
                def vector_of(mod, k):
                    return mod[:, layer * PAIRS:(layer + 1) * PAIRS, :, :, k].rearrange("p n b c -> p c (n b)")

                for ln in range(2):
                    a_out, b_out = (vector_of(mod_p3, 2 + k) if ln else vector_of(mod_p0, k) for k in range(2))
                    gate, gb = vector_of(mod_p3, 4 * ln), vector_of(mod_p3, 4 * ln + 1)
                    shift_v, scale_v, gate_v = modv[:, 3 * ln], modv[:, 3 * ln + 1], modv[:, 3 * ln + 2]
                    if layer == 0:
                        g_ = ln_gb[:, 2 * ln].unsqueeze(2).to_broadcast([P, C, B])
                        b_ = ln_gb[:, 2 * ln + 1].unsqueeze(2).to_broadcast([P, C, B])
                        link(v.tensor_scalar(scale_v, scale_v, 1.0, None, ALU.add))
                        link(v.tensor_tensor(a_out, scale_v, g_, ALU.mult))
                        link(v.tensor_tensor(modt[:], scale_v, b_, ALU.mult))
                        link(v.tensor_tensor(b_out, modt[:], shift_v, ALU.add))
                    else:
                        link(v.tensor_scalar(a_out, scale_v, 1.0, None, ALU.add))
                        link(v.tensor_copy(b_out, shift_v))
                    link(v.tensor_copy(gate, gate_v))
                    ob = out_b[:, layer, ln].unsqueeze(2).to_broadcast([P, C, B])
                    last = v.tensor_tensor(gb, gate_v, ob, ALU.mult)
                    link(last) if ln == 0 else last.then_inc(mod_done, 1)
            dve.wait_ge(mod_done, LAYERS)

            def step(n, first):
                prep = Chain(dve, prep_chain, n, 5).link
                dve.wait_ge(adj_in, 16 * (n + 1))
                prep(v.tensor_reduce(vb[:], adj[:], AX_X, ALU.add))
                v.tensor_scalar(keep[:].rearrange("p u m -> p (u m)"), vb[:], 0.0, None, ALU.is_gt).then_inc(adj_used, 1)
                prep(v.tensor_tensor(prod[:], adj[:], lab[:, 0:L].unsqueeze(1).to_broadcast([P, TILES * 2 * NK, L]), ALU.mult))
                prep(v.tensor_reduce(vb[:], prod[:], AX_X, ALU.add))
                dve.wait_ge(adj_used, 2 * n + 1)
                prep(v.tensor_scalar(neg[:], keep[:].rearrange("p u m -> p (u m)"), -NEG, NEG, ALU.mult, ALU.add))
                v.scalar_tensor_tensor(shift[:].rearrange("p u m -> p (u m)"), vb[:], lab[:, L:L + 1], neg[:],
                                       ALU.add, ALU.add).then_inc(adj_used, 1)
                dve.wait_ge(x_copied, n + 1)
                prep(v.tensor_reduce(rsum[:], x_tok[:], AX_X, ALU.add))
                v.tensor_scalar(nz[:], rsum[:], 0.0, None, ALU.not_equal).then_inc(nz_ready, 1)
                src, done = wait_full(dve, "nz", n)
                v.tensor_copy(nzb[:], src[:]).then_inc(done, 1)
                dve.wait_ge(done, uses.use("nz", n)[1] + 1)
                for oc in range(C):
                    src, done = wait_full(dve, f"s{oc}", n)
                    for b in range(2):
                        t = slice(b * N, (b + 1) * N)
                        last = v.scalar_tensor_tensor(st[:, oc, t], nzb[:, t], qw[:, oc, n, b:b + 1], src[:, t],
                                                      ALU.mult, ALU.add)
                    last.then_inc(done, 1)
                for i in range(2 * C):
                    src, done = wait_full(dve, f"q{i}", n)
                    if i >= 2 or not first:
                        dve.wait_ge(q_lo_done, 2 * C * n + i - 1)
                    v.tensor_scalar(q_f[:, i % 2], src[:], gbias[:, 1 + i // C, i % C:i % C + 1], QSCALE,
                                    ALU.add, ALU.mult).then_inc(done, 1)
                    dve.wait_ge(done, uses.use(f"q{i}", n)[1] + 1)
                    v.tensor_copy(q_hi[:, i], q_f[:, i % 2]).then_inc(q_hi_done, 1)
                kc = Chain(dve, st_chain, n, 1).link
                src, done = wait_full(dve, "k", n)
                last = v.tensor_tensor(k_f[:].rearrange("p i b m -> p i (b m)"),
                                       src[:, 0:2 * C * 2 * NK].rearrange("p (i m) -> p i m", i=2 * C),
                                       gbias[:, 3:5].rearrange("p d c -> p (d c)").unsqueeze(2).to_broadcast(
                                           [P, 2 * C, 2 * NK]), ALU.add)
                last.then_inc(done, 1)
                dve.wait_ge(done, uses.use("k", n)[1] + 1)
                for b in range(2):
                    for i in range(2 * C):
                        last = v.tensor_tensor(kbd[:, b, i].rearrange("p (h m) -> p h m", h=HC),
                                               k_f[:, i, b].unsqueeze(1).to_broadcast([P, HC, NK]),
                                               sel8[:].unsqueeze(2).to_broadcast([P, HC, NK]), ALU.mult)
                kc(last)
                v.tensor_copy(kbd_hi[:], kbd[:]).then_inc(kbd_split, 1)
                dve.wait_ge(kbd_split, 2 * n + 1)
                v.tensor_tensor(kbd_lo[:], kbd[:], kbd_hi[:].bitcast(F32), ALU.subtract).then_inc(kbd_split, 1)
                for d in range(2):
                    src, done = wait_full(dve, f"v{d}", n)
                    last = v.tensor_tensor(vbd[:, d].rearrange("p b g (h r) -> p (b g) h r", h=GH),
                                           src[0:GR].rearrange("p (q h r) -> p q h r", h=GH, r=DH),
                                           sel80[:].unsqueeze(1).unsqueeze(3).to_broadcast([GR, 2 * G, GH, DH]), ALU.mult)
                    last.then_inc(done, 1)
                soft = Chain(dve, soft_chain, n, 3 * NU).link
                def tail(u):
                    dve.wait_ge(exped, NU * n + u + 1)
                    soft(v.tensor_reduce(den[:, u], e[:, u], AX_X, ALU.add))
                    v.reciprocal(den[:, u], den[:, u]).then_inc(dens, 1)

                for u in range(NU):
                    src, done = wait_full(dve, f"aff{u}", n)
                    if u >= 2:
                        dve.wait_ge(exped, NU * n + u - 1)
                    elif not first:
                        dve.wait_ge(exped, NU * n)
                    a = aff[:, u % 2]
                    v.tensor_tensor(a, src[:, 0:H * NK].rearrange("p (h m) -> p h m", h=H),
                                    keep[:, u].unsqueeze(1).to_broadcast([P, H, NK]), ALU.mult).then_inc(done, 1)
                    dve.wait_ge(done, uses.use(f"aff{u}", n)[1] + 1)
                    soft(v.tensor_tensor(a, a, shift[:, u].unsqueeze(1).to_broadcast([P, H, NK]), ALU.add))
                    soft(v.tensor_reduce(mx[:], a, AX_X, ALU.max))
                    v.tensor_tensor(a, a, mx[:].unsqueeze(2).to_broadcast([P, H, NK]), ALU.subtract).then_inc(shifted, 1)
                    if u >= 1:
                        tail(u - 1)
                tail(NU - 1)
                for c in range(C):
                    src, done = wait_full(dve, f"out{c}", n)
                    v.tensor_tensor(feat[:, c], src[:], st[:, c], ALU.add).then_inc(done, 1)
                for i in range(2):
                    src, done = wait_full(dve, f"back{i}", n)
                    xs = xres[:, n, 2 * i:2 * i + 2, :]
                    v.tensor_tensor(xs, src[:].rearrange("p (t f) -> p t f", t=2), xs, ALU.add).then_inc(done, 1)

            pair_loop(dve, step)

        @block.scalar
        def _(act):
            a = nc.scalar
            act.wait_ge(consts, 160)
            a.activation(cond_silu[:], cond[:], ACT.Silu).then_inc(silu, 1)
            act.wait_ge(mod_raw, 1)
            a.activation(modv[:, 2], modv[:, 2], ACT.Tanh).then_inc(mod_tanh, 1)
            a.activation(modv[:, 5], modv[:, 5], ACT.Tanh).then_inc(mod_tanh, 1)

            def step(n, first):
                if first:
                    act.wait_ge(x_in[0], 16)
                else:
                    for i in (0, 1):
                        act.wait_ge(full[i], uses.use(f"xt{i}", n - 1)[1] + 1)
                    act.wait_ge(nz_ready, n)
                a.copy(x_tok[:], xres[:, n]).then_inc(x_copied, 1)
                for c in range(C):
                    src, done = wait_full(act, f"xt{c}", n)
                    if c == 0 and not first:
                        for i in (6, 7):
                            act.wait_ge(full[i], uses.use(f"back{i - 6}", n - 1)[1] + 1)
                    a.copy(feat[:, c], src[:]).then_inc(done, 1)
                for oc in range(C):
                    act.wait_ge(free[3 + oc], uses.use(f"s{oc}", n)[1] + 1)
                    a.activation(st[:, oc], st[:, oc], ACT.Identity, bias=gbias[:, 0, oc:oc + 1]).then_inc(s_ready, 1)
                for u in range(NU):
                    act.wait_ge(shifted, NU * n + u + 1)
                    a.activation(e[:, u], aff[:, u % 2], ACT.Exp).then_inc(exped, 1)
                for i in range(2 * G):
                    src, done = wait_full(act, f"wt{i}", n)
                    a.copy(wt[:, i // G, i % G], src[0:GR]).then_inc(done, 1)
                for c in range(C):
                    act.wait_ge(free[2 + c], uses.use(f"out{c}", n)[1] + 1)
                    a.activation(feat[:, c], feat[:, c], ACT.Relu, bias=bout[:, c:c + 1]).then_inc(relu_out, 1)

            act.wait_ge(ready, 3)
            step(0, True)
            for i in range(1, PAIRS):
                act.wait_ge(x_in[i], 16)
            with act.Fori(1, PAIRS) as n:
                step(n, False)

        @block.gpsimd
        def _(pool):
            g = nc.gpsimd

            def split(hi, lo, src, sem_, base):
                settle(pool, passed, base)
                g.tensor_scalar(hi, src, 1.0, None, ALU.mult).then_inc(sem_, 1)
                pool.wait_ge(sem_, base + 1)
                g.tensor_tensor(lo, src, hi.bitcast(F32), ALU.subtract).then_inc(sem_, 1)

            def step(n, first):
                for c in range(C):
                    pool.wait_ge(free[c], uses.use(f"xt{c}", n)[1] + 1)
                    if c == 0 and not first:
                        pool.wait_ge(full[4], uses.use("s1", n - 1)[1] + 1)
                    split(f_hi[:, c], f_lo[:, c], feat[:, c], xt_split, 2 * C * n + 2 * c)
                if not first:
                    pool.wait_ge(full[1], uses.use("k", n - 1)[1] + 1)
                for c in range(C):
                    pool.wait_ge(s_ready, C * n + c + 1)
                    split(s_hi[:, c], s_lo[:, c], st[:, c], s_split, 2 * C * n + 2 * c)
                if not first:
                    pool.wait_ge(full[3], uses.use("v1", n - 1)[1] + 1)
                for k, part in enumerate((s_hi, s_lo)):
                    pool.wait_ge(s_split, 2 * C * (n + 1))
                    settle(pool, passed, n)
                    for c in range(C):
                        for b in range(2):
                            last = g.tensor_copy(s_rep[:, k, c, b].rearrange("p (h m) -> p h m", h=GH),
                                                 part[:, c, b * N:b * N + NK].unsqueeze(1).to_broadcast([P, GH, NK]))
                    last.then_inc(rep_ready, 1)
                for i in range(2 * C):
                    pool.wait_ge(q_hi_done, 2 * C * n + i + 1)
                    g.tensor_tensor(q_lo[:, i], q_f[:, i % 2], q_hi[:, i].bitcast(F32), ALU.subtract).then_inc(q_lo_done, 1)
                for u in range(NU):
                    pool.wait_ge(dens, NU * n + u + 1)
                    g.tensor_tensor(e[:, u], e[:, u], den[:, u].unsqueeze(2).to_broadcast([P, H, NK]),
                                    ALU.mult).then_inc(weights, 1)

            pair_loop(pool, step)



USES = ([("proj0", 0, "B"), ("proj1", 1, "B"), ("ln1_0", 2, "F"), ("ln1_1", 0, "F"), ("mr1", 1, "M"), ("xa0", 2, "B"),
         ("xa1", 0, "B"), ("qk0", 1, "F"), ("qk1", 2, "F"), ("qk2", 0, "F"), ("qk3", 1, "F"), ("v0", 2, "F"),
         ("ln2_0", 0, "B"), ("ln2_1", 1, "B"), ("otm0", 2, "O"), ("otm1", 0, "O"), ("v1", 1, "F"), ("otm2", 2, "O"),
         ("otm3", 0, "O"), ("ofm0", 1, "O"), ("fc1_0", 2, "B"), ("ofm1", 0, "O")]
        + [(f"fc1_{j}", 2, "B") for j in range(1, J)] + [("fc2_0", 0, "B"), ("fc2_1", 1, "B")]
        + [("mr0", 2, "N"), ("xb0", 2, "B"), ("xb1", 0, "B")])


def uses_of(parts):
    return [(name, bank) for name, bank, part in USES if part in parts]


def transformer_layers(nc, ins, xres, mod_p0, mod_p3, ident, identb, out_dram, scr_qk, scr_max, scr_mask):
    STEPS = LAYERS * PAIRS
    with ExitStack() as ctx:
        def sb(name, shape, dt=F32):
            return ctx.enter_context(nc.sbuf_tensor("t_" + name, shape, dt))

        def sem(name):
            return ctx.enter_context(nc.semaphore("t_" + name))

        def ps(name):
            return ctx.enter_context(nc.psum_tensor("t_" + name, [P, 512], F32))

        lin = [ps(f"lin{i}") for i in range(3)]
        scb = [ps(f"scb{i}") for i in range(SC)]
        avb = ps("avb")

        w0_hi = sb("w0_hi", [P, C, 3 * D], F32R)
        w0_lo = sb("w0_lo", [P, C, 3 * D], F32R)
        wp_hi = sb("wp_hi", [P, C, D], F32R)
        wp_lo = sb("wp_lo", [P, C, D], F32R)
        w1_hi = sb("w1_hi", [P, C, DFF], F32R)
        w1_lo = sb("w1_lo", [P, C, DFF], F32R)
        w2_hi = sb("w2_hi", [P, J, D], F32R)
        w2_lo = sb("w2_lo", [P, J, D], F32R)
        bias0 = sb("bias0", [P, 2 * C])
        bias3 = sb("bias3", [P, J])
        bias_v = sb("bias_v", [P, STEPS, C])
        m0 = sb("m0", [P, 2, C, 2])
        m3 = sb("m3", [P, 2, C, 6])
        stats = sb("stats", [P, 2, TILES, 6])
        mv = sb("mv", [P, 2, TILES, 2])
        var = sb("var", [P, 2, TILES])
        rstd = sb("rstd", [P, 2, TILES])
        mhalf = sb("mhalf", [P, TILES])
        xh0 = sb("xh0", [P, TILES, D])
        xh3 = sb("xh3", [P, TILES, D])
        h0 = sb("h0", [P, C, T])
        h0_hi = sb("h0_hi", [P, C, T], F32R)
        h0_lo = sb("h0_lo", [P, C, T], F32R)
        h3 = sb("h3", [P, C, T])
        h3_hi = sb("h3_hi", [P, C, T], F32R)
        h3_lo = sb("h3_lo", [P, C, T], F32R)
        qf = sb("qf", [P, T])
        qr = sb("qr", [P, 2, T])
        parts = sb("parts", [P, 2, PARTS, T], BF16)
        qp = [sb(f"qp{b}", [KM, H, N], BF16) for b in range(2)]
        kp = [sb(f"kp{b}", [KM, H, N], BF16) for b in range(2)]
        vaug = sb("vaug", [P, TILES, H, 2 * DH])
        mx = sb("mx", [P, BT, H])
        mr = sb("mr", [P, BT, H])
        mm_parts = sb("mm_parts", [P, BT, PARTS, H], BF16)
        mt = sb("mt", [PARTS * H, N], BF16)
        prob = sb("prob", [P, RING, BT * N])
        oe = sb("oe", [P, 2, G, N])
        rden = sb("rden", [P, TILES, H])
        gl = sb("gl", [P, 2, T])
        g_hi = sb("g_hi", [P, 2, T], F32R)
        g_lo = sb("g_lo", [P, 2, T], F32R)

        full = [sem(f"lin_full{i}") for i in range(3)]
        free = [sem(f"lin_free{i}") for i in range(3)]
        mx_full, mx_free, sc_full, exped, av_full, av_free = (
            sem("mx_full"), sem("mx_free"), sem("sc_full"), sem("exped"), sem("av_full"), sem("av_free"))
        w0_in = [sem(f"w0_in{i}") for i in range(C * 3 * D // W_CHUNK)]
        w3_in = [sem(f"w3_in{i}") for i in range((C * D + C * DFF + J * D) // W_CHUNK)]
        w_split, bias0_in, bias3_in, ready = sem("w_split"), sem("bias0_in"), sem("bias3_in"), sem("ready")
        m0_ready, m3_ready = sem("m0_ready"), sem("m3_ready")
        st0, st3, rstd0, rstd3, xh0_ready, xh3_ready = (
            sem("st0"), sem("st3"), sem("rstd0"), sem("rstd3"), sem("xh0_ready"), sem("xh3_ready"))
        h0_split, o_split, h3_split, gelu_split = sem("h0_split"), sem("o_split"), sem("h3_split"), sem("gelu_split")
        h0_rounded, o_rounded, h3_rounded = sem("h0_rounded"), sem("o_rounded"), sem("h3_rounded")
        qk_chain, part3, scr_in = sem("qk_chain"), sem("part3"), [sem("scr_in0"), sem("scr_in1")]
        pack_in = [sem("pack_in0"), sem("pack_in1")]
        max_chain, mt_scr, mrow_in = sem("max_chain"), sem("mt_scr"), [sem("mrow_in0"), sem("mrow_in1")]
        rden_chain, fc2_read = sem("rden_chain"), sem("fc2_read")
        bias_v_in = sem("bias_v_in")
        outs, half_ready = sem("outs"), sem("half_ready")
        passed = sem("passed")

        nothing = {i: 0 for i in range(3)}
        prelude = Banks(uses_of("FN"), nothing)
        first_ = Banks(uses_of("FMON"), prelude.after(1))
        middle_ = Banks(uses_of("FBMON"), first_.after(1))
        last_ = Banks(uses_of("BMO"), middle_.after(STEPS - 2))
        tail_ = Banks(uses_of("B"), last_.after(1))

        class Kind:

            def __init__(self, banks, at):
                self.banks, self.at = banks, at

            def full(self, eng, name):
                i, k = self.banks.use(name, self.at)
                eng.wait_ge(full[i], k + 1)
                return lin[i], free[i]

            def read(self, eng, name):
                i, k = self.banks.use(name, self.at)
                eng.wait_ge(free[i], k + 1)

            def take(self, pe, name):
                i, k = self.banks.use(name, self.at)
                if not isinstance(k, int) or k > 0:
                    pe.wait_ge(free[i], k)
                return lin[i], full[i]

        PACKS = len(Q_PART) + len(K_PART) + 1
        PRE = Kind(prelude, 0)
        FST = Kind(first_, 0)
        LST = Kind(last_, 0)
        TAIL = Kind(tail_, 0)

        W0_CHUNKS, W3_CHUNKS = len(w0_in), len(w3_in)
        CHUNKS = W0_CHUNKS + W3_CHUNKS

        LATE = 2
        MAXES = [4] * (J - 1) + [2]
        MR_AFTER = sum(MAXES[:J - 1])

        def schedule(eng, prelude_, body, back, switch0, switch3):
            prelude_()
            body(0, FST, True, False)
            with eng.Fori(1, PAIRS - 1) as t:
                body(t, Kind(middle_, t - 1), True, True)
            with eng.Fori(1, LAYERS) as l:
                switch0(l)
                with eng.Fori(0, 2) as i:
                    t = l * PAIRS + i - 1
                    body(t, Kind(middle_, t - 1), True, True)
                switch3(l)
                with eng.Fori(0, PAIRS - 2) as i:
                    t = l * PAIRS + i + 1
                    body(t, Kind(middle_, t - 1), True, True)
            body(STEPS - 1, LST, False, True)
            back(STEPS - 1, TAIL)

        block = ctx.enter_context(nc.Block())

        @block.tensor
        def _(pe):
            def mmx(out, w_hi, w_lo, oc, hi, lo):
                o = slice(oc * P, (oc + 1) * P)
                for c in range(C):
                    mm = mm3(pe, out, w_hi[:, c, o], w_lo[:, c, o], hi[:, c], lo[:, c], c == 0, c == C - 1)
                return mm

            def to_features(kind, name, src, c):
                out, done = kind.take(pe, name)
                for i in range(TILES):
                    mm = pe.transpose(out[:, i * P:(i + 1) * P], src[:, i, c * P:(c + 1) * P], ident[:])
                mm.then_inc(done, 1)

            def to_tokens(kind, name, i):
                out, done = kind.take(pe, name)
                for tt in range(2):
                    for c in range(C):
                        t = slice((2 * i + tt) * P, (2 * i + tt + 1) * P)
                        mm = pe.transpose(out[:, tt * D + c * P:tt * D + (c + 1) * P], h3[:, c, t], ident[:])
                mm.then_inc(done, 1)

            def ln1(kind, n, c):
                pe.wait_ge(xh0_ready, TILES * (n + 1))
                to_features(kind, f"ln1_{c}", xh0, c)

            def qk(kind, n, i):
                pe.wait_ge(h0_split, C * (n + 1))
                out, done = kind.take(pe, f"qk{i}")
                mmx(out[:], w0_hi, w0_lo, i, h0_hi, h0_lo).then_inc(done, 1)

            def values(kind, n, b):
                pe.wait_ge(h0_split, C * (n + 1))
                out, done = kind.take(pe, f"v{b}")
                for i in range(BT):
                    t = slice(b * N + i * P, b * N + (i + 1) * P)
                    for c in range(C):
                        mm = mm3(pe, out[:, i * D:(i + 1) * D], h0_hi[:, c, t], h0_lo[:, c, t],
                                 w0_hi[:, c, 2 * D:], w0_lo[:, c, 2 * D:], c == 0, c == C - 1)
                mm.then_inc(done, 1)

            def max_scores(n, b, h):
                v = b * H + h
                if h == 0:
                    pe.wait_ge(pack_in[b], 16 * PACKS * (n + 1))
                if v >= SC:
                    pe.wait_ge(mx_free, UNITS * n + v - SC + 1)
                elif not isinstance(n, int) or n > 0:
                    pe.wait_ge(exped, UNITS * n + v - SC + 1)
                for i in range(BT):
                    mm = pe.matmul(scb[v % SC][:, i * N:(i + 1) * N], qp[b][0:KA, h, i * P:(i + 1) * P], kp[b][0:KA, h, :],
                                   start=True, stop=True)
                mm.then_inc(mx_full, 1)

            def max_rows(kind, n, b):
                pe.wait_ge(max_chain, 8 * n + 4 * b + 4)
                out, done = kind.take(pe, f"mr{b}")
                settle(pe, passed, n)
                out = out[0:PARTS * H, 0:N // 2].bitcast(BF16)
                for i in range(BT):
                    mm = pe.transpose(out[:, i * P:(i + 1) * P], mm_parts[:, i].rearrange("p k h -> p (k h)"), identb[:])
                mm.then_inc(done, 1)

            def exp_scores(t, u):
                b, h = u // H, u % H
                if h == 0:
                    pe.wait_ge(mrow_in[b], 16 * (t + 1))
                if u >= SC:
                    pe.wait_ge(exped, UNITS * t + u - SC + 1)
                else:
                    pe.wait_ge(mx_free, UNITS * (t + 1) + u - SC + 1)
                for i in range(BT):
                    mm = pe.matmul(scb[u % SC][:, i * N:(i + 1) * N], kp[b][:, h, i * P:(i + 1) * P], qp[b][:, h, :],
                                   start=True, stop=True)
                mm.then_inc(sc_full, 1)

            def attend(t, gg):
                b, g = gg // G, gg % G
                pe.wait_ge(exped, UNITS * t + GH * (gg + 1))
                if gg or not isinstance(t, int) or t > 0:
                    pe.wait_ge(av_free, 2 * G * t + gg)
                for i in range(BT):
                    for hh in range(GH):
                        mm = pe.matmul(avb[32 * hh:32 * hh + 32, 0:N], vaug[:, b * BT + i, g * GH + hh, :],
                                       prob[:, (gg * GH + hh) % RING, i * N:(i + 1) * N], start=(i == 0), stop=(i == BT - 1),
                                       skip_group_check=True)
                mm.then_inc(av_full, 1)

            def o_tokens(kind, n, i):
                pe.wait_ge(av_free, 2 * G * n + G * (i // BT + 1))
                out, done = kind.take(pe, f"otm{i}")
                for g in range(G):
                    mm = pe.transpose(out[:, g * P:(g + 1) * P], oe[:, i // BT, g, (i % BT) * P:(i % BT + 1) * P], ident[:])
                mm.then_inc(done, 1)

            def o_features(kind, n, b):
                for i in range(BT):
                    kind.read(pe, f"otm{b * BT + i}")
                out, done = kind.take(pe, f"ofm{b}")
                for c in range(C):
                    for i in range(BT):
                        mm = pe.transpose(out[:, c * N + i * P:c * N + (i + 1) * P], xh3[:, b * BT + i, c * P:(c + 1) * P],
                                          ident[:])
                mm.then_inc(done, 1)

            def project(kind, n, oc):
                pe.wait_ge(o_split, C * (n + 1))
                out, done = kind.take(pe, f"proj{oc}")
                mmx(out[:], wp_hi, wp_lo, oc, h0_hi, h0_lo).then_inc(done, 1)

            def x_mid_back(kind, n, i):
                for oc in range(C):
                    kind.read(pe, f"proj{oc}")
                to_tokens(kind, f"xa{i}", i)

            def ln2(kind, n):
                pe.wait_ge(xh3_ready, TILES * (n + 1))
                for c in range(C):
                    to_features(kind, f"ln2_{c}", xh3, c)

            def fc1(kind, n, j):
                pe.wait_ge(h3_split, C * (n + 1))
                out, done = kind.take(pe, f"fc1_{j}")
                mmx(out[:], w1_hi, w1_lo, j, h3_hi, h3_lo).then_inc(done, 1)

            def fc2(kind, n, j):
                pe.wait_ge(gelu_split, J * n + j + 1)
                for oc in range(C):
                    i, k = kind.banks.use(f"fc2_{oc}", kind.at)
                    if j == 0:
                        kind.take(pe, f"fc2_{oc}")
                    o = slice(oc * P, (oc + 1) * P)
                    mm = mm3(pe, lin[i][:], w2_hi[:, j, o], w2_lo[:, j, o], g_hi[:, j % 2], g_lo[:, j % 2], j == 0, j == J - 1)
                    if j == J - 1:
                        mm.then_inc(full[i], 1)
                if j < J - 1:
                    mm.then_inc(fc2_read, 1)

            def x_out_back(kind, n, i):
                for oc in range(C):
                    kind.read(pe, f"fc2_{oc}")
                to_tokens(kind, f"xb{i}", i)

            def switch0(l):
                pe.wait_ge(w_split, 2 * (CHUNKS * l + W0_CHUNKS))
                settle(pe, passed, l)

            def switch3(l):
                pe.wait_ge(w_split, 2 * CHUNKS * (l + 1))
                settle(pe, passed, l)

            def maxes(n):
                left = iter([(b, h) for b in range(2) for h in range(H)])

                def some(k):
                    for _ in range(k):
                        max_scores(n, *next(left))
                return some

            def prelude_():
                switch0(0)
                pe.wait_ge(ready, 5)
                for c in range(C):
                    ln1(PRE, 0, c)
                for i in range(2 * C):
                    qk(PRE, 0, i)
                for b in range(2):
                    values(PRE, 0, b)
                some = maxes(0)
                some(MR_AFTER)
                max_rows(PRE, 0, 0)
                some(UNITS - MR_AFTER)
                switch3(0)

            def mlp(kind, n, extra):
                for j in range(J):
                    if j + 1 < J:
                        fc1(kind, n, j + 1)
                    extra(j, 0)
                    fc2(kind, n, j)
                    extra(j, 1)
                for i in range(2):
                    x_out_back(kind, n, i)
                extra(J, 0)

            def body(t, kind, front, back):
                slots = {}

                def at(u, f, *args):
                    slots.setdefault(u, []).append(lambda: f(kind, *args))

                if back:
                    for oc in range(C):
                        at(1 + oc, project, t - 1, oc)
                if front:
                    for c in range(C):
                        at(2 + c, ln1, t + 1, c)
                at(4, max_rows, t, 1)
                if back:
                    for i in range(2):
                        at(6 + i, x_mid_back, t - 1, i)
                if front:
                    for i in range(2 * C):
                        at(9 + 2 * i, qk, t + 1, i)
                    at(19, values, t + 1, 0)
                if back:
                    at(23, ln2, t - 1)
                for i in range(BT):
                    at(29 + i, o_tokens, t, i)
                for u in range(UNITS):
                    exp_scores(t, u)
                    if u % GH == 2 and u > GH:
                        attend(t, u // GH - 1)
                    for f in slots.get(u, []):
                        f()
                attend(t, 2 * G - 1)
                if front:
                    values(kind, t + 1, 1)
                for i in range(BT, TILES):
                    o_tokens(kind, t, i)
                o_features(kind, t, 0)
                if back:
                    fc1(kind, t - 1, 0)
                o_features(kind, t, 1)
                some = maxes(t + 1)
                if back:
                    def extra(j, k):
                        if front:
                            some(MAXES[j] // 2 if j < J else LATE)
                            if j == J - 2 and k == 1:
                                max_rows(kind, t + 1, 0)
                    mlp(kind, t - 1, extra)
                elif front:
                    some(MR_AFTER)
                    max_rows(kind, t + 1, 0)
                    some(UNITS - MR_AFTER)

            def back(t, kind):
                for oc in range(C):
                    project(kind, t, oc)
                for i in range(2):
                    x_mid_back(kind, t, i)
                ln2(kind, t)
                fc1(kind, t, 0)
                mlp(kind, t, lambda j, k: None)

            schedule(pe, prelude_, body, back, switch0, switch3)

        @block.vector
        def _(dve):
            v = nc.vector

            def norm_stats(x, k, n, st):
                settle(dve, passed, n)
                for i in range(TILES):
                    v.bn_stats(stats[:, k, i], x[:, i]).then_inc(st, 1)
                dve.wait_ge(st, (2 * TILES + 1) * n + TILES)
                settle(dve, passed, n)
                for i in range(TILES):
                    v.bn_aggr(mv[:, k, i], stats[:, k, i]).then_inc(st, 1)
                dve.wait_ge(st, (2 * TILES + 1) * n + 2 * TILES)
                v.tensor_scalar(var[:, k], mv[:, k, :, 1], EPS, None, ALU.add).then_inc(st, 1)

            def normalise(x, k, n, rstd_ready, xh, ready_):
                dve.wait_ge(rstd_ready, n + 1)
                for i in range(TILES):
                    v.tensor_scalar(xh[:, i], x[:, i], mv[:, k, i, 0:1], rstd[:, k, i:i + 1],
                                    ALU.subtract, ALU.mult).then_inc(ready_, 1)

            def front_norm(n):
                norm_stats(xres[:, n % PAIRS], 0, n, st0)
                normalise(xres[:, n % PAIRS], 0, n, rstd0, xh0, xh0_ready)

            def load_m0(n):
                v.tensor_copy(m0[:], mod_p0[:, n]).then_inc(m0_ready, 1)

            def load_m3(n):
                v.tensor_copy(m3[:], mod_p3[:, n]).then_inc(m3_ready, 1)

            def round_h0(kind, n):
                if not isinstance(n, int) or n > 1:
                    kind.full(dve, "proj1")
                for c in range(C):
                    kind.read(dve, f"ln1_{c}")
                    v.tensor_copy(h0_hi[:, c], h0[:, c]).then_inc(h0_rounded, 1)

            def round_h3(kind, n):
                for c in range(C):
                    kind.read(dve, f"ln2_{c}")
                    v.tensor_copy(h3_hi[:, c], h3[:, c]).then_inc(h3_rounded, 1)

            def o_out(kind, n):
                for b in range(2):
                    src, done = kind.full(dve, f"ofm{b}")
                    for c in range(C):
                        last = v.tensor_scalar(h0[:, c, b * N:(b + 1) * N], src[:, c * N:(c + 1) * N],
                                               bias_v[:, n, c:c + 1], None, ALU.add)
                    last.then_inc(done, 1)
                for b in range(2):
                    kind.read(dve, f"ofm{b}")
                for c in range(C):
                    v.tensor_copy(h0_hi[:, c], h0[:, c]).then_inc(o_rounded, 1)

            def qk(kind, n, i):
                src, done = kind.full(dve, f"qk{i}")
                link = Chain(dve, qk_chain, n, 3 * 2 * C, 3 * i).link
                if not isinstance(n, int) or n > 0 or i >= 2:
                    dve.wait_ge(scr_in[i % 2], 16 * (2 * n + i // 2))
                    dve.wait_ge(part3, 2 * C * n + i - 1)
                p = parts[:, i % 2]
                last = v.tensor_scalar(qf[:], src[:], bias0[:, i:i + 1], QSCALE if i < C else 1.0, ALU.add, ALU.mult)
                last.then_inc(done, 1)
                kind.read(dve, f"qk{i}")
                link(v.tensor_copy(p[:, 0], qf[:]))
                link(v.tensor_tensor(qr[:, i % 2], qf[:], p[:, 0], ALU.subtract))
                v.tensor_copy(p[:, 1], qr[:, i % 2]).then_inc(qk_chain, 1)

            def values(kind, n, b):
                src, done = kind.full(dve, f"v{b}")
                if not isinstance(n, int) or n > 0:
                    dve.wait_ge(av_full, 2 * G * n - (0 if b else G))
                v.tensor_copy(vaug[:, b * BT:(b + 1) * BT, :, 0:DH],
                              src[:].rearrange("p (i h d) -> p i h d", i=BT, h=H)).then_inc(done, 1)
                kind.read(dve, f"v{b}")

            def row_max(n, b, h):
                u = b * H + h
                dve.wait_ge(mx_full, UNITS * n + u + 1)
                v.tensor_reduce(mx[:, :, h], scb[u % SC][:].rearrange("p (i k) -> p i k", i=BT), AX_X,
                                ALU.max).then_inc(mx_free, 1)

            def max_parts(n, b):
                dve.wait_ge(mx_free, UNITS * n + H * (b + 1))
                link = Chain(dve, max_chain, n, 8, 4 * b).link
                link(v.tensor_scalar(mm_parts[:, :, 0], mx[:], -1.0, None, ALU.mult))
                link(v.scalar_tensor_tensor(mr[:], mx[:], -1.0, mm_parts[:, :, 0], ALU.mult, ALU.subtract))
                link(v.tensor_copy(mm_parts[:, :, 1], mr[:]))
                v.tensor_tensor(mm_parts[:, :, 2], mr[:], mm_parts[:, :, 1], ALU.subtract).then_inc(max_chain, 1)

            def max_rows(kind, n, b):
                src, done = kind.full(dve, f"mr{b}")
                if b or not isinstance(n, int) or n > 0:
                    dve.wait_ge(mt_scr, 16 * (2 * n + b))
                v.tensor_copy(mt[:], src[0:PARTS * H, 0:N // 2].bitcast(BF16)).then_inc(done, 1)

            def o_norm(kind, n, i):
                src, done = kind.full(dve, f"otm{i}")
                o = src[:].rearrange("p (h r) -> p h r", h=H)
                v.reciprocal(rden[:, i], o[:, :, DH]).then_inc(rden_chain, 1)
                dve.wait_ge(rden_chain, TILES * n + i + 1)
                v.tensor_tensor(xh3[:, i].rearrange("p (h d) -> p h d", h=H), o[:, :, 0:DH],
                                rden[:, i].unsqueeze(2).to_broadcast([P, H, DH]), ALU.mult).then_inc(done, 1)

            def add_x(kind, name, n, i):
                src, done = kind.full(dve, name)
                xs = xres[:, n % PAIRS, 2 * i:2 * i + 2, :]
                v.tensor_tensor(xs, src[:].rearrange("p (t f) -> p t f", t=2), xs, ALU.add).then_inc(done, 1)
                kind.read(dve, name)

            def split_weights(l, base, loaded, chunks):
                for k, (hi, lo) in enumerate(chunks):
                    dve.wait_ge(loaded[k], 16 * (l + 1))
                    v.tensor_copy(hi, prob[:, k % RING]).then_inc(w_split, 1)
                    dve.wait_ge(w_split, 2 * (CHUNKS * l + base + k) + 1)
                    v.tensor_tensor(lo, prob[:, k % RING], hi.bitcast(F32), ALU.subtract).then_inc(w_split, 1)

            def pieces(hi, lo):
                h, o = (x[:].rearrange("p a b -> p (a b)") for x in (hi, lo))
                return [(h[:, k:k + W_CHUNK], o[:, k:k + W_CHUNK]) for k in range(0, h.shape[1], W_CHUNK)]

            def switch0(l):
                dve.wait_ge(bias0_in, 16 * (l + 1))
                split_weights(l, 0, w0_in, pieces(w0_hi, w0_lo))

            def switch3(l):
                split_weights(l, W0_CHUNKS, w3_in, pieces(wp_hi, wp_lo) + pieces(w1_hi, w1_lo) + pieces(w2_hi, w2_lo))
                dve.wait_ge(bias3_in, 16 * (l + 1))
                settle(dve, passed, l)

            def maxima(kind, n, units):
                for u in units:
                    row_max(n, u // H, u % H)
                    if u % H == H - 1:
                        max_parts(n, u // H)
                    if u == MR_AFTER - 1:
                        max_rows(kind, n, 0)

            def prelude_():
                v.memset(vaug[:, :, :, DH:], 1.0).then_inc(ready, 1)
                for b in range(2):
                    v.memset(kp[b][KR:KM], 1.0).then_inc(ready, 1)
                    v.memset(qp[b][KR:KA], 1.0).then_inc(ready, 1)
                front_norm(0)
                load_m0(0)
                switch0(0)
                round_h0(PRE, 0)
                for i in range(2 * C):
                    qk(PRE, 0, i)
                for b in range(2):
                    values(PRE, 0, b)
                front_norm(1)
                dve.wait_ge(bias_v_in, 16)
                switch3(0)
                maxima(PRE, 0, range(UNITS))

            def body(t, kind, front, back):
                if front:
                    load_m0(t + 1)
                if back:
                    load_m3(t - 1)
                if front:
                    round_h0(kind, t + 1)
                max_rows(kind, t, 1)
                if back:
                    for i in range(2):
                        add_x(kind, f"xa{i}", t - 1, i)
                    norm_stats(xres[:, (t - 1) % PAIRS], 1, t - 1, st3)
                if front:
                    for i in range(C):
                        qk(kind, t + 1, i)
                if back:
                    normalise(xres[:, (t - 1) % PAIRS], 1, t - 1, rstd3, xh3, xh3_ready)
                if front:
                    for i in range(C, 2 * C):
                        qk(kind, t + 1, i)
                    values(kind, t + 1, 0)
                if back:
                    round_h3(kind, t - 1)
                if front:
                    front_norm(t + 2)
                for i in range(BT):
                    o_norm(kind, t, i)
                if front:
                    values(kind, t + 1, 1)
                for i in range(BT, TILES):
                    o_norm(kind, t, i)
                o_out(kind, t)
                late = UNITS - LATE if back else UNITS
                if front:
                    maxima(kind, t + 1, range(late))
                if back:
                    for i in range(2):
                        add_x(kind, f"xb{i}", t - 1, i)
                if front:
                    maxima(kind, t + 1, range(late, UNITS))

            def back(t, kind):
                load_m3(t)
                for i in range(2):
                    add_x(kind, f"xa{i}", t, i)
                norm_stats(xres[:, t % PAIRS], 1, t, st3)
                normalise(xres[:, t % PAIRS], 1, t, rstd3, xh3, xh3_ready)
                round_h3(kind, t)
                for i in range(2):
                    add_x(kind, f"xb{i}", t, i)

            schedule(dve, prelude_, body, back, switch0, switch3)

        @block.scalar
        def _(act):
            a = nc.scalar

            def modulate(kind, names, dst, m, scale, shift_):
                for c, name in enumerate(names):
                    src, done = kind.full(act, name)
                    for b in range(2):
                        t = slice(b * N, (b + 1) * N)
                        last = a.activation(dst[:, c, t], src[:, t], ACT.Identity, bias=m[:, b, c, shift_:shift_ + 1],
                                            scale=m[:, b, c, scale:scale + 1])
                    last.then_inc(done, 1)

            def ln1(kind, n):
                act.wait_ge(m0_ready, n + 1)
                if not isinstance(n, int) or n > 0:
                    act.wait_ge(h0_split, C * n)
                if not isinstance(n, int) or n > 1:
                    act.wait_ge(o_split, C * (n - 1))
                modulate(kind, ("ln1_0", "ln1_1"), h0, m0, 0, 1)

            def project(kind, n):
                act.wait_ge(m3_ready, n + 1)
                modulate(kind, ("proj0", "proj1"), h3, m3, 0, 1)

            def ln2(kind, n):
                for i in range(2):
                    kind.full(act, f"xa{i}")
                modulate(kind, ("ln2_0", "ln2_1"), h3, m3, 2, 3)

            def gelus(kind, n):
                for j in range(J):
                    src, done = kind.full(act, f"fc1_{j}")
                    if j >= 2:
                        act.wait_ge(gelu_split, J * n + j - 1)
                        act.wait_ge(fc2_read, (J - 1) * n + j - 1)
                    bias = bias3[:, j:j + 1]
                    a.activation(g_hi[:, j % 2], src[:], ACT.Gelu, bias=bias)
                    a.activation(gl[:, j % 2], src[:], ACT.Gelu, bias=bias).then_inc(done, 1)
                act.wait_ge(h3_split, C * (n + 1))
                modulate(kind, ("fc2_0", "fc2_1"), h3, m3, 4, 5)

            def o_copy(t, gg):
                act.wait_ge(av_full, 2 * G * t + gg + 1)
                a.copy(oe[:, gg // G, gg % G], avb[:, 0:N]).then_inc(av_free, 1)

            def switch0(l):
                act.wait_ge(w_split, 2 * (CHUNKS * l + W0_CHUNKS))

            def switch3(l):
                act.wait_ge(w_split, 2 * CHUNKS * (l + 1))

            def prelude_():
                ln1(PRE, 0)
                switch3(0)

            def body(t, kind, front, back):
                for u in range(UNITS):
                    act.wait_ge(sc_full, UNITS * t + u + 1)
                    gg = u // GH
                    if gg >= 2 or not isinstance(t, int) or t > 0:
                        act.wait_ge(av_full, 2 * G * t + gg - 1)
                    a.activation(prob[:, u % RING], scb[u % SC][:], ACT.Exp).then_inc(exped, 1)
                    if u % GH == 3 and u > GH:
                        o_copy(t, gg - 1)
                    if back and u == 3:
                        project(kind, t - 1)
                    if front and u == 5:
                        ln1(kind, t + 1)
                    if back and u == 25:
                        ln2(kind, t - 1)
                o_copy(t, 2 * G - 1)
                if back:
                    gelus(kind, t - 1)

            def back(t, kind):
                project(kind, t)
                ln2(kind, t)
                gelus(kind, t)

            schedule(act, prelude_, body, back, switch0, switch3)

        @block.gpsimd
        def _(pool):
            g = nc.gpsimd

            def rest(lo, src, hi, done):
                g.tensor_tensor(lo, src, hi.bitcast(F32), ALU.subtract).then_inc(done, 1)

            def power(k, n, st, ready_):
                pool.wait_ge(st, (2 * TILES + 1) * (n + 1))
                g.tensor_tensor(rstd[:, k], var[:, k], mhalf[:], ALU.pow).then_inc(ready_, 1)

            def front_h0(kind, n):
                for c in range(C):
                    pool.wait_ge(h0_rounded, C * n + c + 1)
                    rest(h0_lo[:, c], h0[:, c], h0_hi[:, c], h0_split)

            def third(kind, n, i):
                pool.wait_ge(qk_chain, 3 * 2 * C * n + 3 * (i + 1))
                g.tensor_tensor(parts[:, i % 2, 2], qr[:, i % 2], parts[:, i % 2, 1], ALU.subtract).then_inc(part3, 1)

            def back_o(kind, n):
                for c in range(C):
                    pool.wait_ge(o_rounded, C * n + c + 1)
                    rest(h0_lo[:, c], h0[:, c], h0_hi[:, c], o_split)

            def back_ln2(kind, n):
                for c in range(C):
                    pool.wait_ge(h3_rounded, C * n + c + 1)
                    rest(h3_lo[:, c], h3[:, c], h3_hi[:, c], h3_split)

            def back_gelu(kind, n, chunks):
                for j in chunks:
                    kind.read(pool, f"fc1_{j}")
                    if j >= 2:
                        pool.wait_ge(fc2_read, (J - 1) * n + j - 1)
                    rest(g_lo[:, j % 2], gl[:, j % 2], g_hi[:, j % 2], gelu_split)

            def switch0(l):
                pass

            def switch3(l):
                pass

            def prelude_():
                g.memset(mhalf[:], -0.5).then_inc(half_ready, 1)
                pool.wait_ge(half_ready, 1)
                power(0, 0, st0, rstd0)
                front_h0(PRE, 0)
                for i in range(2 * C):
                    third(PRE, 0, i)
                power(0, 1, st0, rstd0)

            def body(t, kind, front, back):
                if front:
                    front_h0(kind, t + 1)
                if back:
                    power(1, t - 1, st3, rstd3)
                if front:
                    for i in range(2 * C):
                        third(kind, t + 1, i)
                if back:
                    back_ln2(kind, t - 1)
                if front:
                    power(0, t + 2, st0, rstd0)
                if back:
                    back_gelu(kind, t - 1, range(2))
                back_o(kind, t)
                if back:
                    back_gelu(kind, t - 1, range(2, J))

            def back(t, kind):
                power(1, t, st3, rstd3)
                back_ln2(kind, t)
                back_gelu(kind, t, range(J))

            schedule(pool, prelude_, body, back, switch0, switch3)

        @block.sync
        def _(sp):
            def load_weights(l, base, loaded):
                for k, done in enumerate(loaded):
                    if k >= RING:
                        sp.wait_ge(w_split, 2 * (CHUNKS * l + base + k - RING + 1))
                    sp.dma_start(prob[:, k % RING], ins["tw"][l, :, base + k]).then_inc(done, 16)

            def switch0(l):
                if not isinstance(l, int):
                    sp.wait_ge(part3, 2 * C * PAIRS * l)
                    sp.wait_ge(av_full, 2 * G * (PAIRS * l - 1))
                sp.dma_start(bias0[:], ins["tbias"][l, :, 0:2 * C]).then_inc(bias0_in, 16)
                load_weights(l, 0, w0_in)

            def switch3(l):
                if not isinstance(l, int):
                    sp.wait_ge(av_full, 2 * G * (PAIRS * l + 1))
                    load_weights(l, W0_CHUNKS, w3_in)
                    sp.wait_ge(gelu_split, J * PAIRS * l)
                else:
                    sp.wait_ge(w_split, 2 * W0_CHUNKS)
                    load_weights(l, W0_CHUNKS, w3_in)
                sp.dma_start(bias3[:], ins["tbias"][l, :, 3 * C:]).then_inc(bias3_in, 16)

            def scratch(n):
                for i in range(2 * C):
                    if i == 0 and (not isinstance(n, int) or n > 0):
                        for b in range(2):
                            sp.wait_ge(pack_in[b], 16 * PACKS * n)
                    sp.wait_ge(part3, 2 * C * n + i + 1)
                    sp.dma_start(scr_qk[i // C, :, (i % C) * P:(i % C + 1) * P, :].rearrange("k p t -> p k t"),
                                 parts[:, i % 2]).then_inc(scr_in[i % 2], 16)

            def pack(n, b):
                for r in range(2):
                    sp.wait_ge(scr_in[r], 16 * 2 * (n + 1))
                if not isinstance(n, int) or n > 0:
                    sp.wait_ge(sc_full, UNITS * n - (0 if b else H))
                for side, dst, which in ((0, qp[b], Q_PART), (1, kp[b], K_PART)):
                    for j, part in enumerate(which):
                        src = scr_qk[side, part].rearrange("(h d) t -> d h t", d=DH)[:, :, b * N:(b + 1) * N]
                        sp.dma_start(dst[16 * j:16 * (j + 1)], src).then_inc(pack_in[b], 16)
                mask = scr_mask[2 * n + b].unsqueeze(0).unsqueeze(0).to_broadcast([1, H, N])
                sp.dma_start(kp[b][KR:KA], mask).then_inc(pack_in[b], 16)

            def max_rows(kind, n, b):
                kind.read(sp, f"mr{b}")
                sp.dma_start(scr_max[b], mt[:]).then_inc(mt_scr, 16)
                sp.wait_ge(mt_scr, 16 * (2 * n + b + 1))
                sp.dma_start(qp[b][KA:KM], scr_max[b].rearrange("(k h) t -> k h t", k=PARTS)).then_inc(mrow_in[b], 16)

            def pair_in(kind, n):
                scratch(n)
                for b in range(2):
                    pack(n, b)

            def prelude_():
                switch0(0)
                sp.dma_start(bias_v[:], ins["bias_v"]).then_inc(bias_v_in, 16)
                sp.wait_ge(ready, 5)
                pair_in(PRE, 0)
                switch3(0)
                max_rows(PRE, 0, 0)

            def store(kind, pair):
                for i in range(2):
                    kind.read(sp, f"xb{i}")
                sp.dma_start(out_dram[pair], xres[:, pair]).then_inc(outs, 16)

            def body(t, kind, front, back):
                if not front:
                    for pair in range(PAIRS - 2):
                        store(Kind(middle_, STEPS - 3), pair)
                max_rows(kind, t, 1)
                if front:
                    pair_in(kind, t + 1)
                    max_rows(kind, t + 1, 0)

            def back(t, kind):
                store(LST, PAIRS - 2)
                store(kind, PAIRS - 1)
                sp.wait_ge(outs, 16 * PAIRS)

            schedule(sp, prelude_, body, back, switch0, switch3)


def build(nc, ins, out_dram):
    with ExitStack() as ctx:
        def sb(name, shape, dt=F32):
            return ctx.enter_context(nc.sbuf_tensor(name, shape, dt))

        xres = sb("xres", [P, PAIRS, TILES, D])
        mod_p0 = sb("mod_p0", [P, LAYERS * PAIRS, 2, C, 2])
        mod_p3 = sb("mod_p3", [P, LAYERS * PAIRS, 2, C, 6])
        ident = sb("ident", [P, P])
        identb = sb("identb", [P, P], BF16)
        scr_qk = nc.dram_tensor("scr_qk", (2, PARTS, D, T), BF16, kind="Internal").ap()
        scr_max = nc.dram_tensor("scr_max", (2, PARTS * H, N), BF16, kind="Internal").ap()
        scr_mask = nc.dram_tensor("scr_mask", (LAYERS * B, N), BF16, kind="Internal").ap()
        graph_layer(nc, ins, xres, mod_p0, mod_p3, ident, identb, scr_mask)
        transformer_layers(nc, ins, xres, mod_p0, mod_p3, ident, identb, out_dram, scr_qk, scr_max, scr_mask)


def kernel(**a):
    import concourse.bacc as bacc
    from concourse.bass_utils import run_bass_kernel_spmd

    def arr(name):
        return np.asarray(a[name])

    def rows(w):
        return np.asarray(w).reshape(-1, P, w.shape[-1]).transpose(1, 0, 2)

    def cols(v, k=C):
        return np.asarray(v).reshape(k, P).T

    f32 = np.float32
    x = arr("x").reshape(PAIRS, TILES, P, D).transpose(0, 2, 1, 3)
    mask = arr("mask_BxSxSx11_ik0")
    adj = np.stack([mask[:, :, :NK, :], mask[:, :NK, :, :].transpose(0, 2, 1, 3)], axis=2)
    adj = adj.reshape(PAIRS, TILES, P, 2 * NK, L).transpose(0, 2, 1, 3, 4).reshape(PAIRS, P, TILES * 2 * NK, L)
    w_self = arr("L0_cond_W_self")
    wq, wk, wout = arr("L0_cond_Wq"), arr("L0_cond_Wk"), arr("L0_cond_Wout").reshape(2, D, D)
    gw = np.stack([rows(w.T) for w in (w_self[:, :D], wq[0], wq[1], wk[0], wk[1], wout[0], wout[1])])
    bq, bk, bo = arr("L0_cond_bq"), arr("L0_cond_bk"), arr("L0_cond_bout")
    gbias = np.stack([cols(v) for v in (arr("L0_cond_b_self"), bq[0], bq[1], bk[0], bk[1], bo[0], bo[1])], axis=1)
    lab = np.broadcast_to(np.concatenate([arr("L0_cond_w_bias"), arr("L0_cond_b_bias").reshape(1)]), (P, L + 1))

    def m1(k):
        return arr(f"L1_cond_{k}")

    def m2(k):
        return arr(f"L2_cond_{k}")

    def m3(k):
        return arr(f"L3_cond_{k}")

    vec1 = ("b1", "g1", "a1", "b2", "g2", "a2")
    ada = [rows(np.concatenate([m1(v + "_w") for v in vec1], axis=1)), rows(m2("w_ada"))]
    w31, w32 = m3("w_adaln1"), m3("w_adaln2")
    ada.append(rows(np.concatenate([w31[D:], w31[:D], w32[D:], w32[:D]], axis=0).T))
    b31, b32 = m3("b_adaln1"), m3("b_adaln2")
    zero = np.zeros(D, f32)
    ada_b = np.stack([np.stack([cols(m1(v + "_b")) for v in vec1], axis=1),
                      np.stack([cols(v) for v in m2("b_ada").reshape(6, D)], axis=1),
                      np.stack([cols(v) for v in (b31[D:], b31[:D], zero, b32[D:], b32[:D], zero)], axis=1)], axis=1)
    ln_gb = np.stack([cols(m1(v)) for v in ("ln1_g", "ln1_b", "ln2_g", "ln2_b")], axis=1)
    out_b = np.stack([np.stack([cols(p), cols(f)], axis=1) for p, f in (
        (m1("proj_b"), m1("fc2_b")), (m2("b_proj"), m2("b_fc2")), (m3("bo"), m3("b2")))], axis=1)

    blocks = [(m1("qkv_w"), m1("proj_w"), m1("fc1_w"), m1("fc2_w")), (m2("w_qkv"), m2("w_proj"), m2("w_fc1"), m2("w_fc2")),
              (np.concatenate([m3("wq").T, m3("wk").T, m3("wv").T], axis=1), m3("wo").T, m3("w1").T, m3("w2").T)]
    tw = np.stack([np.concatenate([rows(w).reshape(P, -1) for w in ws], axis=1).reshape(P, -1, W_CHUNK) for ws in blocks])
    qkv_b = [m1("qkv_b"), np.zeros(3 * D, f32), np.concatenate([m3("bq"), m3("bk"), m3("bv")])]
    fc1_b = [m1("fc1_b"), m2("b_fc1"), m3("b1")]
    tbias = np.stack([np.concatenate([cols(b, 3 * C), cols(f, J)], axis=1) for b, f in zip(qkv_b, fc1_b)])

    bias_v = np.repeat(np.stack([cols(b, 3 * C)[:, 2 * C:] for b in qkv_b], axis=1), PAIRS, axis=1)

    sel8 = np.kron(np.eye(HC, dtype=f32), np.ones((DH, 1), f32))
    sel80 = np.kron(np.eye(GH, dtype=f32), np.ones((NK, 1), f32))
    inputs = {"x": x, "mask": arr("mask_BxS_bf0"), "adj": adj, "cond": cols_of(arr("cond_1024")), "wq_self": rows(w_self[:, D:].T), "gw": gw, "gbias": gbias,
              "lab": lab, "sel8": sel8, "sel80": sel80, "ident": np.eye(P, dtype=f32), "ada0": ada[0], "ada1": ada[1],
              "ada2": ada[2], "ada_b": ada_b, "ln_gb": ln_gb, "out_b": out_b, "tw": tw, "tbias": tbias, "bias_v": bias_v}
    inputs = {k: np.ascontiguousarray(v) for k, v in inputs.items()}

    nc = bacc.Bacc("TRN2", target_bir_lowering=False, num_devices=1)
    ins = {k: nc.dram_tensor(f"in_{k}", v.shape, mybir.dt.from_np(v.dtype), kind="ExternalInput").ap()
           for k, v in inputs.items()}
    out = nc.dram_tensor("out_x", (PAIRS, P, TILES, D), F32, kind="ExternalOutput").ap()
    build(nc, ins, out)
    r = run_bass_kernel_spmd(nc, [{f"in_{k}": v for k, v in inputs.items()}], core_ids=[0])
    y = r.results[0]["out_x"]
    return y.transpose(0, 2, 1, 3).reshape(B, N, D)


def cols_of(cond):
    return cond.T.reshape(C, P, B).transpose(1, 0, 2)
```

```python
from contextlib import ExitStack

import numpy as np
import concourse.bass as bass
from concourse import mybir

F32 = mybir.dt.float32
F32R = mybir.dt.float32r
BF16 = mybir.dt.bfloat16
I32 = mybir.dt.int32
ALU = mybir.AluOpType
ACT = mybir.ActivationFunctionType
AX_X = mybir.AxisListType.X

P = 128
B, N, D = 16, 256, 256
C = D // P
H, DH = 16, 16
HC = P // DH
PAIRS = B // 2
T = 2 * N
TILES = T // P
BT = N // P
LAYERS = 3
DFF = 1024
J = DFF // P
NK, L = 20, 11
NEG = -9000000000000000.0
EPS = 1e-5
QSCALE = DH ** -0.5
PARTS = 3
Q_PART = (0, 0, 1, 1, 0, 2)
K_PART = (0, 1, 0, 1, 2, 0)
KR = 16 * len(Q_PART)
KA = KR + 1
KM = KA + PARTS
MASKED = -1e30
GH = 4
G = H // GH
RING = 8
GR = GH * NK
SC = 4
UNITS = 2 * H
W_CHUNK = 512


class Banks:

    def __init__(self, order, before):
        self.where, self.uses = {}, {}
        for name, bank in order:
            k = self.uses.get(bank, 0)
            self.where[name] = (bank, k)
            self.uses[bank] = k + 1
        self.before = before

    def use(self, name, step):
        bank, k = self.where[name]
        return bank, step * self.uses[bank] + self.before.get(bank, 0) + k

    def after(self, steps):
        banks = set(self.uses) | set(self.before)
        return {b: self.before.get(b, 0) + steps * self.uses.get(b, 0) for b in banks}


class Chain:

    def __init__(self, eng, sem, step, per_step, at=0):
        self.eng, self.sem, self.base, self.per_step, self.k = eng, sem, step * per_step, per_step, at

    def link(self, ins):
        self.k += 1
        assert self.k <= self.per_step
        ins.then_inc(self.sem, 1)
        self.eng.wait_ge(self.sem, self.base + self.k)


def mm3(pe, out, a_hi, a_lo, b_hi, b_lo, first, last):
    pe.matmul(out, a_hi, b_hi, start=first, stop=False)
    pe.matmul(out, a_hi, b_lo, start=False, stop=False)
    return pe.matmul(out, a_lo, b_hi, start=False, stop=last)


def settle(eng, passed, n):
    if not isinstance(n, int):
        eng.sem_inc(passed)


def graph_layer(nc, ins, xres, mod_p0, mod_p3, ident, identb, scr_mask):
    with ExitStack() as ctx:
        def sb(name, shape, dt=F32):
            return ctx.enter_context(nc.sbuf_tensor("g_" + name, shape, dt))

        def sem(name):
            return ctx.enter_context(nc.semaphore("g_" + name))

        bank = [ctx.enter_context(nc.psum_tensor(f"g_bank{i}", [P, 512], F32)) for i in range(8)]

        NW = 7
        AFFS = 3
        NU = TILES * 2
        w_hi = sb("w_hi", [P, NW, C, D], F32R)
        w_lo = sb("w_lo", [P, NW, C, D], F32R)
        w_raw = sb("w_raw", [P, 2, C, D])
        wq_self = sb("wq_self", [P, C, D])
        ada_w = sb("ada_w", [P, C, 6 * D])
        cond = sb("cond", [P, C, B])
        cond_silu = sb("cond_silu", [P, C, B])
        ada_b = sb("ada_b", [P, LAYERS, 6, C])
        ln_gb = sb("ln_gb", [P, 4, C])
        out_b = sb("out_b", [P, LAYERS, 2, C])
        modv = sb("modv", [P, 6, C, B])
        mask = sb("mask", [LAYERS * B, N], mybir.dt.uint8)
        mask_rows = sb("mask_rows", [LAYERS * B, N], BF16)
        modt = sb("modt", [P, C, B])
        gbias = sb("gbias", [P, 7, C])
        bout = sb("bout", [P, C])
        bq = sb("bq", [P, 2 * C])
        lab = sb("lab", [P, L + 1])
        sel8 = sb("sel8", [P, HC])
        sel80 = sb("sel80", [GR, GH])
        qw = sb("qw", [P, C, PAIRS, 2])
        adj = sb("adj", [P, TILES * 2 * NK, L], I32)
        prod = sb("prod", [P, TILES * 2 * NK, L])
        vb = sb("vb", [P, TILES * 2 * NK])
        keep = sb("keep", [P, TILES * 2, NK])
        shift = sb("shift", [P, TILES * 2, NK])
        neg = sb("neg", [P, TILES * 2 * NK])
        x_tok = sb("x_tok", [P, TILES, D])
        rsum = sb("rsum", [P, TILES])
        nz = sb("nz", [P, TILES], BF16)
        nzb = sb("nzb", [P, T])
        feat = sb("feat", [P, C, T])
        f_hi = sb("f_hi", [P, C, T], F32R)
        f_lo = sb("f_lo", [P, C, T], F32R)
        st = sb("st", [P, C, T])
        outp = sb("outp", [P, C, T])
        s_hi = sb("s_hi", [P, C, T], F32R)
        s_lo = sb("s_lo", [P, C, T], F32R)
        q_f = sb("q_f", [P, 2, T])
        q_hi = sb("q_hi", [P, 2 * C, T], F32R)
        q_lo = sb("q_lo", [P, 2 * C, T], F32R)
        k_f = sb("k_f", [P, 2 * C, 2, NK])
        kbd = sb("kbd", [P, 2, 2 * C, HC * NK])
        kbd_hi = sb("kbd_hi", [P, 2, 2 * C, HC * NK], F32R)
        kbd_lo = sb("kbd_lo", [P, 2, 2 * C, HC * NK], F32R)
        s_rep = sb("s_rep", [P, 2, C, 2, GR], F32R)
        vbd = sb("vbd", [GR, 2, 2, G, GH * DH])
        aff = sb("aff", [P, AFFS, H, NK])
        e = sb("e", [P, NU, H, NK])
        mx = sb("mx", [P, AFFS, H])
        den = sb("den", [P, NU, H])
        wt = sb("wt", [GR, 2, G, T])

        raw_in = [sem(f"raw_in{i}") for i in range(2)]
        x_in = sem("x_in")
        consts, ada_in, adj_in = sem("consts"), sem("ada_in"), sem("adj_in")
        w_split, qw_ps, qw_done, mod_ps, mod_done = sem("w_split"), sem("qw_ps"), sem("qw_done"), sem("mod_ps"), sem("mod_done")
        mod_raw, mod_tanh, silu = sem("mod_raw"), sem("mod_tanh"), sem("silu")
        ready = sem("ready")
        mask_in, mask_done, mask_out = sem("mask_in"), sem("mask_done"), sem("mask_out")
        passed = sem("passed")
        adj_used, x_copied, nz_ready, xt_split, s_ready, s_split = (
            sem("adj_used"), sem("x_copied"), sem("nz_ready"), sem("xt_split"), sem("s_ready"), sem("s_split"))
        q_lo_done, kbd_split, rep_ready = sem("q_lo_done"), sem("kbd_split"), sem("rep_ready")
        maxed = sem("maxed")
        s_rounded, kept, sum_ready, summed = sem("s_rounded"), sem("kept"), sem("sum_ready"), sem("summed")
        shifted, exped, dens, weights, relu_out = (
            sem("shifted"), sem("exped"), sem("dens"), sem("weights"), sem("relu_out"))
        prep_chain, soft_chain, st_chain, set_chain = sem("prep_chain"), sem("soft_chain"), sem("st_chain"), sem("set_chain")

        aff_bank = [4 + u % 4 for u in range(NU)]
        order = ([(f"aff{u}", aff_bank[u], "B") for u in range(4)] + [("xt0", 0, "F"), ("xt1", 1, "F"), ("nz", 2, "F")]
                 + [("aff4", aff_bank[4], "B"), ("s0", 3, "F"), ("s1", 0, "F")]
                 + [(f"aff{u}", aff_bank[u], "B") for u in range(5, NU)]
                 + [("q0", 1, "F"), ("q1", 2, "F"), ("q2", 3, "F"), ("q3", 0, "F"), ("k", 1, "F")]
                 + [(f"wt{i}", (2, 3, 0, 1)[i % 4], "B") for i in range(2 * G)] + [("out0", 4, "B"), ("out1", 5, "B")]
                 + [("v0", 2, "F"), ("v1", 3, "F"), ("back0", 6, "B"), ("back1", 7, "B")])
        start_ = Banks([x[:2] for x in order if x[2] == "F"], {i: 0 for i in range(8)})
        loop_ = Banks([x[:2] for x in order], start_.after(1))
        end_ = Banks([x[:2] for x in order if x[2] == "B"], loop_.after(PAIRS - 1))
        full = [sem(f"full{i}") for i in range(8)]
        free = [sem(f"free{i}") for i in range(8)]

        class Kind:

            def __init__(self, banks, at):
                self.banks, self.at = banks, at

            def full(self, eng, name):
                i, k = self.banks.use(name, self.at)
                eng.wait_ge(full[i], k + 1)
                return bank[i], free[i]

            def read(self, eng, name):
                i, k = self.banks.use(name, self.at)
                eng.wait_ge(free[i], k + 1)

            def take(self, pe, name):
                i, k = self.banks.use(name, self.at)
                if not isinstance(k, int) or k > 0:
                    pe.wait_ge(free[i], k)
                return bank[i], full[i]

        START, END = Kind(start_, 0), Kind(end_, 0)
        MODS = (4, 5, 4)

        def pair_loop(eng, start, step, end):
            start(START)
            with eng.Fori(0, PAIRS - 1) as n:
                step(Kind(loop_, n), n)
            end(END)

        block = ctx.enter_context(nc.Block())

        @block.sync
        def _(sp):
            for dst, src in ((cond[:], "cond"), (wq_self[:], "wq_self"), (ident[:], "ident"), (gbias[:], "gbias"),
                             (lab[:], "lab"), (sel8[:], "sel8"), (sel80[:], "sel80"), (ada_b[:], "ada_b"),
                             (ln_gb[:], "ln_gb"), (out_b[:], "out_b")):
                sp.dma_start(dst, ins[src]).then_inc(consts, 16)
            def load_w(i):
                if i >= 2:
                    sp.wait_ge(w_split, 2 * (i - 1))
                sp.dma_start(w_raw[:, i % 2], ins["gw"][i]).then_inc(raw_in[i % 2], 16)

            def load_ada(layer):
                if layer:
                    sp.wait_ge(mod_ps, layer)
                w = (6 if layer < 2 else 4) * D
                sp.dma_start(ada_w[:, :, 0:w], ins[f"ada{layer}"]).then_inc(ada_in, 16)

            sp.dma_start(xres[:, 0], ins["x"][0]).then_inc(x_in, 16)
            for i in range(3):
                load_w(i)
            sp.dma_start(adj[:], ins["adj"][0]).then_inc(adj_in, 16)
            load_ada(0)
            for i in range(3, NW):
                load_w(i)
            sp.wait_ge(x_in, 16)
            sp.dma_start(xres[:, 1], ins["x"][1]).then_inc(x_in, 16)
            load_ada(1)
            sp.dma_start(mask[(LAYERS - 1) * B:], ins["mask"]).then_inc(mask_in, 16)
            load_ada(2)
            with sp.Fori(1, PAIRS - 1) as n:
                sp.wait_ge(adj_used, 2 * n)
                sp.dma_start(adj[:], ins["adj"][n]).then_inc(adj_in, 16)
                sp.wait_ge(x_in, 16 * (n + 1))
                sp.dma_start(xres[:, n + 1], ins["x"][n + 1]).then_inc(x_in, 16)
            sp.wait_ge(adj_used, 2 * (PAIRS - 1))
            sp.dma_start(adj[:], ins["adj"][PAIRS - 1]).then_inc(adj_in, 16)
            sp.wait_ge(mask_done, 2)
            sp.dma_start(scr_mask, mask_rows[:]).then_inc(mask_out, 16)
            sp.wait_ge(mask_out, 16)

        @block.tensor
        def _(pe):
            def modulation(layer):
                pe.wait_ge(silu, 1)
                pe.wait_ge(ada_in, 16 * (layer + 1))
                if layer == 2:
                    END.read(pe, f"aff{NU - 4}")
                rhs = cond_silu if layer == 1 else cond
                for v in range(6 if layer < 2 else 4):
                    for oc in range(C):
                        at, o = (v * C + oc) * B, slice(v * D + oc * P, v * D + (oc + 1) * P)
                        for c in range(C):
                            mm = pe.matmul(bank[MODS[layer]][:, at:at + B], ada_w[:, c, o], rhs[:, c, :],
                                           start=(c == 0), stop=(c == C - 1))
                mm.then_inc(mod_ps, 1)

            def linear(out, w, oc, hi, lo):
                o = slice(oc * P, (oc + 1) * P)
                for c in range(C):
                    mm = mm3(pe, out[:], w_hi[:, w, c, o], w_lo[:, w, c, o], hi[:, c], lo[:, c], c == 0, c == C - 1)
                return mm

            def x_features(kind, n):
                pe.wait_ge(x_copied, n + 1)
                for c in range(C):
                    out, done = kind.take(pe, f"xt{c}")
                    for i in range(TILES):
                        mm = pe.transpose(out[:, i * P:(i + 1) * P], x_tok[:, i, c * P:(c + 1) * P], ident[:])
                    mm.then_inc(done, 1)

            def nonzero(kind, n):
                pe.wait_ge(nz_ready, n + 1)
                out, done = kind.take(pe, "nz")
                for i in range(TILES):
                    mm = pe.matmul(out[:, i * P:(i + 1) * P], nz[:, i:i + 1].to_broadcast([P, P]), identb[:],
                                   start=True, stop=True)
                mm.then_inc(done, 1)

            def self_features(kind, n):
                pe.wait_ge(xt_split, C * (n + 1))
                for oc in range(C):
                    out, done = kind.take(pe, f"s{oc}")
                    linear(out, 0, oc, f_hi, f_lo).then_inc(done, 1)

            def queries(kind, n):
                pe.wait_ge(s_split, C * (n + 1))
                for i in range(2 * C):
                    out, done = kind.take(pe, f"q{i}")
                    linear(out, 1 + i // C, i % C, s_hi, s_lo).then_inc(done, 1)

            def keys(kind, n):
                out, done = kind.take(pe, "k")
                for i in range(2 * C):
                    o, w = slice((i % C) * P, (i % C + 1) * P), 3 + i // C
                    for c in range(C):
                        hi = s_hi[:, c, :].rearrange("p (b t) -> p b t", b=2)[:, :, 0:NK]
                        lo = s_lo[:, c, :].rearrange("p (b t) -> p b t", b=2)[:, :, 0:NK]
                        mm = mm3(pe, out[:, i * 2 * NK:(i + 1) * 2 * NK], w_hi[:, w, c, o], w_lo[:, w, c, o], hi, lo,
                                 c == 0, c == C - 1)
                mm.then_inc(done, 1)

            def values(kind, n):
                pe.wait_ge(rep_ready, 2 * (n + 1))
                for d in range(2):
                    out, done = kind.take(pe, f"v{d}")
                    for b in range(2):
                        for c in range(C):
                            mm = mm3(pe, out[0:GR, b * D:(b + 1) * D], s_rep[:, 0, c, b], s_rep[:, 1, c, b],
                                     w_hi[:, 5 + d, c], w_lo[:, 5 + d, c], c == 0, c == C - 1)
                    mm.then_inc(done, 1)

            def scores(kind, n, u):
                if u == 0:
                    pe.wait_ge(kbd_split, 2 * (n + 1))
                    pe.wait_ge(q_lo_done, 2 * C * (n + 1))
                i, d = u // 2, u % 2
                out, done = kind.take(pe, f"aff{u}")
                for c in range(C):
                    t, at = slice(i * P, (i + 1) * P), c * HC * NK
                    mm = mm3(pe, out[:, at:at + HC * NK], q_hi[:, d * C + c, t], q_lo[:, d * C + c, t],
                             kbd_hi[:, i // BT, d * C + c], kbd_lo[:, i // BT, d * C + c], True, True)
                mm.then_inc(done, 1)

            def output(kind, n):
                pe.wait_ge(weights, NU * (n + 1))
                for d in range(2):
                    for g in range(G):
                        out, done = kind.take(pe, f"wt{d * G + g}")
                        for i in range(TILES):
                            src = e[:, i * 2 + d, g * GH:(g + 1) * GH].rearrange("p h m -> p (h m)")
                            mm = pe.transpose(out[0:GR, i * P:(i + 1) * P], src, ident[:])
                        mm.then_inc(done, 1)
                for i in range(2 * G - 4, 2 * G):
                    kind.read(pe, f"wt{i}")
                for c in range(C):
                    out, done = kind.take(pe, f"out{c}")
                    for b in range(2):
                        for d in range(2):
                            for gg in range(2):
                                g = 2 * c + gg
                                mm = pe.matmul(out[64 * gg:64 * gg + GH * DH, b * N:(b + 1) * N], vbd[:, d, b, g],
                                               wt[:, d, g, b * N:(b + 1) * N], start=(d == 0), stop=(d == 1))
                    mm.then_inc(done, 1)

            def back_to_tokens(kind, n):
                pe.wait_ge(relu_out, C * (n + 1))
                for i in range(2):
                    out, done = kind.take(pe, f"back{i}")
                    for tt in range(2):
                        for c in range(C):
                            t = slice((2 * i + tt) * P, (2 * i + tt + 1) * P)
                            mm = pe.transpose(out[:, tt * D + c * P:tt * D + (c + 1) * P], outp[:, c, t], ident[:])
                    mm.then_inc(done, 1)

            def start(kind):
                pe.wait_ge(consts, 160)
                for oc in range(C):
                    for c in range(C):
                        mm = pe.matmul(bank[7][:, oc * B:(oc + 1) * B], wq_self[:, c, oc * P:(oc + 1) * P], cond[:, c, :],
                                       start=(c == 0), stop=(c == C - 1))
                mm.then_inc(qw_ps, 1)
                x_features(kind, 0)
                pe.wait_ge(ready, 4)
                nonzero(kind, 0)
                pe.wait_ge(w_split, 2)
                self_features(kind, 0)
                modulation(0)
                pe.wait_ge(w_split, 2 * 3)
                queries(kind, 0)
                pe.wait_ge(w_split, 2 * 5)
                keys(kind, 0)
                pe.wait_ge(w_split, 2 * NW)
                values(kind, 0)
                modulation(1)
                pe.wait_ge(qw_done, 1)
                pe.wait_ge(mod_raw, 2)

            def step(kind, n):
                for u in range(4):
                    scores(kind, n, u)
                x_features(kind, n + 1)
                nonzero(kind, n + 1)
                scores(kind, n, 4)
                self_features(kind, n + 1)
                for u in range(5, NU):
                    scores(kind, n, u)
                queries(kind, n + 1)
                keys(kind, n + 1)
                output(kind, n)
                values(kind, n + 1)
                back_to_tokens(kind, n)

            def end(kind):
                n = PAIRS - 1
                for u in range(NU):
                    scores(kind, n, u)
                modulation(2)
                pe.wait_ge(mod_raw, 3)
                output(kind, n)
                back_to_tokens(kind, n)

            pair_loop(pe, start, step, end)

        @block.vector
        def _(dve):
            v = nc.vector
            link = Chain(dve, set_chain, 0, 100).link

            def split_w(i):
                dve.wait_ge(raw_in[i % 2], 16 * (i // 2 + 1))
                v.tensor_copy(w_hi[:, i], w_raw[:, i % 2]).then_inc(w_split, 1)
                dve.wait_ge(w_split, 2 * i + 1)
                v.tensor_tensor(w_lo[:, i], w_raw[:, i % 2], w_hi[:, i].bitcast(F32), ALU.subtract).then_inc(w_split, 1)

            def key_mask():
                v.memset(mask_rows[:], 0.0).then_inc(mask_done, 1)
                dve.wait_ge(mask_in, 16)
                dve.wait_ge(mask_done, 1)
                v.tensor_scalar(mask_rows[(LAYERS - 1) * B:], mask[(LAYERS - 1) * B:], MASKED, None,
                                ALU.mult).then_inc(mask_done, 1)

            def modulation(layer):
                order_v = (0, 1, 2, 3, 4, 5) if layer < 2 else (0, 1, 3, 4)
                dve.wait_ge(mod_ps, layer + 1)
                if layer:
                    dve.wait_ge(mod_done, layer)
                for k, vec in enumerate(order_v):
                    last = v.tensor_tensor(modv[:, vec], bank[MODS[layer]][:, k * C * B:(k + 1) * C * B].rearrange(
                        "p (c b) -> p c b", c=C), ada_b[:, layer, vec].unsqueeze(2).to_broadcast([P, C, B]), ALU.add)
                last.then_inc(mod_raw, 1)
                dve.wait_ge(mod_raw, layer + 1)
                if layer == 0:
                    dve.wait_ge(mod_tanh, 2)
                    link(v.tensor_scalar(modv[:, 2], modv[:, 2], 0.1, None, ALU.mult))
                    link(v.tensor_scalar(modv[:, 5], modv[:, 5], 0.1, None, ALU.mult))
                if layer == 2:
                    link(v.memset(modv[:, 2], 1.0))
                    link(v.memset(modv[:, 5], 1.0))

                def vector_of(mod, k):
                    return mod[:, layer * PAIRS:(layer + 1) * PAIRS, :, :, k].rearrange("p n b c -> p c (n b)")

                for ln in range(2):
                    scale_out, shift_out = (vector_of(mod_p3, 2 + k) if ln else vector_of(mod_p0, k) for k in range(2))
                    gate, gate_bias = vector_of(mod_p3, 4 * ln), vector_of(mod_p3, 4 * ln + 1)
                    shift_v, scale_v, gate_v = modv[:, 3 * ln], modv[:, 3 * ln + 1], modv[:, 3 * ln + 2]
                    if layer == 0:
                        gain = ln_gb[:, 2 * ln].unsqueeze(2).to_broadcast([P, C, B])
                        offset = ln_gb[:, 2 * ln + 1].unsqueeze(2).to_broadcast([P, C, B])
                        link(v.tensor_scalar(scale_v, scale_v, 1.0, None, ALU.add))
                        link(v.tensor_tensor(scale_out, scale_v, gain, ALU.mult))
                        link(v.tensor_tensor(modt[:], scale_v, offset, ALU.mult))
                        link(v.tensor_tensor(shift_out, modt[:], shift_v, ALU.add))
                    else:
                        link(v.tensor_scalar(scale_out, scale_v, 1.0, None, ALU.add))
                        link(v.tensor_copy(shift_out, shift_v))
                    link(v.tensor_copy(gate, gate_v))
                    bias = out_b[:, layer, ln].unsqueeze(2).to_broadcast([P, C, B])
                    last = v.tensor_tensor(gate_bias, gate_v, bias, ALU.mult)
                    link(last) if ln == 0 else last.then_inc(mod_done, 1)

            PREP = 4

            def edges(n):
                prep = Chain(dve, prep_chain, n, PREP).link
                dve.wait_ge(adj_in, 16 * (n + 1))
                prep(v.tensor_reduce(vb[:], adj[:], AX_X, ALU.add))
                v.tensor_scalar(keep[:].rearrange("p u m -> p (u m)"), vb[:], 0.0, None, ALU.is_gt).then_inc(adj_used, 1)
                prep(v.tensor_tensor(prod[:], adj[:], lab[:, 0:L].unsqueeze(1).to_broadcast([P, TILES * 2 * NK, L]), ALU.mult))
                prep(v.tensor_reduce(vb[:], prod[:], AX_X, ALU.add))
                dve.wait_ge(adj_used, 2 * n + 1)
                prep(v.tensor_scalar(neg[:], keep[:].rearrange("p u m -> p (u m)"), -NEG, NEG, ALU.mult, ALU.add))
                v.scalar_tensor_tensor(shift[:].rearrange("p u m -> p (u m)"), vb[:], lab[:, L:L + 1], neg[:],
                                       ALU.add, ALU.add).then_inc(adj_used, 1)

            def row_sums(n):
                dve.wait_ge(x_copied, n + 1)
                v.tensor_reduce(rsum[:], x_tok[:], AX_X, ALU.add).then_inc(sum_ready, 1)
                dve.wait_ge(sum_ready, n + 1)
                v.tensor_scalar(nz[:], rsum[:], 0.0, None, ALU.not_equal).then_inc(nz_ready, 1)

            def self_features(kind, n):
                src, done = kind.full(dve, "nz")
                v.tensor_copy(nzb[:], src[:]).then_inc(done, 1)
                kind.read(dve, "nz")
                for oc in range(C):
                    src, done = kind.full(dve, f"s{oc}")
                    for b in range(2):
                        t = slice(b * N, (b + 1) * N)
                        last = v.scalar_tensor_tensor(st[:, oc, t], nzb[:, t], qw[:, oc, n, b:b + 1], src[:, t],
                                                      ALU.mult, ALU.add)
                    last.then_inc(done, 1)

            def keys(kind, n):
                src, done = kind.full(dve, "k")
                v.tensor_tensor(k_f[:].rearrange("p i b m -> p i (b m)"),
                                src[:, 0:2 * C * 2 * NK].rearrange("p (i m) -> p i m", i=2 * C),
                                gbias[:, 3:5].rearrange("p d c -> p (d c)").unsqueeze(2).to_broadcast(
                                    [P, 2 * C, 2 * NK]), ALU.add).then_inc(done, 1)
                kind.read(dve, "k")
                for b in range(2):
                    for i in range(2 * C):
                        last = v.tensor_tensor(kbd[:, b, i].rearrange("p (h m) -> p h m", h=HC),
                                               k_f[:, i, b].unsqueeze(1).to_broadcast([P, HC, NK]),
                                               sel8[:].unsqueeze(2).to_broadcast([P, HC, NK]), ALU.mult)
                last.then_inc(st_chain, 1)
                dve.wait_ge(st_chain, n + 1)
                v.tensor_copy(kbd_hi[:], kbd[:]).then_inc(kbd_split, 1)
                dve.wait_ge(kbd_split, 2 * n + 1)
                v.tensor_tensor(kbd_lo[:], kbd[:], kbd_hi[:].bitcast(F32), ALU.subtract).then_inc(kbd_split, 1)

            def values(kind, n):
                for d in range(2):
                    src, done = kind.full(dve, f"v{d}")
                    v.tensor_tensor(vbd[:, d].rearrange("p b g (h r) -> p (b g) h r", h=GH),
                                    src[0:GR].rearrange("p (q h r) -> p q h r", h=GH, r=DH),
                                    sel80[:].unsqueeze(1).unsqueeze(3).to_broadcast([GR, 2 * G, GH, DH]),
                                    ALU.mult).then_inc(done, 1)

            def biased_scores(kind, n, u):
                src, done = kind.full(dve, f"aff{u}")
                if u >= AFFS:
                    dve.wait_ge(exped, NU * n + u - AFFS + 1)
                soft = Chain(dve, soft_chain, n, NU, u).link
                a = aff[:, u % AFFS]
                v.tensor_tensor(a, src[:, 0:H * NK].rearrange("p (h m) -> p h m", h=H),
                                keep[:, u].unsqueeze(1).to_broadcast([P, H, NK]), ALU.mult).then_inc(done, 1)
                kind.read(dve, f"aff{u}")
                soft(v.tensor_tensor(a, a, shift[:, u].unsqueeze(1).to_broadcast([P, H, NK]), ALU.add))
                v.tensor_reduce(mx[:, u % AFFS], a, AX_X, ALU.max).then_inc(maxed, 1)

            def denominators(n, u):
                dve.wait_ge(exped, NU * n + u + 1)
                v.tensor_reduce(den[:, u], e[:, u], AX_X, ALU.add).then_inc(summed, 1)
                dve.wait_ge(summed, NU * n + u + 1)
                v.reciprocal(den[:, u], den[:, u]).then_inc(dens, 1)

            def add_output(kind, n):
                for c in range(C):
                    src, done = kind.full(dve, f"out{c}")
                    v.tensor_tensor(outp[:, c], src[:], outp[:, c], ALU.add).then_inc(done, 1)

            def add_x(kind, n):
                for i in range(2):
                    src, done = kind.full(dve, f"back{i}")
                    xs = xres[:, n, 2 * i:2 * i + 2, :]
                    v.tensor_tensor(xs, src[:].rearrange("p (t f) -> p t f", t=2), xs, ALU.add).then_inc(done, 1)

            def start(kind):
                v.memset(vbd[:], 0.0).then_inc(ready, 1)
                dve.wait_ge(consts, 160)
                v.tensor_copy(identb[:], ident[:]).then_inc(ready, 1)
                v.tensor_tensor(bout[:], gbias[:, 5], gbias[:, 6], ALU.add).then_inc(ready, 1)
                v.tensor_scalar(bq[:], gbias[:, 1:3].rearrange("p d c -> p (d c)"), QSCALE, None, ALU.mult).then_inc(ready, 1)
                dve.wait_ge(qw_ps, 1)
                v.tensor_copy(qw[:].rearrange("p c n b -> p (c n b)"), bank[7][:, 0:C * B]).then_inc(qw_done, 1)
                dve.wait_ge(qw_done, 1)
                row_sums(0)
                split_w(0)
                split_w(1)
                self_features(kind, 0)
                for i in range(2, NW):
                    split_w(i)
                edges(0)
                keys(kind, 0)
                values(kind, 0)
                modulation(0)
                modulation(1)

            def step(kind, n):
                for u in range(NU):
                    biased_scores(kind, n, u)
                    if u >= 2:
                        denominators(n, u - 2)
                    if u == 1:
                        row_sums(n + 1)
                    if u == 4:
                        dve.wait_ge(kept, n + 1)
                        self_features(kind, n + 1)
                denominators(n, NU - 2)
                denominators(n, NU - 1)
                edges(n + 1)
                keys(kind, n + 1)
                add_output(kind, n)
                values(kind, n + 1)
                add_x(kind, n)

            def end(kind):
                n = PAIRS - 1
                for u in range(NU):
                    biased_scores(kind, n, u)
                    if u >= 2:
                        denominators(n, u - 2)
                denominators(n, NU - 2)
                denominators(n, NU - 1)
                key_mask()
                modulation(2)
                dve.wait_ge(kept, n + 1)
                add_output(kind, n)
                add_x(kind, n)
                dve.wait_ge(mod_done, LAYERS)

            pair_loop(dve, start, step, end)

        @block.scalar
        def _(act):
            a = nc.scalar

            def copy_x(n):
                act.wait_ge(x_in, 16 * (n + 1))
                if not isinstance(n, int) or n > 0:
                    act.wait_ge(nz_ready, n)
                a.copy(x_tok[:], xres[:, n]).then_inc(x_copied, 1)

            def x_features(kind, n):
                if not isinstance(n, int) or n > 0:
                    act.wait_ge(xt_split, C * n)
                for c in range(C):
                    src, done = kind.full(act, f"xt{c}")
                    a.copy(f_hi[:, c], src[:])
                    a.copy(feat[:, c], src[:]).then_inc(done, 1)

            def self_features(kind, n):
                if not isinstance(n, int) or n > 0:
                    act.wait_ge(rep_ready, 2 * n)
                for oc in range(C):
                    kind.read(act, f"s{oc}")
                    a.activation(s_hi[:, oc], st[:, oc], ACT.Identity, bias=gbias[:, 0, oc:oc + 1]).then_inc(s_rounded, 1)
                    act.wait_ge(s_rounded, C * n + oc + 1)
                    a.activation(st[:, oc], st[:, oc], ACT.Identity, bias=gbias[:, 0, oc:oc + 1]).then_inc(s_ready, 1)

            def query(kind, n, i):
                src, done = kind.full(act, f"q{i}")
                if i >= 2 or not isinstance(n, int) or n > 0:
                    act.wait_ge(q_lo_done, 2 * C * n + i - 1)
                a.activation(q_hi[:, i], src[:], ACT.Identity, bias=bq[:, i:i + 1], scale=QSCALE)
                a.activation(q_f[:, i % 2], src[:], ACT.Identity, bias=bq[:, i:i + 1], scale=QSCALE).then_inc(done, 1)

            def keep_self(kind, n):
                kind.full(act, "aff0")
                act.wait_ge(s_ready, C * (n + 1))
                a.copy(outp[:], st[:]).then_inc(kept, 1)

            def exp(n, u):
                act.wait_ge(shifted, NU * n + u + 1)
                a.activation(e[:, u], aff[:, u % AFFS], ACT.Exp).then_inc(exped, 1)

            def output(kind, n):
                for i in range(2 * G):
                    src, done = kind.full(act, f"wt{i}")
                    a.copy(wt[:, i // G, i % G], src[0:GR]).then_inc(done, 1)
                for c in range(C):
                    kind.read(act, f"out{c}")
                    a.activation(outp[:, c], outp[:, c], ACT.Relu, bias=bout[:, c:c + 1]).then_inc(relu_out, 1)

            def start(kind):
                act.wait_ge(consts, 160)
                a.activation(cond_silu[:], cond[:], ACT.Silu).then_inc(silu, 1)
                act.wait_ge(ready, 4)
                copy_x(0)
                x_features(kind, 0)
                self_features(kind, 0)
                for i in range(2 * C):
                    query(kind, 0, i)
                act.wait_ge(mod_raw, 1)
                a.activation(modv[:, 2], modv[:, 2], ACT.Tanh).then_inc(mod_tanh, 1)
                a.activation(modv[:, 5], modv[:, 5], ACT.Tanh).then_inc(mod_tanh, 1)

            def step(kind, n):
                copy_x(n + 1)
                keep_self(kind, n)
                exp(n, 0)
                x_features(kind, n + 1)
                for u in range(1, 5):
                    exp(n, u)
                self_features(kind, n + 1)
                exp(n, 5)
                exp(n, 6)
                query(kind, n + 1, 0)
                exp(n, 7)
                for i in range(1, 2 * C):
                    query(kind, n + 1, i)
                output(kind, n)

            def end(kind):
                n = PAIRS - 1
                keep_self(kind, n)
                for u in range(NU):
                    exp(n, u)
                output(kind, n)

            pair_loop(act, start, step, end)

        @block.gpsimd
        def _(pool):
            g = nc.gpsimd

            def x_rest(kind, n):
                for c in range(C):
                    kind.read(pool, f"xt{c}")
                    g.tensor_tensor(f_lo[:, c], feat[:, c], f_hi[:, c].bitcast(F32), ALU.subtract).then_inc(xt_split, 1)

            def self_rest(n):
                for c in range(C):
                    pool.wait_ge(s_ready, C * n + c + 1)
                    g.tensor_tensor(s_lo[:, c], st[:, c], s_hi[:, c].bitcast(F32), ALU.subtract).then_inc(s_split, 1)

            def repeat_keys(n):
                pool.wait_ge(s_split, C * (n + 1))
                settle(pool, passed, n)
                for k, part in enumerate((s_hi, s_lo)):
                    for c in range(C):
                        for b in range(2):
                            last = g.tensor_copy(s_rep[:, k, c, b].rearrange("p (h m) -> p h m", h=GH),
                                                 part[:, c, b * N:b * N + NK].unsqueeze(1).to_broadcast([P, GH, NK]))
                    last.then_inc(rep_ready, 1)

            def query_rest(kind, n, i):
                kind.read(pool, f"q{i}")
                g.tensor_tensor(q_lo[:, i], q_f[:, i % 2], q_hi[:, i].bitcast(F32), ALU.subtract).then_inc(q_lo_done, 1)

            def shift_scores(n, u):
                pool.wait_ge(maxed, NU * n + u + 1)
                a = aff[:, u % AFFS]
                g.tensor_tensor(a, a, mx[:, u % AFFS].unsqueeze(2).to_broadcast([P, H, NK]), ALU.subtract).then_inc(shifted, 1)

            def weigh(n, u):
                pool.wait_ge(dens, NU * n + u + 1)
                g.tensor_tensor(e[:, u], e[:, u], den[:, u].unsqueeze(2).to_broadcast([P, H, NK]),
                                ALU.mult).then_inc(weights, 1)

            def start(kind):
                x_rest(kind, 0)
                self_rest(0)
                repeat_keys(0)
                for i in range(2 * C):
                    query_rest(kind, 0, i)

            def step(kind, n):
                shift_scores(n, 0)
                shift_scores(n, 1)
                x_rest(kind, n + 1)
                for u in range(2, 5):
                    shift_scores(n, u)
                    weigh(n, u - 2)
                self_rest(n + 1)
                for u in range(5, NU):
                    shift_scores(n, u)
                    weigh(n, u - 2)
                query_rest(kind, n + 1, 0)
                weigh(n, NU - 2)
                weigh(n, NU - 1)
                for i in range(1, 2 * C):
                    query_rest(kind, n + 1, i)
                repeat_keys(n + 1)

            def end(kind):
                n = PAIRS - 1
                for u in range(NU):
                    shift_scores(n, u)
                    if u >= 2:
                        weigh(n, u - 2)
                weigh(n, NU - 2)
                weigh(n, NU - 1)

            pair_loop(pool, start, step, end)


USES = ([("ln1_0", 2, "F"), ("xb0", 0, "X"), ("xb1", 1, "X"), ("ln1_1", 2, "F"), ("proj0", 0, "B"), ("proj1", 1, "B"),
         ("mr1", 2, "M"), ("xa0", 0, "B"), ("xa1", 1, "B"), ("qk0", 2, "F"), ("qk1", 0, "F"), ("qk2", 1, "F"),
         ("qk3", 2, "F"), ("v0", 0, "F"), ("ln2_0", 1, "B"), ("ln2_1", 2, "B"), ("otm0", 0, "O"), ("otm1", 1, "O"),
         ("v1", 2, "F"), ("fc1_0", 2, "B"), ("otm2", 0, "O"), ("otm3", 1, "O"), ("ofm0", 0, "O"), ("ofm1", 1, "O")]
        + [(f"fc1_{j}", 2, "B") for j in range(1, J)] + [("fc2_0", 0, "B"), ("fc2_1", 1, "B"), ("mr0", 2, "N")])


def uses_of(parts):
    return [(name, bank) for name, bank, part in USES if part in parts]


def transformer_layers(nc, ins, xres, mod_p0, mod_p3, ident, identb, out_dram, scr_qk, scr_max, scr_mask):
    STEPS = LAYERS * PAIRS
    with ExitStack() as ctx:
        def sb(name, shape, dt=F32):
            return ctx.enter_context(nc.sbuf_tensor("t_" + name, shape, dt))

        def sem(name):
            return ctx.enter_context(nc.semaphore("t_" + name))

        def ps(name):
            return ctx.enter_context(nc.psum_tensor("t_" + name, [P, 512], F32))

        lin = [ps(f"lin{i}") for i in range(3)]
        scb = [ps(f"scb{i}") for i in range(SC)]
        avb = ps("avb")

        w0_hi = sb("w0_hi", [P, C, 3 * D], F32R)
        w0_lo = sb("w0_lo", [P, C, 3 * D], F32R)
        wp_hi = sb("wp_hi", [P, C, D], F32R)
        wp_lo = sb("wp_lo", [P, C, D], F32R)
        w1_hi = sb("w1_hi", [P, C, DFF], F32R)
        w1_lo = sb("w1_lo", [P, C, DFF], F32R)
        w2_hi = sb("w2_hi", [P, J, D], F32R)
        w2_lo = sb("w2_lo", [P, J, D], F32R)
        bias0 = sb("bias0", [P, 2 * C])
        bias3 = sb("bias3", [P, J])
        bias_v = sb("bias_v", [P, STEPS, C])
        m0 = sb("m0", [P, 2, C, 2])
        m3 = sb("m3", [P, 2, C, 6])
        stats = sb("stats", [P, 2, TILES, 6])
        mv = sb("mv", [P, 2, TILES, 2])
        var = sb("var", [P, 2, TILES])
        rstd = sb("rstd", [P, 2, TILES])
        mhalf = sb("mhalf", [P, TILES])
        xh0 = sb("xh0", [P, TILES, D])
        xh3 = sb("xh3", [P, TILES, D])
        h0 = sb("h0", [P, C, T])
        h0_hi = sb("h0_hi", [P, C, T], F32R)
        h0_lo = sb("h0_lo", [P, C, T], F32R)
        h3 = sb("h3", [P, C, T])
        h3_hi = sb("h3_hi", [P, C, T], F32R)
        h3_lo = sb("h3_lo", [P, C, T], F32R)
        qf = sb("qf", [P, T])
        qr = sb("qr", [P, 2, T])
        parts = sb("parts", [P, 2, PARTS, T], BF16)
        qp = [sb(f"qp{b}", [KM, H, N], BF16) for b in range(2)]
        kp = [sb(f"kp{b}", [KM, H, N], BF16) for b in range(2)]
        vaug = sb("vaug", [P, TILES, H, 2 * DH])
        mx = sb("mx", [P, BT, H])
        mr = sb("mr", [P, BT, H])
        mm_parts = sb("mm_parts", [P, BT, PARTS, H], BF16)
        mt = sb("mt", [PARTS * H, N], BF16)
        prob = sb("prob", [P, RING, BT * N])
        oe = sb("oe", [P, 2, G, N])
        rden = sb("rden", [P, TILES, H])
        gl = sb("gl", [P, 2, T])
        g_hi = sb("g_hi", [P, 2, T], F32R)
        g_lo = sb("g_lo", [P, 2, T], F32R)

        full = [sem(f"lin_full{i}") for i in range(3)]
        free = [sem(f"lin_free{i}") for i in range(3)]
        mx_full, mx_free, sc_full, exped, av_full, av_free = (
            sem("mx_full"), sem("mx_free"), sem("sc_full"), sem("exped"), sem("av_full"), sem("av_free"))
        w0_in = [sem(f"w0_in{i}") for i in range(C * 3 * D // W_CHUNK)]
        w3_in = [sem(f"w3_in{i}") for i in range((C * D + C * DFF + J * D) // W_CHUNK)]
        w_split, bias0_in, bias3_in, ready = sem("w_split"), sem("bias0_in"), sem("bias3_in"), sem("ready")
        m0_ready, m3_ready = sem("m0_ready"), sem("m3_ready")
        st0, st3, rstd0, rstd3, xh0_ready, xh3_ready = (
            sem("st0"), sem("st3"), sem("rstd0"), sem("rstd3"), sem("xh0_ready"), sem("xh3_ready"))
        h0_split, o_split, h3_split, gelu_split = sem("h0_split"), sem("o_split"), sem("h3_split"), sem("gelu_split")
        h0_rounded, o_rounded, h3_rounded = sem("h0_rounded"), sem("o_rounded"), sem("h3_rounded")
        qk_chain, part3, scr_in = sem("qk_chain"), sem("part3"), [sem("scr_in0"), sem("scr_in1")]
        pack_in = [sem("pack_in0"), sem("pack_in1")]
        max_chain, mt_scr, mrow_in = sem("max_chain"), sem("mt_scr"), [sem("mrow_in0"), sem("mrow_in1")]
        rden_chain, fc2_read = sem("rden_chain"), sem("fc2_read")
        bias_v_in = sem("bias_v_in")
        outs, half_ready = sem("outs"), sem("half_ready")
        passed = sem("passed")

        nothing = {i: 0 for i in range(3)}
        prelude = Banks(uses_of("FN"), nothing)
        first_ = Banks(uses_of("FMON"), prelude.after(1))
        second_ = Banks(uses_of("FBMON"), first_.after(1))
        middle_ = Banks(uses_of("XFBMON"), second_.after(1))
        last_ = Banks(uses_of("XBMO"), middle_.after(STEPS - 3))
        tail_ = Banks(uses_of("XB"), last_.after(1))
        final_ = Banks(uses_of("X"), tail_.after(1))

        class Kind:

            def __init__(self, banks, at):
                self.banks, self.at = banks, at

            def full(self, eng, name):
                i, k = self.banks.use(name, self.at)
                eng.wait_ge(full[i], k + 1)
                return lin[i], free[i]

            def read(self, eng, name):
                i, k = self.banks.use(name, self.at)
                eng.wait_ge(free[i], k + 1)

            def of(self, name):
                i, _ = self.banks.use(name, self.at)
                return lin[i], full[i]

            def take(self, pe, name):
                i, k = self.banks.use(name, self.at)
                if not isinstance(k, int) or k > 0:
                    pe.wait_ge(free[i], k)
                return lin[i], full[i]

        PACKS = len(Q_PART) + len(K_PART) + 1
        PRE = Kind(prelude, 0)
        FST = Kind(first_, 0)
        LST = Kind(last_, 0)
        SND = Kind(second_, 0)
        TAIL = Kind(tail_, 0)
        FINAL = Kind(final_, 0)

        W0_CHUNKS, W3_CHUNKS = len(w0_in), len(w3_in)
        CHUNKS = W0_CHUNKS + W3_CHUNKS

        MAXES = UNITS // (2 * J)
        MR_AFTER = MAXES * 2 * (J - 1)

        def schedule(eng, prelude_, body, back, switch0, switch3):
            prelude_()
            body(0, FST, True, False, False)
            body(1, SND, True, True, False)
            with eng.Fori(2, PAIRS - 1) as t:
                body(t, Kind(middle_, t - 2), True, True, True)
            with eng.Fori(1, LAYERS) as l:
                switch0(l)
                with eng.Fori(0, 2) as i:
                    t = l * PAIRS + i - 1
                    body(t, Kind(middle_, t - 2), True, True, True)
                switch3(l)
                with eng.Fori(0, PAIRS - 2) as i:
                    t = l * PAIRS + i + 1
                    body(t, Kind(middle_, t - 2), True, True, True)
            body(STEPS - 1, LST, False, True, True)
            back(STEPS - 1)

        block = ctx.enter_context(nc.Block())

        @block.tensor
        def _(pe):
            def mmx(out, w_hi, w_lo, oc, hi, lo, chunks=range(C)):
                o = slice(oc * P, (oc + 1) * P)
                for c in chunks:
                    mm = mm3(pe, out, w_hi[:, c, o], w_lo[:, c, o], hi[:, c], lo[:, c], c == 0, c == C - 1)
                return mm

            def to_features(kind, name, src, c):
                out, done = kind.take(pe, name)
                for i in range(TILES):
                    mm = pe.transpose(out[:, i * P:(i + 1) * P], src[:, i, c * P:(c + 1) * P], ident[:])
                mm.then_inc(done, 1)

            def to_tokens(kind, name, i):
                out, done = kind.take(pe, name)
                for tt in range(2):
                    for c in range(C):
                        t = slice((2 * i + tt) * P, (2 * i + tt + 1) * P)
                        mm = pe.transpose(out[:, tt * D + c * P:tt * D + (c + 1) * P], h3[:, c, t], ident[:])
                mm.then_inc(done, 1)

            def ln1(kind, n, c):
                pe.wait_ge(xh0_ready, TILES * (n + 1))
                to_features(kind, f"ln1_{c}", xh0, c)

            def qk(kind, n, i, chunks=range(C)):
                if 0 in chunks:
                    pe.wait_ge(h0_split, C * (n + 1))
                    kind.take(pe, f"qk{i}")
                out, done = kind.of(f"qk{i}")
                mm = mmx(out[:], w0_hi, w0_lo, i, h0_hi, h0_lo, chunks)
                if C - 1 in chunks:
                    mm.then_inc(done, 1)

            def values(kind, n, b, tiles=range(BT)):
                if 0 in tiles:
                    pe.wait_ge(h0_split, C * (n + 1))
                    kind.take(pe, f"v{b}")
                out, done = kind.of(f"v{b}")
                for i in tiles:
                    t = slice(b * N + i * P, b * N + (i + 1) * P)
                    for c in range(C):
                        mm = mm3(pe, out[:, i * D:(i + 1) * D], h0_hi[:, c, t], h0_lo[:, c, t],
                                 w0_hi[:, c, 2 * D:], w0_lo[:, c, 2 * D:], c == 0, c == C - 1)
                if BT - 1 in tiles:
                    mm.then_inc(done, 1)

            def max_scores(n, b, h):
                v = b * H + h
                if h == 0:
                    pe.wait_ge(pack_in[b], 16 * PACKS * (n + 1))
                if v >= SC:
                    pe.wait_ge(mx_free, UNITS * n + v - SC + 1)
                elif not isinstance(n, int) or n > 0:
                    pe.wait_ge(exped, UNITS * n + v - SC + 1)
                for i in range(BT):
                    mm = pe.matmul(scb[v % SC][:, i * N:(i + 1) * N], qp[b][0:KA, h, i * P:(i + 1) * P], kp[b][0:KA, h, :],
                                   start=True, stop=True)
                mm.then_inc(mx_full, 1)

            def max_rows(kind, n, b):
                pe.wait_ge(max_chain, 8 * n + 4 * b + 4)
                out, done = kind.take(pe, f"mr{b}")
                settle(pe, passed, n)
                out = out[0:PARTS * H, 0:N // 2].bitcast(BF16)
                for i in range(BT):
                    mm = pe.transpose(out[:, i * P:(i + 1) * P], mm_parts[:, i].rearrange("p k h -> p (k h)"), identb[:])
                mm.then_inc(done, 1)

            def exp_scores(t, u):
                b, h = u // H, u % H
                if h == 0:
                    pe.wait_ge(mrow_in[b], 16 * (t + 1))
                if u >= SC:
                    pe.wait_ge(exped, UNITS * t + u - SC + 1)
                else:
                    pe.wait_ge(mx_free, UNITS * (t + 1) + u - SC + 1)
                for i in range(BT):
                    mm = pe.matmul(scb[u % SC][:, i * N:(i + 1) * N], kp[b][:, h, i * P:(i + 1) * P], qp[b][:, h, :],
                                   start=True, stop=True)
                mm.then_inc(sc_full, 1)

            def attend(t, gg):
                b, g = gg // G, gg % G
                pe.wait_ge(exped, UNITS * t + GH * (gg + 1))
                if gg or not isinstance(t, int) or t > 0:
                    pe.wait_ge(av_free, 2 * G * t + gg)
                for i in range(BT):
                    for hh in range(GH):
                        mm = pe.matmul(avb[32 * hh:32 * hh + 32, 0:N], vaug[:, b * BT + i, g * GH + hh, :],
                                       prob[:, (gg * GH + hh) % RING, i * N:(i + 1) * N], start=(i == 0), stop=(i == BT - 1),
                                       skip_group_check=True)
                mm.then_inc(av_full, 1)

            def o_tokens(kind, n, i):
                pe.wait_ge(av_free, 2 * G * n + G * (i // BT + 1))
                out, done = kind.take(pe, f"otm{i}")
                for g in range(G):
                    mm = pe.transpose(out[:, g * P:(g + 1) * P], oe[:, i // BT, g, (i % BT) * P:(i % BT + 1) * P], ident[:])
                mm.then_inc(done, 1)

            def o_features(kind, n, b):
                for i in range(BT):
                    kind.read(pe, f"otm{b * BT + i}")
                out, done = kind.take(pe, f"ofm{b}")
                for c in range(C):
                    for i in range(BT):
                        mm = pe.transpose(out[:, c * N + i * P:c * N + (i + 1) * P], xh3[:, b * BT + i, c * P:(c + 1) * P],
                                          ident[:])
                mm.then_inc(done, 1)

            def project(kind, n, oc):
                pe.wait_ge(o_split, C * (n + 1))
                out, done = kind.take(pe, f"proj{oc}")
                mmx(out[:], wp_hi, wp_lo, oc, h0_hi, h0_lo).then_inc(done, 1)

            def x_mid_back(kind, n, i):
                for oc in range(C):
                    kind.read(pe, f"proj{oc}")
                to_tokens(kind, f"xa{i}", i)

            def ln2(kind, n, c):
                pe.wait_ge(xh3_ready, TILES * (n + 1))
                to_features(kind, f"ln2_{c}", xh3, c)

            def fc1(kind, n, j):
                pe.wait_ge(h3_split, C * (n + 1))
                out, done = kind.take(pe, f"fc1_{j}")
                mmx(out[:], w1_hi, w1_lo, j, h3_hi, h3_lo).then_inc(done, 1)

            def fc2(kind, n, j):
                pe.wait_ge(gelu_split, J * n + j + 1)
                for oc in range(C):
                    i, k = kind.banks.use(f"fc2_{oc}", kind.at)
                    if j == 0:
                        kind.take(pe, f"fc2_{oc}")
                    o = slice(oc * P, (oc + 1) * P)
                    mm = mm3(pe, lin[i][:], w2_hi[:, j, o], w2_lo[:, j, o], g_hi[:, j % 2], g_lo[:, j % 2], j == 0, j == J - 1)
                    if j == J - 1:
                        mm.then_inc(full[i], 1)
                if j < J - 1:
                    mm.then_inc(fc2_read, 1)

            def x_out_back(kind, n):
                for i in range(2):
                    kind.take(pe, f"xb{i}")
                for i in range(2):
                    to_tokens(kind, f"xb{i}", i)

            def switch0(l):
                pe.wait_ge(w_split, 2 * (CHUNKS * l + W0_CHUNKS))
                settle(pe, passed, l)

            def switch3(l):
                pe.wait_ge(w_split, 2 * CHUNKS * (l + 1))
                settle(pe, passed, l)

            def maxes(n):
                left = iter([(b, h) for b in range(2) for h in range(H)])

                def some(k):
                    for _ in range(k):
                        max_scores(n, *next(left))
                return some

            def prelude_():
                switch0(0)
                pe.wait_ge(ready, 5)
                for c in range(C):
                    ln1(PRE, 0, c)
                for i in range(2 * C):
                    qk(PRE, 0, i)
                for b in range(2):
                    values(PRE, 0, b)
                some = maxes(0)
                some(MR_AFTER)
                max_rows(PRE, 0, 0)
                some(UNITS - MR_AFTER)
                switch3(0)

            def mlp(kind, n, extra):
                for j in range(J):
                    if j + 1 < J:
                        fc1(kind, n, j + 1)
                    extra(j, 0)
                    fc2(kind, n, j)
                    extra(j, 1)

            def body(t, kind, front, back, far):
                if front:
                    ln1(kind, t + 1, 0)
                if far:
                    x_out_back(kind, t - 2)
                slots = {}

                def at(u, f, *args):
                    slots.setdefault(u, []).append(lambda: f(kind, *args))

                if front:
                    at(2, ln1, t + 1, 1)
                if back:
                    for oc in range(C):
                        at(3 + oc, project, t - 1, oc)
                at(5, max_rows, t, 1)
                if back:
                    for i in range(2):
                        at(7 + i, x_mid_back, t - 1, i)
                if front:
                    for i in range(2 * C):
                        for c in range(C):
                            at(9 + 3 * i + c, qk, t + 1, i, (c,))
                    for i in range(BT):
                        at(19 + 2 * i, values, t + 1, 0, (i,))
                if back:
                    for c in range(C):
                        at(23 + c, ln2, t - 1, c)
                for i in range(BT):
                    at(27 + i, o_tokens, t, i)
                for u in range(UNITS):
                    exp_scores(t, u)
                    if u % GH == 2 and u > GH:
                        attend(t, u // GH - 1)
                    for f in slots.get(u, []):
                        f()
                if front:
                    values(kind, t + 1, 1)
                attend(t, 2 * G - 1)
                if back:
                    fc1(kind, t - 1, 0)
                for i in range(BT, TILES):
                    o_tokens(kind, t, i)
                o_features(kind, t, 0)
                o_features(kind, t, 1)
                some = maxes(t + 1)
                if back:
                    def extra(j, k):
                        if front:
                            some(MAXES)
                            if j == J - 2 and k == 1:
                                max_rows(kind, t + 1, 0)
                    mlp(kind, t - 1, extra)
                elif front:
                    some(MR_AFTER)
                    max_rows(kind, t + 1, 0)
                    some(UNITS - MR_AFTER)

            def back(t):
                kind = TAIL
                x_out_back(kind, t - 1)
                for oc in range(C):
                    project(kind, t, oc)
                for i in range(2):
                    x_mid_back(kind, t, i)
                for c in range(C):
                    ln2(kind, t, c)
                fc1(kind, t, 0)
                mlp(kind, t, lambda j, k: None)
                x_out_back(FINAL, t)

            schedule(pe, prelude_, body, back, switch0, switch3)

        @block.vector
        def _(dve):
            v = nc.vector

            def norm_stats(x, k, n, st):
                settle(dve, passed, n)
                for i in range(TILES):
                    v.bn_stats(stats[:, k, i], x[:, i]).then_inc(st, 1)
                dve.wait_ge(st, (2 * TILES + 1) * n + TILES)
                settle(dve, passed, n)
                for i in range(TILES):
                    v.bn_aggr(mv[:, k, i], stats[:, k, i]).then_inc(st, 1)
                dve.wait_ge(st, (2 * TILES + 1) * n + 2 * TILES)
                v.tensor_scalar(var[:, k], mv[:, k, :, 1], EPS, None, ALU.add).then_inc(st, 1)

            def normalise(x, k, n, rstd_ready, xh, ready_):
                dve.wait_ge(rstd_ready, n + 1)
                for i in range(TILES):
                    v.tensor_scalar(xh[:, i], x[:, i], mv[:, k, i, 0:1], rstd[:, k, i:i + 1],
                                    ALU.subtract, ALU.mult).then_inc(ready_, 1)

            def front_norm(n):
                norm_stats(xres[:, n % PAIRS], 0, n, st0)
                normalise(xres[:, n % PAIRS], 0, n, rstd0, xh0, xh0_ready)

            def load_m0(n):
                v.tensor_copy(m0[:], mod_p0[:, n]).then_inc(m0_ready, 1)

            def load_m3(n):
                v.tensor_copy(m3[:], mod_p3[:, n]).then_inc(m3_ready, 1)

            def round_h0(kind, n):
                if not isinstance(n, int) or n > 1:
                    kind.full(dve, "proj1")
                for c in range(C):
                    kind.read(dve, f"ln1_{c}")
                    v.tensor_copy(h0_hi[:, c], h0[:, c]).then_inc(h0_rounded, 1)

            def round_h3(kind, n):
                for c in range(C):
                    kind.read(dve, f"ln2_{c}")
                    v.tensor_copy(h3_hi[:, c], h3[:, c]).then_inc(h3_rounded, 1)

            def o_out(kind, n):
                for b in range(2):
                    src, done = kind.full(dve, f"ofm{b}")
                    for c in range(C):
                        last = v.tensor_scalar(h0[:, c, b * N:(b + 1) * N], src[:, c * N:(c + 1) * N],
                                               bias_v[:, n, c:c + 1], None, ALU.add)
                    last.then_inc(done, 1)
                for b in range(2):
                    kind.read(dve, f"ofm{b}")
                for c in range(C):
                    v.tensor_copy(h0_hi[:, c], h0[:, c]).then_inc(o_rounded, 1)

            def qk(kind, n, i):
                src, done = kind.full(dve, f"qk{i}")
                link = Chain(dve, qk_chain, n, 3 * 2 * C, 3 * i).link
                if not isinstance(n, int) or n > 0 or i >= 2:
                    dve.wait_ge(scr_in[i % 2], 16 * (2 * n + i // 2))
                    dve.wait_ge(part3, 2 * C * n + i - 1)
                p = parts[:, i % 2]
                last = v.tensor_scalar(qf[:], src[:], bias0[:, i:i + 1], QSCALE if i < C else 1.0, ALU.add, ALU.mult)
                last.then_inc(done, 1)
                kind.read(dve, f"qk{i}")
                link(v.tensor_copy(p[:, 0], qf[:]))
                link(v.tensor_tensor(qr[:, i % 2], qf[:], p[:, 0], ALU.subtract))
                v.tensor_copy(p[:, 1], qr[:, i % 2]).then_inc(qk_chain, 1)

            def values(kind, n, b):
                src, done = kind.full(dve, f"v{b}")
                if not isinstance(n, int) or n > 0:
                    dve.wait_ge(av_full, 2 * G * n - (0 if b else G))
                v.tensor_copy(vaug[:, b * BT:(b + 1) * BT, :, 0:DH],
                              src[:].rearrange("p (i h d) -> p i h d", i=BT, h=H)).then_inc(done, 1)
                kind.read(dve, f"v{b}")

            def row_max(n, b, h):
                u = b * H + h
                dve.wait_ge(mx_full, UNITS * n + u + 1)
                v.tensor_reduce(mx[:, :, h], scb[u % SC][:].rearrange("p (i k) -> p i k", i=BT), AX_X,
                                ALU.max).then_inc(mx_free, 1)

            def max_parts(n, b):
                dve.wait_ge(mx_free, UNITS * n + H * (b + 1))
                link = Chain(dve, max_chain, n, 8, 4 * b).link
                link(v.tensor_scalar(mm_parts[:, :, 0], mx[:], -1.0, None, ALU.mult))
                link(v.scalar_tensor_tensor(mr[:], mx[:], -1.0, mm_parts[:, :, 0], ALU.mult, ALU.subtract))
                link(v.tensor_copy(mm_parts[:, :, 1], mr[:]))
                v.tensor_tensor(mm_parts[:, :, 2], mr[:], mm_parts[:, :, 1], ALU.subtract).then_inc(max_chain, 1)

            def max_rows(kind, n, b):
                src, done = kind.full(dve, f"mr{b}")
                if b or not isinstance(n, int) or n > 0:
                    dve.wait_ge(mt_scr, 16 * (2 * n + b))
                v.tensor_copy(mt[:], src[0:PARTS * H, 0:N // 2].bitcast(BF16)).then_inc(done, 1)

            def o_norm(kind, n, i):
                src, done = kind.full(dve, f"otm{i}")
                o = src[:].rearrange("p (h r) -> p h r", h=H)
                v.reciprocal(rden[:, i], o[:, :, DH]).then_inc(rden_chain, 1)
                dve.wait_ge(rden_chain, TILES * n + i + 1)
                v.tensor_tensor(xh3[:, i].rearrange("p (h d) -> p h d", h=H), o[:, :, 0:DH],
                                rden[:, i].unsqueeze(2).to_broadcast([P, H, DH]), ALU.mult).then_inc(done, 1)

            def add_x(kind, name, n, i):
                src, done = kind.full(dve, name)
                xs = xres[:, n % PAIRS, 2 * i:2 * i + 2, :]
                v.tensor_tensor(xs, src[:].rearrange("p (t f) -> p t f", t=2), xs, ALU.add).then_inc(done, 1)
                kind.read(dve, name)

            def split_weights(l, base, loaded, chunks):
                for k, (hi, lo) in enumerate(chunks):
                    dve.wait_ge(loaded[k], 16 * (l + 1))
                    v.tensor_copy(hi, prob[:, k % RING]).then_inc(w_split, 1)
                    dve.wait_ge(w_split, 2 * (CHUNKS * l + base + k) + 1)
                    v.tensor_tensor(lo, prob[:, k % RING], hi.bitcast(F32), ALU.subtract).then_inc(w_split, 1)

            def pieces(hi, lo):
                h, o = (x[:].rearrange("p a b -> p (a b)") for x in (hi, lo))
                return [(h[:, k:k + W_CHUNK], o[:, k:k + W_CHUNK]) for k in range(0, h.shape[1], W_CHUNK)]

            def switch0(l):
                dve.wait_ge(bias0_in, 16 * (l + 1))
                split_weights(l, 0, w0_in, pieces(w0_hi, w0_lo))

            def switch3(l):
                split_weights(l, W0_CHUNKS, w3_in, pieces(wp_hi, wp_lo) + pieces(w1_hi, w1_lo) + pieces(w2_hi, w2_lo))
                dve.wait_ge(bias3_in, 16 * (l + 1))
                settle(dve, passed, l)

            def maxima(kind, n):
                for u in range(UNITS):
                    row_max(n, u // H, u % H)
                    if u % H == H - 1:
                        max_parts(n, u // H)
                    if u == MR_AFTER - 1:
                        max_rows(kind, n, 0)

            def prelude_():
                v.memset(vaug[:, :, :, DH:], 1.0).then_inc(ready, 1)
                for b in range(2):
                    v.memset(kp[b][KR:KM], 1.0).then_inc(ready, 1)
                    v.memset(qp[b][KR:KA], 1.0).then_inc(ready, 1)
                front_norm(0)
                load_m0(0)
                switch0(0)
                round_h0(PRE, 0)
                for i in range(2 * C):
                    qk(PRE, 0, i)
                for b in range(2):
                    values(PRE, 0, b)
                front_norm(1)
                dve.wait_ge(bias_v_in, 16)
                switch3(0)
                maxima(PRE, 0)

            def body(t, kind, front, back, far):
                if front:
                    load_m0(t + 1)
                if far:
                    for i in range(2):
                        add_x(kind, f"xb{i}", t - 2, i)
                if back:
                    load_m3(t - 1)
                if front:
                    round_h0(kind, t + 1)
                max_rows(kind, t, 1)
                if back:
                    for i in range(2):
                        add_x(kind, f"xa{i}", t - 1, i)
                    norm_stats(xres[:, (t - 1) % PAIRS], 1, t - 1, st3)
                if front:
                    for i in range(C):
                        qk(kind, t + 1, i)
                if back:
                    normalise(xres[:, (t - 1) % PAIRS], 1, t - 1, rstd3, xh3, xh3_ready)
                if front:
                    for i in range(C, 2 * C):
                        qk(kind, t + 1, i)
                    values(kind, t + 1, 0)
                if back:
                    round_h3(kind, t - 1)
                if front:
                    front_norm(t + 2)
                for i in range(BT):
                    o_norm(kind, t, i)
                if front:
                    values(kind, t + 1, 1)
                for i in range(BT, TILES):
                    o_norm(kind, t, i)
                o_out(kind, t)
                if front:
                    maxima(kind, t + 1)

            def back(t):
                kind = TAIL
                for i in range(2):
                    add_x(kind, f"xb{i}", t - 1, i)
                load_m3(t)
                for i in range(2):
                    add_x(kind, f"xa{i}", t, i)
                norm_stats(xres[:, t % PAIRS], 1, t, st3)
                normalise(xres[:, t % PAIRS], 1, t, rstd3, xh3, xh3_ready)
                round_h3(kind, t)
                for i in range(2):
                    add_x(FINAL, f"xb{i}", t, i)

            schedule(dve, prelude_, body, back, switch0, switch3)

        @block.scalar
        def _(act):
            a = nc.scalar

            def modulate(kind, name, c, dst, m, scale, shift_):
                src, done = kind.full(act, name)
                for b in range(2):
                    t = slice(b * N, (b + 1) * N)
                    last = a.activation(dst[:, c, t], src[:, t], ACT.Identity, bias=m[:, b, c, shift_:shift_ + 1],
                                        scale=m[:, b, c, scale:scale + 1])
                last.then_inc(done, 1)

            def ln1(kind, n, c):
                if c == 0:
                    act.wait_ge(m0_ready, n + 1)
                    if not isinstance(n, int) or n > 0:
                        act.wait_ge(h0_split, C * n)
                    if not isinstance(n, int) or n > 1:
                        act.wait_ge(o_split, C * (n - 1))
                modulate(kind, f"ln1_{c}", c, h0, m0, 0, 1)

            def project(kind, n):
                act.wait_ge(m3_ready, n + 1)
                for c in range(C):
                    modulate(kind, f"proj{c}", c, h3, m3, 0, 1)

            def ln2(kind, n):
                for i in range(2):
                    kind.full(act, f"xa{i}")
                for c in range(C):
                    modulate(kind, f"ln2_{c}", c, h3, m3, 2, 3)

            def gelus(kind, n):
                for j in range(J):
                    src, done = kind.full(act, f"fc1_{j}")
                    if j >= 2:
                        act.wait_ge(gelu_split, J * n + j - 1)
                        act.wait_ge(fc2_read, (J - 1) * n + j - 1)
                    bias = bias3[:, j:j + 1]
                    a.activation(g_hi[:, j % 2], src[:], ACT.Gelu, bias=bias)
                    a.activation(gl[:, j % 2], src[:], ACT.Gelu, bias=bias).then_inc(done, 1)
                act.wait_ge(h3_split, C * (n + 1))
                for c in range(C):
                    modulate(kind, f"fc2_{c}", c, h3, m3, 4, 5)

            def o_copy(t, gg):
                act.wait_ge(av_full, 2 * G * t + gg + 1)
                a.copy(oe[:, gg // G, gg % G], avb[:, 0:N]).then_inc(av_free, 1)

            def switch0(l):
                act.wait_ge(w_split, 2 * (CHUNKS * l + W0_CHUNKS))

            def switch3(l):
                act.wait_ge(w_split, 2 * CHUNKS * (l + 1))

            def prelude_():
                for c in range(C):
                    ln1(PRE, 0, c)
                switch3(0)

            def body(t, kind, front, back, far):
                if front:
                    ln1(kind, t + 1, 0)
                for u in range(UNITS):
                    act.wait_ge(sc_full, UNITS * t + u + 1)
                    gg = u // GH
                    if gg >= 2 or not isinstance(t, int) or t > 0:
                        act.wait_ge(av_full, 2 * G * t + gg - 1)
                    a.activation(prob[:, u % RING], scb[u % SC][:], ACT.Exp).then_inc(exped, 1)
                    if u % GH == 3 and u > GH:
                        o_copy(t, gg - 1)
                    if front and u == 2:
                        ln1(kind, t + 1, 1)
                    if back and u == 4:
                        project(kind, t - 1)
                    if back and u == 23:
                        ln2(kind, t - 1)
                o_copy(t, 2 * G - 1)
                if back:
                    gelus(kind, t - 1)

            def back(t):
                kind = TAIL
                project(kind, t)
                ln2(kind, t)
                gelus(kind, t)

            schedule(act, prelude_, body, back, switch0, switch3)

        @block.gpsimd
        def _(pool):
            g = nc.gpsimd

            def rest(lo, src, hi, done):
                g.tensor_tensor(lo, src, hi.bitcast(F32), ALU.subtract).then_inc(done, 1)

            def power(k, n, st, ready_):
                pool.wait_ge(st, (2 * TILES + 1) * (n + 1))
                g.tensor_tensor(rstd[:, k], var[:, k], mhalf[:], ALU.pow).then_inc(ready_, 1)

            def front_h0(kind, n):
                for c in range(C):
                    pool.wait_ge(h0_rounded, C * n + c + 1)
                    rest(h0_lo[:, c], h0[:, c], h0_hi[:, c], h0_split)

            def third(kind, n, i):
                pool.wait_ge(qk_chain, 3 * 2 * C * n + 3 * (i + 1))
                g.tensor_tensor(parts[:, i % 2, 2], qr[:, i % 2], parts[:, i % 2, 1], ALU.subtract).then_inc(part3, 1)

            def back_o(kind, n):
                for c in range(C):
                    pool.wait_ge(o_rounded, C * n + c + 1)
                    rest(h0_lo[:, c], h0[:, c], h0_hi[:, c], o_split)

            def back_ln2(kind, n):
                for c in range(C):
                    pool.wait_ge(h3_rounded, C * n + c + 1)
                    rest(h3_lo[:, c], h3[:, c], h3_hi[:, c], h3_split)

            def back_gelu(kind, n, chunks):
                for j in chunks:
                    kind.read(pool, f"fc1_{j}")
                    if j >= 2:
                        pool.wait_ge(fc2_read, (J - 1) * n + j - 1)
                    rest(g_lo[:, j % 2], gl[:, j % 2], g_hi[:, j % 2], gelu_split)

            def switch0(l):
                pass

            def switch3(l):
                pass

            def prelude_():
                g.memset(mhalf[:], -0.5).then_inc(half_ready, 1)
                pool.wait_ge(half_ready, 1)
                power(0, 0, st0, rstd0)
                front_h0(PRE, 0)
                for i in range(2 * C):
                    third(PRE, 0, i)
                power(0, 1, st0, rstd0)

            def body(t, kind, front, back, far):
                if front:
                    front_h0(kind, t + 1)
                if back:
                    power(1, t - 1, st3, rstd3)
                if front:
                    for i in range(2 * C):
                        third(kind, t + 1, i)
                if back:
                    back_ln2(kind, t - 1)
                if front:
                    power(0, t + 2, st0, rstd0)
                if back:
                    back_gelu(kind, t - 1, range(2))
                back_o(kind, t)
                if back:
                    back_gelu(kind, t - 1, range(2, J))

            def back(t):
                kind = TAIL
                power(1, t, st3, rstd3)
                back_ln2(kind, t)
                back_gelu(kind, t, range(J))

            schedule(pool, prelude_, body, back, switch0, switch3)

        @block.sync
        def _(sp):
            def load_weights(l, base, loaded, pieces=None):
                for k, done in enumerate(loaded):
                    if pieces is not None and k not in pieces:
                        continue
                    if k >= RING:
                        sp.wait_ge(w_split, 2 * (CHUNKS * l + base + k - RING + 1))
                    sp.dma_start(prob[:, k % RING], ins["tw"][l, :, base + k]).then_inc(done, 16)

            def switch0(l):
                if not isinstance(l, int):
                    sp.wait_ge(part3, 2 * C * PAIRS * l)
                    sp.wait_ge(av_full, 2 * G * (PAIRS * l - 1))
                sp.dma_start(bias0[:], ins["tbias"][l, :, 0:2 * C]).then_inc(bias0_in, 16)
                load_weights(l, 0, w0_in)

            def switch3(l):
                sp.wait_ge(av_full, 2 * G * (PAIRS * l + 1))
                load_weights(l, W0_CHUNKS, w3_in)
                sp.wait_ge(gelu_split, J * PAIRS * l)
                sp.dma_start(bias3[:], ins["tbias"][l, :, 3 * C:]).then_inc(bias3_in, 16)

            def scratch(n):
                for i in range(2 * C):
                    if i == 0 and (not isinstance(n, int) or n > 0):
                        for b in range(2):
                            sp.wait_ge(pack_in[b], 16 * PACKS * n)
                    sp.wait_ge(part3, 2 * C * n + i + 1)
                    sp.dma_start(scr_qk[i // C, :, (i % C) * P:(i % C + 1) * P, :].rearrange("k p t -> p k t"),
                                 parts[:, i % 2]).then_inc(scr_in[i % 2], 16)

            def pack(n, b):
                for r in range(2):
                    sp.wait_ge(scr_in[r], 16 * 2 * (n + 1))
                if not isinstance(n, int) or n > 0:
                    sp.wait_ge(sc_full, UNITS * n - (0 if b else H))
                for side, dst, which in ((0, qp[b], Q_PART), (1, kp[b], K_PART)):
                    for j, part in enumerate(which):
                        src = scr_qk[side, part].rearrange("(h d) t -> d h t", d=DH)[:, :, b * N:(b + 1) * N]
                        sp.dma_start(dst[16 * j:16 * (j + 1)], src).then_inc(pack_in[b], 16)
                mask = scr_mask[2 * n + b].unsqueeze(0).unsqueeze(0).to_broadcast([1, H, N])
                sp.dma_start(kp[b][KR:KA], mask).then_inc(pack_in[b], 16)

            def max_rows(kind, n, b):
                kind.read(sp, f"mr{b}")
                sp.dma_start(scr_max[b], mt[:]).then_inc(mt_scr, 16)
                sp.wait_ge(mt_scr, 16 * (2 * n + b + 1))
                sp.dma_start(qp[b][KA:KM], scr_max[b].rearrange("(k h) t -> k h t", k=PARTS)).then_inc(mrow_in[b], 16)

            def pair_in(kind, n):
                scratch(n)
                for b in range(2):
                    pack(n, b)

            def prelude_():
                switch0(0)
                sp.dma_start(bias_v[:], ins["bias_v"]).then_inc(bias_v_in, 16)
                sp.wait_ge(w_split, 2 * W0_CHUNKS)
                load_weights(0, W0_CHUNKS, w3_in, range(RING))
                sp.wait_ge(ready, 5)
                pair_in(PRE, 0)
                load_weights(0, W0_CHUNKS, w3_in, range(RING, W3_CHUNKS))
                sp.dma_start(bias3[:], ins["tbias"][0, :, 3 * C:]).then_inc(bias3_in, 16)
                max_rows(PRE, 0, 0)

            def store(kind, pair):
                for i in range(2):
                    kind.read(sp, f"xb{i}")
                sp.dma_start(out_dram[pair], xres[:, pair]).then_inc(outs, 16)

            def body(t, kind, front, back, far):
                if not front:
                    for pair in range(PAIRS - 3):
                        store(Kind(middle_, STEPS - 4), pair)
                max_rows(kind, t, 1)
                if front:
                    pair_in(kind, t + 1)
                    max_rows(kind, t + 1, 0)

            def back(t):
                for n, kind in enumerate((LST, TAIL, FINAL)):
                    store(kind, PAIRS - 3 + n)
                sp.wait_ge(outs, 16 * PAIRS)

            schedule(sp, prelude_, body, back, switch0, switch3)


def build(nc, ins, out_dram):
    with ExitStack() as ctx:
        def sb(name, shape, dt=F32):
            return ctx.enter_context(nc.sbuf_tensor(name, shape, dt))

        xres = sb("xres", [P, PAIRS, TILES, D])
        mod_p0 = sb("mod_p0", [P, LAYERS * PAIRS, 2, C, 2])
        mod_p3 = sb("mod_p3", [P, LAYERS * PAIRS, 2, C, 6])
        ident = sb("ident", [P, P])
        identb = sb("identb", [P, P], BF16)
        scr_qk = nc.dram_tensor("scr_qk", (2, PARTS, D, T), BF16, kind="Internal").ap()
        scr_max = nc.dram_tensor("scr_max", (2, PARTS * H, N), BF16, kind="Internal").ap()
        scr_mask = nc.dram_tensor("scr_mask", (LAYERS * B, N), BF16, kind="Internal").ap()
        graph_layer(nc, ins, xres, mod_p0, mod_p3, ident, identb, scr_mask)
        transformer_layers(nc, ins, xres, mod_p0, mod_p3, ident, identb, out_dram, scr_qk, scr_max, scr_mask)


def kernel(**a):
    import concourse.bacc as bacc
    from concourse.bass_utils import run_bass_kernel_spmd

    def arr(name):
        return np.asarray(a[name])

    def rows(w):
        return np.asarray(w).reshape(-1, P, w.shape[-1]).transpose(1, 0, 2)

    def cols(v, k=C):
        return np.asarray(v).reshape(k, P).T

    f32 = np.float32
    x = arr("x").reshape(PAIRS, TILES, P, D).transpose(0, 2, 1, 3)
    mask = arr("mask_BxSxSx11_ik0")
    adj = np.stack([mask[:, :, :NK, :], mask[:, :NK, :, :].transpose(0, 2, 1, 3)], axis=2)
    adj = adj.reshape(PAIRS, TILES, P, 2 * NK, L).transpose(0, 2, 1, 3, 4).reshape(PAIRS, P, TILES * 2 * NK, L)
    w_self = arr("L0_cond_W_self")
    wq, wk, wout = arr("L0_cond_Wq"), arr("L0_cond_Wk"), arr("L0_cond_Wout").reshape(2, D, D)
    gw = np.stack([rows(w.T) for w in (w_self[:, :D], wq[0], wq[1], wk[0], wk[1], wout[0], wout[1])])
    bq, bk, bo = arr("L0_cond_bq"), arr("L0_cond_bk"), arr("L0_cond_bout")
    gbias = np.stack([cols(v) for v in (arr("L0_cond_b_self"), bq[0], bq[1], bk[0], bk[1], bo[0], bo[1])], axis=1)
    lab = np.broadcast_to(np.concatenate([arr("L0_cond_w_bias"), arr("L0_cond_b_bias").reshape(1)]), (P, L + 1))

    def m1(k):
        return arr(f"L1_cond_{k}")

    def m2(k):
        return arr(f"L2_cond_{k}")

    def m3(k):
        return arr(f"L3_cond_{k}")

    vec1 = ("b1", "g1", "a1", "b2", "g2", "a2")
    ada = [rows(np.concatenate([m1(v + "_w") for v in vec1], axis=1)), rows(m2("w_ada"))]
    w31, w32 = m3("w_adaln1"), m3("w_adaln2")
    ada.append(rows(np.concatenate([w31[D:], w31[:D], w32[D:], w32[:D]], axis=0).T))
    b31, b32 = m3("b_adaln1"), m3("b_adaln2")
    zero = np.zeros(D, f32)
    ada_b = np.stack([np.stack([cols(m1(v + "_b")) for v in vec1], axis=1),
                      np.stack([cols(v) for v in m2("b_ada").reshape(6, D)], axis=1),
                      np.stack([cols(v) for v in (b31[D:], b31[:D], zero, b32[D:], b32[:D], zero)], axis=1)], axis=1)
    ln_gb = np.stack([cols(m1(v)) for v in ("ln1_g", "ln1_b", "ln2_g", "ln2_b")], axis=1)
    out_b = np.stack([np.stack([cols(p), cols(f)], axis=1) for p, f in (
        (m1("proj_b"), m1("fc2_b")), (m2("b_proj"), m2("b_fc2")), (m3("bo"), m3("b2")))], axis=1)

    blocks = [(m1("qkv_w"), m1("proj_w"), m1("fc1_w"), m1("fc2_w")), (m2("w_qkv"), m2("w_proj"), m2("w_fc1"), m2("w_fc2")),
              (np.concatenate([m3("wq").T, m3("wk").T, m3("wv").T], axis=1), m3("wo").T, m3("w1").T, m3("w2").T)]
    tw = np.stack([np.concatenate([rows(w).reshape(P, -1) for w in ws], axis=1).reshape(P, -1, W_CHUNK) for ws in blocks])
    qkv_b = [m1("qkv_b"), np.zeros(3 * D, f32), np.concatenate([m3("bq"), m3("bk"), m3("bv")])]
    fc1_b = [m1("fc1_b"), m2("b_fc1"), m3("b1")]
    tbias = np.stack([np.concatenate([cols(b, 3 * C), cols(f, J)], axis=1) for b, f in zip(qkv_b, fc1_b)])

    bias_v = np.repeat(np.stack([cols(b, 3 * C)[:, 2 * C:] for b in qkv_b], axis=1), PAIRS, axis=1)

    sel8 = np.kron(np.eye(HC, dtype=f32), np.ones((DH, 1), f32))
    sel80 = np.kron(np.eye(GH, dtype=f32), np.ones((NK, 1), f32))
    inputs = {"x": x, "mask": arr("mask_BxS_bf0"), "adj": adj, "cond": cols_of(arr("cond_1024")), "wq_self": rows(w_self[:, D:].T), "gw": gw, "gbias": gbias,
              "lab": lab, "sel8": sel8, "sel80": sel80, "ident": np.eye(P, dtype=f32), "ada0": ada[0], "ada1": ada[1],
              "ada2": ada[2], "ada_b": ada_b, "ln_gb": ln_gb, "out_b": out_b, "tw": tw, "tbias": tbias, "bias_v": bias_v}
    inputs = {k: np.ascontiguousarray(v) for k, v in inputs.items()}

    nc = bacc.Bacc("TRN2", target_bir_lowering=False, num_devices=1)
    ins = {k: nc.dram_tensor(f"in_{k}", v.shape, mybir.dt.from_np(v.dtype), kind="ExternalInput").ap()
           for k, v in inputs.items()}
    out = nc.dram_tensor("out_x", (PAIRS, P, TILES, D), F32, kind="ExternalOutput").ap()
    build(nc, ins, out)
    r = run_bass_kernel_spmd(nc, [{f"in_{k}": v for k, v in inputs.items()}], core_ids=[0])
    y = r.results[0]["out_x"]
    return y.transpose(0, 2, 1, 3).reshape(B, N, D)


def cols_of(cond):
    return cond.T.reshape(C, P, B).transpose(1, 0, 2)
```
